# Optimizing a Trainium2 kernel written in Bass

```python
import numpy as np
import jax
import jax.numpy as jnp

def _softmax(x, axis=-1):
    return jax.nn.softmax(x, axis=axis)

def _gelu(x):
    return jax.nn.gelu(x, approximate=True)

def _silu(x):
    return jax.nn.silu(x)

def _sigmoid(x):
    return jax.nn.sigmoid(x)

def _layernorm(x, axis=-1, eps=1e-05):
    m = jnp.mean(x, axis=axis, keepdims=True)
    v = jnp.var(x, axis=axis, keepdims=True)
    return (x - m) / jnp.sqrt(v + eps)

def _scatter_add(tgt, idx, src, axis=0):
    return tgt.at[idx].add(src)

def _segment_sum(src, seg, n):
    return jax.ops.segment_sum(src, seg, n)
kernel_name = 'mk_macaron_d1_jaxref_r8_542a7a'

def setup_inputs(seed: int=0):
    np.random.seed(seed)
    _w = jnp.asarray

    def _L0_attn_setup():
        import jax, jax.numpy as jnp
        import numpy as np
        B, L, D, H = (4, 128, 128, 16)
        HD = D // H
        MAX_LEN = 128
        SCALE = HD ** 0.5

        def _rel_idx(seq_len):
            r = jnp.arange(seq_len)
            dist = r[None, :] - r[:, None]
            return jnp.clip(dist, -MAX_LEN, MAX_LEN) + MAX_LEN
        key = jax.random.key(seed)
        ks = jax.random.split(key, 7)
        sd = 1.0 / np.sqrt(D)
        x = jax.random.normal(ks[0], (B, L, D), dtype=jnp.float32)
        Wq = jax.random.normal(ks[1], (D, D), dtype=jnp.float32) * sd
        Wk = jax.random.normal(ks[2], (D, D), dtype=jnp.float32) * sd
        Wv = jax.random.normal(ks[3], (D, D), dtype=jnp.float32) * sd
        Wo = jax.random.normal(ks[4], (D, D), dtype=jnp.float32) * sd
        pek = jax.random.normal(ks[5], (2 * MAX_LEN + 1, HD), dtype=jnp.float32) / np.sqrt(HD)
        pev = jax.random.normal(ks[6], (2 * MAX_LEN + 1, HD), dtype=jnp.float32) / np.sqrt(HD)
        return {'x': x, 'Wq': Wq, 'Wk': Wk, 'Wv': Wv, 'Wo': Wo, 'pek': pek, 'pev': pev}
    _L0_attn_in = _L0_attn_setup()

    def _L0_ffn_setup():
        import jax, jax.numpy as jnp
        import numpy as np
        B, S, D = (4, 512, 128)
        DD = 4 * D
        N_EXPERTS = 8
        CAPACITY = 1.0
        LN_EPS = 1e-05
        key = jax.random.key(seed)
        ks = jax.random.split(key, 8)
        s1 = 1.0 / np.sqrt(D)
        s2 = 1.0 / np.sqrt(DD)
        return {'x': jax.random.normal(ks[0], (B, S, D), jnp.float32), 'gate_w': jax.random.normal(ks[1], (N_EXPERTS, D), jnp.float32) * 0.02, 'ln_w': jnp.ones((D,), jnp.float32), 'ln_b': jnp.zeros((D,), jnp.float32), 'fc1s': jax.random.normal(ks[2], (N_EXPERTS, DD, D), jnp.float32) * s1, 'b1s': jax.random.normal(ks[3], (N_EXPERTS, DD), jnp.float32) * s1, 'fc2s': jax.random.normal(ks[4], (N_EXPERTS, D, DD), jnp.float32) * s2, 'b2s': jax.random.normal(ks[5], (N_EXPERTS, D), jnp.float32) * s2}
    _L0_ffn_in = _L0_ffn_setup()
    _d = {'L0_attn_x': _L0_attn_in['x'], 'L0_attn_Wq': _L0_attn_in['Wq'], 'L0_attn_Wk': _L0_attn_in['Wk'], 'L0_attn_Wv': _L0_attn_in['Wv'], 'L0_attn_Wo': _L0_attn_in['Wo'], 'L0_attn_pek': _L0_attn_in['pek'], 'L0_attn_pev': _L0_attn_in['pev'], 'L0_ffn_gate_w': _L0_ffn_in['gate_w'], 'L0_ffn_ln_w': _L0_ffn_in['ln_w'], 'L0_ffn_ln_b': _L0_ffn_in['ln_b'], 'L0_ffn_fc1s': _L0_ffn_in['fc1s'], 'L0_ffn_b1s': _L0_ffn_in['b1s'], 'L0_ffn_fc2s': _L0_ffn_in['fc2s'], 'L0_ffn_b2s': _L0_ffn_in['b2s']}
    _x0 = _d['L0_attn_x']
    _d['L0_attn_x'] = jax.random.normal(jax.random.fold_in(jax.random.key(seed), 1), (16, 256, 128), dtype=_x0.dtype)
    del _x0
    return _d

def reference(L0_attn_x, L0_attn_Wq, L0_attn_Wk, L0_attn_Wv, L0_attn_Wo, L0_attn_pek, L0_attn_pev, L0_ffn_gate_w, L0_ffn_ln_w, L0_ffn_ln_b, L0_ffn_fc1s, L0_ffn_b1s, L0_ffn_fc2s, L0_ffn_b2s):

    def _L0_attn_ref(x, Wq, Wk, Wv, Wo, pek, pev):
        import jax, jax.numpy as jnp
        import numpy as np
        B, L, D, H = (4, 128, 128, 16)
        HD = D // H
        MAX_LEN = 128
        SCALE = HD ** 0.5

        def _rel_idx(seq_len):
            r = jnp.arange(seq_len)
            dist = r[None, :] - r[:, None]
            return jnp.clip(dist, -MAX_LEN, MAX_LEN) + MAX_LEN
        b, s, _ = x.shape

        def proj(W):
            return (x @ W.T).reshape(b, s, H, HD).transpose(0, 2, 1, 3)
        Q, K, V = (proj(Wq), proj(Wk), proj(Wv))
        scores = jnp.einsum('bhqd,bhkd->bhqk', Q, K) / SCALE
        idx = _rel_idx(s)
        rel_k = pek[idx]
        scores = scores + jnp.einsum('bhqd,qkd->bhqk', Q, rel_k) / SCALE
        causal = jnp.tril(jnp.ones((s, s), dtype=bool))
        scores = jnp.where(causal[None, None], scores, -jnp.inf)
        attn = jax.nn.softmax(scores, axis=-1)
        out = jnp.einsum('bhqk,bhkd->bhqd', attn, V)
        rel_v = pev[idx]
        out = out + jnp.einsum('bhqk,qkd->bhqd', attn, rel_v)
        out = out.transpose(0, 2, 1, 3).reshape(b, s, D)
        return out @ Wo.T

    def _L0_ffn_ref(x, gate_w, ln_w, ln_b, fc1s, b1s, fc2s, b2s):
        import jax, jax.numpy as jnp
        import numpy as np
        B, S, D = (4, 512, 128)
        DD = 4 * D
        N_EXPERTS = 8
        CAPACITY = 1.0
        LN_EPS = 1e-05
        og_shape = x.shape
        d = og_shape[-1]
        xf = x.reshape(-1, d)
        bs = xf.shape[0]
        n = gate_w.shape[0]
        k = int(bs * CAPACITY) // n
        scores = jax.nn.softmax(xf @ gate_w.T, axis=-1)
        vals, idx = jax.lax.top_k(scores.T, k)
        kept_w = vals.T
        kept_idx = idx.T
        flat_idx = kept_idx.reshape(-1)
        y = xf[flat_idx].reshape(k, n, d)
        mu = y.mean(-1, keepdims=True)
        var = ((y - mu) ** 2).mean(-1, keepdims=True)
        y = (y - mu) * jax.lax.rsqrt(var + LN_EPS) * ln_w + ln_b
        h = jnp.einsum('knd,nfd->knf', y, fc1s) + b1s
        h = jax.nn.gelu(h, approximate=True)
        out = jnp.einsum('knf,ndf->knd', h, fc2s) + b2s
        out = out * kept_w[..., None]
        xf = xf.at[flat_idx].add(out.reshape(k * n, d))
        return xf.reshape(og_shape)
    x = L0_attn_x
    x = x + 0.5 * _L0_ffn_ref(_layernorm(x, axis=-1), L0_ffn_gate_w, L0_ffn_ln_w, L0_ffn_ln_b, L0_ffn_fc1s, L0_ffn_b1s, L0_ffn_fc2s, L0_ffn_b2s)
    x = x + _L0_attn_ref(_layernorm(x, axis=-1), L0_attn_Wq, L0_attn_Wk, L0_attn_Wv, L0_attn_Wo, L0_attn_pek, L0_attn_pev)
    x = x + 0.5 * _L0_ffn_ref(_layernorm(x, axis=-1), L0_ffn_gate_w, L0_ffn_ln_w, L0_ffn_ln_b, L0_ffn_fc1s, L0_ffn_b1s, L0_ffn_fc2s, L0_ffn_b2s)
    return x

_drawn_inputs = setup_inputs


def setup_inputs(seed=0):
    import zlib

    import numpy as np

    out = dict(_drawn_inputs(seed))
    spreads = {'L0_ffn_ln_w': (1.0, 0.6), 'L0_ffn_ln_b': (0.0, 0.8)}
    factors = {'L0_ffn_b1s': 8.0, 'L0_ffn_b2s': 8.0}
    for name, (base, spread) in spreads.items():
        noise = np.random.default_rng([zlib.crc32(name.encode()), seed]).standard_normal(out[name].shape)
        drawn = base * np.exp(spread * noise) if base else spread * noise
        out[name] = jnp.asarray(drawn.astype(out[name].dtype))
    for name, factor in factors.items():
        out[name] = (out[name] * factor).astype(out[name].dtype)
    return out
```

```python
from contextlib import ExitStack

import concourse.bass as bass
from concourse import mybir

F32 = mybir.dt.float32
BF16 = mybir.dt.bfloat16
I32 = mybir.dt.int32
U32 = mybir.dt.uint32
ALU = mybir.AluOpType
ACT = mybir.ActivationFunctionType
AX = mybir.AxisListType
P = 128


class Tally:

    def __init__(self, sem):
        self.sem, self.n, self.base = sem, 0, 0

    def inc(self, instruction, by=1):
        instruction.then_inc(self.sem, by)
        self.n += by
        return self.n

    def now(self):
        return self.n + self.base if not isinstance(self.base, int) or self.base else self.n


def macaron_block(nc, x, wq, wk, wv, wo, pek, pev, gate_w, ln_w, ln_b, fc1s, b1s, fc2s, b2s, out):
    NB, L, D = x.shape
    E, FF, _ = fc1s.shape
    TOK = NB * L
    NT = TOK // P
    CAP = TOK // E
    NJ = CAP // P
    NC = FF // P
    ET = E * NT
    GW = D + E
    EPS = 1e-5
    SCORE_BITS = 30
    LO, HI = 32, CAP // 32
    assert D == P and NJ == 4 and NT == 32 and E == 8 and NC == 4

    ctx = ExitStack()
    with ctx:
        def sem(name):
            return ctx.enter_context(nc.semaphore(name))

        ARENA = 52000
        arena = ctx.enter_context(nc.sbuf_tensor("arena", [P, ARENA], F32))
        psum = ctx.enter_context(nc.psum_tensor("banks", [P, 8, 512], F32))
        taken = [0]
        H, HD = 16, D // 16
        NP = NB // 2
        PT = 2 * L
        TERMS = 6
        Q_PART = (0, 0, 1, 1, 0, 2)
        K_PART = (0, 1, 0, 1, 2, 0)
        BIG = 1e30
        PW = 384
        assert L == 2 * P and H * HD == D and TERMS * 2 * HD <= 96

        def place(words, at=None):
            at = taken[0] if at is None else at
            taken[0] = max(taken[0], at + words)
            assert taken[0] <= ARENA, taken[0]
            return arena[:, at:at + words], at

        ident, _ = place(P)
        ones_bf = place(P // 2)[0].bitcast(BF16)
        before_bf = place(P // 2)[0].bitcast(BF16)
        iota_lo = place(LO // 2)[0].bitcast(BF16)
        iota_p = place(1)[0]
        carry, _ = place(ET)
        ones_row, _ = place(P)
        gwT, _ = place(E)
        b1T, _ = place(E * NC)
        b2row, _ = place(E * D)
        lnw, _ = place(1)
        lnb, _ = place(1)
        iota_i, _ = place(LO)
        wT = place(4 * D)[0].rearrange("p (w d) -> p w d", w=4)
        rel_k = place(PW // 2)[0].bitcast(BF16)
        stats = place(NT * 6)[0].rearrange("p (t s) -> p t s", s=6)
        mv = place(NT * 2)[0].rearrange("p (t s) -> p t s", s=2)
        vare, s0, r0, rstd = (place(NT)[0] for _ in range(4))
        x_sb, _ = place(NT * D)
        x_sb = x_sb.rearrange("p (t d) -> p t d", d=D)
        PHASE = taken[0]

        xn, at_xn = place(NT * D)
        xn = xn.rearrange("p (t d) -> p t d", d=D)
        xnT, _ = place(NT * D)
        zt, _ = place(NT * GW)
        zt = zt.rearrange("p (t g) -> p t g", g=GW)
        w1T, _ = place(E * FF)
        w1T = w1T.rearrange("p (e f) -> p e f", e=E)
        w2T, _ = place(E * FF)
        w2T = w2T.rearrange("p (e c d) -> p e c d", e=E, c=NC)
        raw1, at_raw1 = place(E * FF)
        raw1 = raw1.rearrange("p (e c d) -> p e c d", e=E, c=NC)
        raw2, at_raw2 = place(E * FF)
        raw2 = raw2.rearrange("p (e f) -> p e f", e=E)
        hT, _ = place(2 * NC * CAP)
        hT = hT.rearrange("p (b c s) -> p b c s", b=2, c=NC)
        yT, _ = place(2 * CAP)
        yT = yT.rearrange("p (b s) -> p b s", b=2)
        osb, _ = place(2 * CAP)
        osb = osb.rearrange("p (b j d) -> p b j d", b=2, j=NJ)
        rows = place(E * NJ * GW, at_xn)[0].rearrange("p (s g) -> p s g", g=GW)
        hot_lo = place(ET * LO // 2, at_raw1)[0].bitcast(BF16).rearrange("p (n a) -> p n a", a=LO)
        hot_hi = place(ET * 2 * HI // 2, at_raw2)[0].bitcast(BF16).rearrange("p (n w b) -> p n w b", w=2, b=HI)
        lmax, lsum = place(NT)[0], place(NT)[0]
        logit, _ = place(ET)
        score, _ = place(ET)
        thr, bit, cand, pas, cnt, need = (place(E)[0] for _ in range(6))
        thr_i, bit_i, cand_i, pas_i = (a.bitcast(I32) for a in (thr, bit, cand, pas))
        mask_bf, gt_bf, eq_bf, sel_bf, tie_bf, lo_bf, hi_bf, hit_bf = (
            place(ET // 2)[0].bitcast(BF16) for _ in range(8))
        scan, rank, pos = (place(ET)[0] for _ in range(3))
        pos_i, lo_i, hi_i = (place(ET)[0].bitcast(I32) for _ in range(3))
        idx_p, _ = place(E * HI)
        idx_i = place(E * HI)[0].bitcast(I32)
        idx = place(E * NJ)[0].bitcast(U32)
        eqhi = place(ET * HI // 2)[0].bitcast(BF16).rearrange("p (n b) -> p n b", b=HI)

        taken[0] = PHASE
        probs, at_probs = place(3 * 2 * H * P)
        probs = probs.rearrange("p (k n q) -> p k n q", k=3, n=2 * H)
        q_st, at_q = place(2 * H * PT // 2)
        q_st = q_st.bitcast(BF16).rearrange("p (r h c n) -> p r h c n", r=2, h=H, c=2)
        k_st = place(2 * H * PT // 2)[0].bitcast(BF16).rearrange("p (r h n) -> p r h n", r=2, h=H)
        v_all = place(NT * H * 9)[0].rearrange("p (t h n) -> p t h n", t=NT, h=H)
        v_pair = place(2 * 4 * H * 9)[0].rearrange("p (r t h n) -> p r t h n", r=2, t=4, h=H)
        rel_v = place(2 * P * HD)[0]
        m_row = place(3 * 512)[0].bitcast(BF16).rearrange("p (r n) -> p r n", r=3)
        m_part = place(3 * 32)[0].rearrange("p (r n) -> p r n", r=3)
        m_neg = place(32)[0]
        m_hl = place(3 * 32)[0].bitcast(BF16).rearrange("p (r w n) -> p r w n", r=3, w=2)
        o_sb = place(2 * 512)[0].rearrange("p (r g n) -> p r g n", r=2, g=4)
        r_tmp = place(512)[0]
        r_sb = place(2 * H * 16)[0].rearrange("p (h b u) -> p h b u", h=H, b=2)
        own_q = place(4)[0]
        lane_i, lane_f = place(1)[0].bitcast(I32), place(1)[0]
        assert taken[0] <= ARENA
        an = place(NT * D, at_probs)[0].rearrange("p (t d) -> p t d", d=D)
        anT = place(NT * D, at_probs + NT * D)[0]
        part = place(4 * 3 * 256, at_probs + 2 * NT * D)[0].bitcast(BF16).rearrange("p (r w n) -> p r w n", r=4, w=3)
        rest = place(2 * 512, at_probs + 2 * NT * D + 3072)[0].rearrange("p (r n) -> p r n", r=2)
        o_all = place(TOK, at_q)[0]
        o_sum = place(TOK, at_q + TOK)[0]
        o_rel = place(TOK, at_q + 2 * TOK)[0].rearrange("p (c u) -> p c u", c=16)
        o_nat = place(TOK, at_q + 3 * TOK)[0]

        def by_et(a):
            return a.rearrange("p (e t) -> p e t", e=E)

        def spread(a, n):
            return a.unsqueeze(2).to_broadcast([P, a.shape[1], n])

        table = [nc.dram_tensor(f"table{n}", [TOK, GW], F32).ap() for n in range(2)]
        x_mid = nc.dram_tensor("x_mid", [TOK, D], F32).ap()
        out_rows = out.rearrange("b l d -> (b l) d")
        total = [x_mid, out_rows]
        qs = nc.dram_tensor("query_parts", [3, D, TOK], BF16).ap()
        ks = nc.dram_tensor("key_parts", [3, D, TOK], BF16).ap()
        pv_ext = nc.dram_tensor("rel_v_extended", [PW, HD], F32).ap()
        o_dram = nc.dram_tensor("head_outputs", [P, 4, TOK], F32).ap()
        r_dram = nc.dram_tensor("relative_outputs", [P, H, 2 * P], F32).ap()

        s_par = sem("parameters_loaded")
        s_raw = sem("raw_weights_loaded")
        s_x = [sem(f"x_loaded{c}") for c in range(4)]
        s_const = sem("constants_ready")
        s_dve = Tally(sem("vector_steps"))
        s_pool = Tally(sem("pool_steps"))
        s_act = Tally(sem("scalar_steps"))
        s_sqrt_in, s_sqrt = sem("variance_ready"), sem("root_ready")
        s_tr = sem("transposed_bank")
        s_trf = sem("transposed_bank_read")
        s_xn = sem("xn_ready")
        s_z = sem("table_rows_ready")
        s_init = sem("residual_ready")
        s_logit = sem("logits_ready")
        s_centred = sem("logits_centred")
        s_exp = sem("exp_ready")
        s_mask, s_cnt, s_cntr = sem("mask_ready"), sem("counts_ready"), sem("counts_read")
        s_pre, s_prer = sem("prefix_asked"), sem("prefix_ready")
        s_hot, s_idx = sem("one_hots_ready"), sem("index_sums_ready")
        s_idxi, s_idxd = sem("indices_ready"), sem("indices_spread")
        s_tab, s_acc = sem("table_stored"), sem("residual_stored")
        s_rows = [sem(f"rows_gathered{e}") for e in range(E)]
        s_yT = sem("yT_ready")
        s_h, s_g = sem("fc1_ready"), sem("gelu_ready")
        s_o, s_os = sem("fc2_ready"), sem("out_scaled")
        s_sc = sem("scattered")
        s_back = sem("x_reloaded")
        s_ffn = sem("experts_done")
        s_pe1 = sem("rel_v_extended_stored")
        s_rk = sem("rel_k_rows_loaded")
        s_rv = sem("rel_v_loaded")
        s_ext = sem("rel_k_parts_ready")
        s_an, s_anT = sem("attention_input_ready"), sem("attention_input_transposed")
        s_pj, s_p1, s_p1r = sem("projection_ready"), sem("first_part_ready"), sem("rest_ready")
        s_p2, s_part, s_pst = sem("second_part_ready"), sem("parts_ready"), [sem(f"parts_stored{i}") for i in range(4)]
        s_vp, s_vr = sem("values_projected"), sem("values_read")
        s_zero = sem("attention_buffers_cleared")
        s_load = [sem(f"pair_loaded{i}") for i in range(2)]
        s_vpair = sem("pair_values_ready")
        s_score, s_T, s_tT = sem("scores_ready"), sem("partial_maxima_ready"), sem("maxima_transposed")
        s_row = sem("negated_maxima_ready")
        s_m = [sem(f"maxima_row_loaded{i}") for i in range(3)]
        s_sub, s_prob = sem("maxima_subtracted"), sem("probabilities_ready")
        s_chunk, s_chr = sem("outputs_ready"), sem("head_outputs_read")
        s_rr, s_rrd = sem("relative_outputs_reduced"), sem("relative_bank_read")
        s_ost = [sem(f"head_outputs_stored{i}") for i in range(2)]
        s_rst = sem("relative_outputs_stored")
        s_fin, s_nat = sem("outputs_loaded"), sem("outputs_normalised")
        s_wo, s_wor = sem("output_projected"), sem("output_added")

        block = ctx.enter_context(nc.Block())

        TR = (0, 1)
        B_GATE, B_CNT, B_IDX = 2, 3, 3
        H_B, O_B = (4, 5), (6, 7)

        NWB = 2 * E
        NXB = NT // 4
        NAB = NWB + NXB
        NYB = E
        TRN = NWB + NXB + NYB

        ext = osb.rearrange("p b j d -> p (b j d)")[0:HD, 0:PW]
        ext_rest = osb.rearrange("p b j d -> p (b j d)")[0:HD, PW:2 * PW]
        ext_part = yT.rearrange("p b s -> p (b s)").bitcast(BF16)[0:HD, 0:3 * PW].rearrange("p (w n) -> p w n", w=3)

        def in_pairs(engine, pair):
            pair(0, 0, 0)
            with engine.Fori(0, NP // 2 - 1) as i:
                pair(2 * i + 1, 1, i)
                pair(2 * i + 2, 0, i + 1)
            pair(NP - 1, 1, NP // 2 - 1)

        def reach(engine, semaphore, value):
            if not isinstance(value, int) or value > 0:
                engine.wait_ge(semaphore, value)

        SLOTS = [(0, 0, False), (0, 2, False), (1, 0, False), (1, 2, False)] + \
                [(b, q, True) for b in range(2) for q in range(4, 8)]
        NS = len(SLOTS)
        CHUNK_AT = {2: 0, 3: 1, 4: 2, 5: 3, 7: 4, 8: 5, 9: 6, 10: 7}
        T_BANK, O_BANK = 6, 7

        def tr_bank(k):
            return psum[:, TR[k % 2], :]

        @block.sync
        def _(sp):
            xr = x.rearrange("b l d -> (b l) d").rearrange("(t p) d -> p t d", p=P)
            for c in range(4):
                sp.dma_start(x_sb[:, 8 * c:8 * c + 8, :], xr[:, 8 * c:8 * c + 8, :]).then_inc(s_x[c], 16)
            sp.dma_start(logit[0:E, 0:D], gate_w).then_inc(s_par, 16)
            sp.dma_start(logit[0:E * NC, D:2 * D], b1s.rearrange("e (c p) -> (e c) p", p=P)).then_inc(s_par, 16)
            sp.dma_start(b2row[0:1, :], b2s.rearrange("e d -> (e d)").unsqueeze(0)).then_inc(s_par, 16)
            sp.dma_start(lnw, ln_w.unsqueeze(1)).then_inc(s_par, 16)
            sp.dma_start(lnb, ln_b.unsqueeze(1)).then_inc(s_par, 16)
            for i, w in enumerate((wq, wk, wv, wo)):
                sp.dma_start(hT[:, 0, i, 0:D], w).then_inc(s_par, 16)
            sp.dma_start(hT[:, 1, 0, 0:2 * HD].rearrange("p (t d) -> p t d", t=2),
                         pek[0:2 * P, :].rearrange("(t p) d -> p t d", p=P)).then_inc(s_par, 16)
            sp.dma_start(pv_ext[0:P - 1, :], pev[0:1, :].to_broadcast([P - 1, HD])).then_inc(s_pe1, 16)
            sp.dma_start(pv_ext[P - 1:3 * P - 1, :], pev[0:2 * P, :]).then_inc(s_pe1, 16)

            def expert_layer(n):
                if n:
                    sp.wait_ge(s_wor, NT // 4)
                for h in range(2):
                    es = slice(4 * h, 4 * h + 4)
                    sp.dma_start(raw1[:, es], fc1s[es].rearrange("e (c p) d -> p e c d", p=P)).then_inc(s_raw, 16)
                    sp.dma_start(raw2[:, es], fc2s[es].rearrange("e d f -> d e f")).then_inc(s_raw, 16)
                sp.wait_ge(s_init, n + 1)
                sp.dma_start(total[n].rearrange("(t p) d -> p t d", p=P), x_sb).then_inc(s_acc, 16)
                sp.wait_ge(s_z, n + 1)
                sp.dma_start(table[n].rearrange("(t p) g -> p t g", p=P), zt).then_inc(s_tab, 16)
                sp.wait_ge(s_idxi, n + 1)
                for r in range(4):
                    sp.dma_start(idx[32 * r:32 * r + 32, :],
                                 idx_i[0:32, 32 * r:32 * r + 32].bitcast(U32)).then_inc(s_idxd, 16)

            sp.wait_ge(s_ext, 1)
            sp.wait_ge(s_const, 8)
            for t in range(TERMS):
                for c in range(2):
                    r = (2 * t + c) * HD
                    sp.dma_start(rel_k[r:r + HD, 0:PW - 2], ext_part[:, K_PART[t], 1 - c:PW - 1 - c]).then_inc(s_rk, 16)

            def attention():
                sp.wait_ge(s_ffn, 1)
                xm = x_mid.rearrange("(t p) d -> p t d", p=P)
                for c in range(4):
                    sp.dma_start(x_sb[:, 8 * c:8 * c + 8, :], xm[:, 8 * c:8 * c + 8, :]).then_inc(s_x[c], 16)
                sp.wait_ge(s_pe1, 32)
                sp.dma_start(rel_v, bass.AP(pv_ext.tensor, 0, [[HD, P], [1, 2 * P * HD]])).then_inc(s_rv, 16)
                for i in range(2 * NP):
                    sp.wait_ge(s_part, i + 1)
                    dst = (qs if i % 2 == 0 else ks)[:, :, PT * (i // 2):PT * (i // 2) + PT]
                    sp.dma_start(dst.rearrange("w d n -> d w n"), part[:, i % 4]).then_inc(s_pst[i % 4], 16)

                def pair(pr, r, k):
                    for s in range(NS):
                        sp.wait_ge(s_row, NS * pr + s + 1)
                        for w in range(2):
                            sp.dma_start(m_row[w:w + 1, s % 3, :].rearrange("o (a b) -> o a b", a=32),
                                         m_hl[0:32, s % 3, w, :]).then_inc(s_m[s % 3], 16)

                in_pairs(sp, pair)
                for i in range(2):
                    sp.wait_ge(s_ost[i], 16 * 2 * NP)
                sp.wait_ge(s_rst, 16 * NP)
                for g in range(4):
                    lanes = slice(32 * g, 32 * g + 32)
                    src = o_dram[:, g, :].rearrange("(j d) n -> j d n", j=4)
                    sp.dma_start(o_all[lanes, :], src[:, 0:HD, :]).then_inc(s_fin, 16)
                    sp.dma_start(o_sum[lanes, :], src[:, HD:HD + 1, :].to_broadcast([4, HD, TOK])).then_inc(s_fin, 16)
                for c in range(16):
                    sp.dma_start(o_rel[:, c, :], r_dram[HD * c:HD * c + HD, :, :].rearrange("d h n -> h d n")
                                 ).then_inc(s_fin, 16)

            expert_layer(0)
            attention()
            expert_layer(1)

        @block.gpsimd
        def _(pool):
            def step(i):
                s_pool.inc(i)
                pool.wait_ge(s_pool.sem, s_pool.now())

            step(pool.memset(ident, 0.0))
            pool.affine_select(out=ident, in_=ident, compare_op=ALU.not_equal, fill=1.0, base=0,
                               pattern=[[-1, P]], channel_multiplier=1).then_inc(s_const, 1)
            step(pool.memset(before_bf, 0.0))
            pool.affine_select(out=before_bf, in_=before_bf, compare_op=ALU.is_ge, fill=1.0, base=0,
                               pattern=[[-1, P]], channel_multiplier=1).then_inc(s_const, 1)
            pool.memset(ones_bf, 1.0).then_inc(s_const, 1)
            pool.memset(ones_row, 1.0).then_inc(s_const, 1)
            step(pool.memset(carry, 1.0))
            pool.memset(by_et(carry)[:, :, 0:1], 0.0).then_inc(s_const, 1)
            step(pool.iota(iota_i.bitcast(I32), pattern=[[1, LO]], base=0, channel_multiplier=0))
            pool.tensor_copy(iota_lo, iota_i.bitcast(I32)).then_inc(s_const, 1)
            step(pool.iota(cand_i[:, 0:1], pattern=[[0, 1]], base=0, channel_multiplier=1))
            pool.tensor_copy(iota_p, cand_i[:, 0:1]).then_inc(s_const, 1)

            step(pool.memset(rel_k, 0.0))
            pool.affine_select(out=rel_k[96:P, :], in_=rel_k[96:P, :], compare_op=ALU.is_ge, fill=-BIG,
                               base=2 * P - 2, pattern=[[-1, PW]], channel_multiplier=1).then_inc(s_const, 1)

            def expert_layer(n):
                pool.wait_ge(s_idxd, 64 * (n + 1))
                pool.wait_ge(s_tab, 16 * (n + 1))
                for e in range(E):
                    for j in range(NJ):
                        s = e * NJ + j
                        pool.indirect_dma_start(
                            out=rows[:, s, :], out_offset=None, in_=table[n],
                            in_offset=bass.IndirectOffsetOnAxis(ap=idx[:, s:s + 1], axis=0)).then_inc(s_rows[e], 16)
                pool.wait_ge(s_acc, 16 * (n + 1))
                for e in range(E):
                    pool.wait_ge(s_os, n * E + e + 1)
                    if e:
                        pool.wait_ge(s_sc, 64 * (n * E + e))
                    for j in range(NJ):
                        s = e * NJ + j
                        pool.indirect_dma_start(
                            out=total[n], out_offset=bass.IndirectOffsetOnAxis(ap=idx[:, s:s + 1], axis=0),
                            in_=osb[:, e % 2, j, :], in_offset=None, compute_op=ALU.add).then_inc(s_sc, 16)
                pool.wait_ge(s_sc, 64 * (n + 1) * E)
                pool.nop().then_inc(s_ffn, 1)

            def settled(semaphore, value):
                reach(pool, semaphore, value)
                pool.wait_ge(s_const, 8)

            def stacked(pr, r):
                for t in range(TERMS):
                    q = qs[Q_PART[t]].rearrange("(h d) n -> d h n", d=HD)
                    k = ks[K_PART[t]].rearrange("(h d) n -> d h n", d=HD)
                    for c in range(2):
                        lanes = slice((2 * t + c) * HD, (2 * t + c + 1) * HD)
                        yield q_st[lanes, r, :, c, :], q[:, :, bass.ds(pr * PT + c * L, L)]
                        yield k_st[lanes, r, :, :], k[:, :, bass.ds(pr * PT, PT)]

            def attention():
                for a in (q_st, k_st):
                    last = pool.memset(a, 0.0)
                step(last)
                for r in range(2):
                    step(pool.affine_select(out=q_st[96:P, r], in_=q_st[96:P, r], compare_op=ALU.not_equal, fill=1.0,
                                            base=0, pattern=[[0, H], [-1, 2], [0, L]], channel_multiplier=1))
                pool.memset(v_all[:, :, :, HD:HD + 1], 1.0)
                step(pool.memset(m_row, 0.0))
                for i in range(4):
                    pool.wait_ge(s_pst[i], 16 * (NP // 2))
                for dst, src in stacked(0, 0):
                    pool.dma_start(dst, src).then_inc(s_load[0], 16)

                def pair(pr, r, k):
                    first, last = isinstance(pr, int) and pr == 0, isinstance(pr, int) and pr == NP - 1
                    if first:
                        pool.wait_ge(s_vr, NT // 4)
                    if not first:
                        settled(s_chunk, 8 * pr - 7)
                    pool.tensor_copy(v_pair[:, r], v_all[:, bass.ds(pr * 4, 4)]).then_inc(s_vpair, 1)
                    loads = [] if last else list(stacked(pr + 1, 1 - r))
                    if loads:
                        settled(s_score, NS * pr)

                    def load_some(n):
                        for dst, src in loads[:n]:
                            pool.dma_start(dst, src).then_inc(s_load[1 - r], 16)
                        del loads[:n]

                    def store_heads(i, b, q):
                        settled(s_chr, 4 * pr + i - 1)
                        pool.dma_start(o_dram[:, :, bass.ds(b * L + q * P, P)], o_sb[:, i % 2]
                                       ).then_inc(s_ost[i % 2], 16)

                    def store_relative(before):
                        settled(s_rr, 4 * before + 4)
                        pool.dma_start(r_dram[:, :, bass.ds(before * 32, 32)],
                                       r_sb.rearrange("p h b u -> p h (b u)")).then_inc(s_rst, 16)

                    load_some(6)
                    if not first:
                        store_heads(0, 2 * pr - 2, 1)
                        load_some(4)
                        store_heads(1, 2 * pr - 1, 1)
                        load_some(4)
                        store_relative(pr - 1)
                    load_some(4)
                    store_heads(2, 2 * pr, 0)
                    load_some(4)
                    store_heads(3, 2 * pr + 1, 0)
                    load_some(len(loads))
                    if last:
                        for b in range(2):
                            pool.wait_ge(s_chr, 4 * NP + b - 1)
                            pool.dma_start(o_dram[:, :, (2 * pr + b) * L + P:(2 * pr + b) * L + 2 * P],
                                           o_sb[:, b]).then_inc(s_ost[b], 16)
                        store_relative(pr)

                in_pairs(pool, pair)

            expert_layer(0)
            attention()
            expert_layer(1)

        @block.scalar
        def _(act):
            act.wait_ge(s_tr, 1)
            nc.scalar.copy(b1T, tr_bank(0)[:, 0:E * NC])
            nc.scalar.copy(gwT, tr_bank(0)[:, E * NC:E * NC + E])
            nc.scalar.copy(ext[:, P - 1:3 * P - 1], tr_bank(0)[0:HD, P:3 * P])
            nc.scalar.copy(ext[:, 0:P - 1], tr_bank(0)[0:HD, P:P + 1].to_broadcast([HD, P - 1]))
            nc.scalar.copy(ext[:, 3 * P - 1:3 * P], tr_bank(0)[0:HD, P:P + 1]).then_inc(s_trf, 1)
            act.wait_ge(s_tr, 2)
            nc.scalar.copy(wT, tr_bank(1).rearrange("p (w d) -> p w d", w=4)).then_inc(s_trf, 1)

            def expert_layer(n):
                tr = 2 + n * TRN + (NXB if n else 0)
                for k in range(NWB):
                    act.wait_ge(s_tr, tr + k + 1)
                    if k % 2 == 0:
                        nc.scalar.copy(w1T[:, k // 2, :], tr_bank(tr + k)).then_inc(s_trf, 1)
                    else:
                        nc.scalar.copy(w2T[:, k // 2, :, :],
                                       tr_bank(tr + k).rearrange("p (c d) -> p c d", c=NC)).then_inc(s_trf, 1)
                act.wait_ge(s_sqrt_in, 3 * n + 1)
                nc.scalar.activation(s0, vare, ACT.Sqrt).then_inc(s_sqrt, 1)
                for k in range(NXB):
                    act.wait_ge(s_tr, tr + NWB + k + 1)
                    nc.scalar.copy(xnT[:, 512 * k:512 * k + 512], tr_bank(tr + NWB + k)).then_inc(s_trf, 1)
                act.wait_ge(s_sqrt_in, 3 * n + 2)
                nc.scalar.activation(s0, vare, ACT.Sqrt).then_inc(s_sqrt, 1)
                act.wait_ge(s_centred, n + 1)
                nc.scalar.activation(logit, logit, ACT.Exp).then_inc(s_exp, 1)
                for e in range(E):
                    for c in range(NC):
                        k = (n * E + e) * NC + c
                        act.wait_ge(s_h, k + 1)
                        if e >= 2 or n:
                            act.wait_ge(s_o, n * E + e - 1)
                        nc.scalar.activation(hT[:, e % 2, c, :], psum[:, H_B[k % 2], :], ACT.Gelu_apprx_tanh,
                                             bias=b1T[:, e * NC + c:e * NC + c + 1]).then_inc(s_g, 1)

            def attention():
                act.wait_ge(s_sqrt_in, 3)
                nc.scalar.activation(s0, vare, ACT.Sqrt).then_inc(s_sqrt, 1)
                for k in range(NXB):
                    act.wait_ge(s_tr, 2 + TRN + k + 1)
                    nc.scalar.copy(anT[:, 512 * k:512 * k + 512], tr_bank(2 + TRN + k)).then_inc(s_trf, 1)

                def first_part(i):
                    act.wait_ge(s_pj, i + 1)
                    if i >= 4:
                        act.wait_ge(s_pst[i % 4], 16 * (i // 4))
                    nc.scalar.copy(part[:, i % 4, 0, :], psum[:, 2 + i % 2, :]).then_inc(s_p1, 1)

                def second_part(i):
                    act.wait_ge(s_p1r, i + 1)
                    nc.scalar.copy(part[:, i % 4, 1, :], rest[:, i % 2, :]).then_inc(s_p2, 1)

                first_part(0)
                for i in range(2 * NP):
                    if i + 1 < 2 * NP:
                        first_part(i + 1)
                    second_part(i)
                for k in range(NT // 4):
                    act.wait_ge(s_vp, k + 1)
                    nc.scalar.copy(v_all[:, 4 * k:4 * k + 4, :, 0:HD],
                                   psum[:, 4 + k % 2, :].rearrange("p (t h d) -> p t h d", t=4, h=H)).then_inc(s_vr, 1)

                def exp(s, pr):
                    b, q, later = SLOTS[s]
                    s, g = s % NS, NS * pr + s
                    act.wait_ge(s_sub, g + 1)
                    if s == 0:
                        reach(act, s_chunk, 8 * pr - 4)
                    if s == 4:
                        reach(act, s_chunk, 8 * pr)
                    heads = slice(H * b, H * b + H)
                    if later:
                        dst = probs[:, 1:3, heads, 32 * (q - 4):32 * (q - 4) + 32]
                    else:
                        dst = probs[:, 0, heads, 32 * q:32 * q + 64].rearrange("p h (u n) -> p u h n", u=2)
                    r = s % 3
                    nc.scalar.activation(dst, psum[:, 2 * r:2 * r + 2, :].rearrange("p u (h n) -> p u h n", h=H),
                                         ACT.Exp, scale=HD ** -0.5).then_inc(s_prob, 1)

                def read_heads(pr, i):
                    act.wait_ge(s_chunk, 8 * pr + (i if i < 2 else i + 2) - 3)
                    reach(act, s_ost[i % 2], 16 * (2 * pr + (-1 if i < 2 else 0)))
                    nc.scalar.copy(o_sb[:, i % 2], psum[:, O_BANK, :].rearrange("p (g n) -> p g n", g=4)
                                   ).then_inc(s_chr, 1)

                def pair(pr, r, k):
                    first = isinstance(pr, int) and pr == 0
                    for s in range(NS):
                        if s - 1 in (2, 3) and not first:
                            read_heads(pr, s - 3)
                        if s - 1 in (7, 8):
                            read_heads(pr, s - 6)
                        if s >= 2 or not first:
                            exp(s - 2, pr)

                in_pairs(act, pair)
                for s in (-2, -1):
                    exp(s, NP)
                for i in range(2):
                    read_heads(NP, i)

            expert_layer(0)
            attention()
            expert_layer(1)

        @block.tensor
        def _(pe):
            pe.wait_ge(s_const, 8)
            pe.wait_ge(s_par, 160)
            pe.transpose(tr_bank(0)[:, 0:E * NC], logit[0:E * NC, D:2 * D], ident[0:E * NC, 0:E * NC])
            pe.transpose(tr_bank(0)[:, E * NC:E * NC + E], logit[0:E, 0:D], ident[0:E, 0:E])
            for t in range(2):
                last = pe.transpose(tr_bank(0)[0:HD, P + P * t:2 * P + P * t], hT[:, 1, 0, HD * t:HD * t + HD], ident)
            last.then_inc(s_tr, 1)
            for i in range(4):
                last = pe.transpose(tr_bank(1)[:, D * i:D * i + D], hT[:, 0, i, 0:D], ident)
            last.then_inc(s_tr, 1)

            def expert_layer(n):
                tr = 2 + n * TRN + (NXB if n else 0)

                def bank_of(k):
                    read = 2 + n * (NAB + NXB) + k - 1
                    if k < NAB + 2:
                        pe.wait_ge(s_trf, read)
                    return tr_bank(tr + k)

                pe.wait_ge(s_raw, 64 * (n + 1))
                for k in range(NWB):
                    bank, e = bank_of(k), k // 2
                    for c in range(NC):
                        src = raw2[:, e, P * c:P * c + P] if k % 2 else raw1[:, e, c, :]
                        last = pe.transpose(bank[:, P * c:P * c + P], src, ident)
                    last.then_inc(s_tr, 1)
                for k in range(NXB):
                    pe.wait_ge(s_xn, n * NXB + k + 1)
                    bank = bank_of(NWB + k)
                    for c in range(4):
                        last = pe.transpose(bank[:, P * c:P * c + P], xn[:, 4 * k + c, :], ident)
                    last.then_inc(s_tr, 1)
                for t in range(NT):
                    if t % 4 == 0:
                        pe.wait_ge(s_trf, 2 + n * (NAB + NXB) + NWB + t // 4 + 1)
                    last = pe.matmul(psum[:, B_GATE, E * t:E * t + E], xnT[:, P * t:P * t + P], gwT,
                                     start=True, stop=True)
                last.then_inc(s_logit, 1)
                with pe.Fori(0, SCORE_BITS) as i:
                    pe.wait_ge(s_mask, i + n * SCORE_BITS + 1)
                    pe.matmul(psum[:, B_CNT, 0:ET], ones_bf, mask_bf, start=True, stop=True).then_inc(s_cnt, 1)
                pe.wait_ge(s_pre, 2 * n + 1)
                pe.matmul(psum[:, B_GATE, 0:ET], ones_bf, gt_bf, start=True, stop=True)
                pe.matmul(psum[:, B_CNT, 0:ET], ones_bf, eq_bf, start=True, stop=True)
                pe.matmul(psum[:, B_CNT, ET:2 * ET], before_bf, eq_bf, start=True, stop=True).then_inc(s_prer, 1)
                pe.wait_ge(s_pre, 2 * n + 2)
                pe.matmul(psum[:, B_GATE, 0:ET], ones_bf, sel_bf, start=True, stop=True)
                pe.matmul(psum[:, B_GATE, ET:2 * ET], before_bf, sel_bf, start=True, stop=True).then_inc(s_prer, 1)
                pe.wait_ge(s_hot, n + 1)
                for e in range(E):
                    for t in range(NT):
                        last = pe.matmul(psum[0:LO, B_IDX, 2 * HI * e:2 * HI * e + 2 * HI],
                                         hot_lo[:, e * NT + t, :],
                                         hot_hi[:, e * NT + t, :, :].rearrange("p w b -> p (w b)"),
                                         start=(t == 0), stop=(t == NT - 1))
                last.then_inc(s_idx, 1)

                def first_half(e):
                    pe.wait_ge(s_rows[e], 64 * (n + 1))
                    bank = bank_of(NWB + NXB + e)
                    for j in range(NJ):
                        last = pe.transpose(bank[:, P * j:P * j + P], rows[:, e * NJ + j, 0:D], ident)
                    last.then_inc(s_tr, 1)
                    pe.wait_ge(s_yT, n * E + e + 1)
                    for c in range(NC):
                        k = (n * E + e) * NC + c
                        if k >= 2:
                            pe.wait_ge(s_g, k - 1)
                        pe.matmul(psum[:, H_B[k % 2], :], w1T[:, e, P * c:P * c + P], yT[:, e % 2, :],
                                  start=True, stop=True).then_inc(s_h, 1)

                def second_half(e):
                    pe.wait_ge(s_g, (n * E + e + 1) * NC)
                    if n * E + e >= 2:
                        pe.wait_ge(s_os, n * E + e - 1)
                    for j in range(NJ):
                        o = psum[:, O_B[e % 2], P * j:P * j + P]
                        for c in range(NC):
                            pe.matmul(o, hT[:, e % 2, c, P * j:P * j + P], w2T[:, e, c, :],
                                      start=(c == 0), stop=False)
                        last = pe.matmul(o, ones_row[0:1, :], b2row[0:1, D * e:D * e + D], start=False, stop=True)
                    last.then_inc(s_o, 1)

                first_half(0)
                for e in range(1, E):
                    first_half(e)
                    second_half(e - 1)
                second_half(E - 1)

            def attention():
                for k in range(NXB):
                    pe.wait_ge(s_an, k + 1)
                    if k >= 2:
                        pe.wait_ge(s_trf, 2 + NAB + k - 1)
                    for c in range(4):
                        last = pe.transpose(tr_bank(2 + TRN + k)[:, P * c:P * c + P], an[:, 4 * k + c, :], ident)
                    last.then_inc(s_tr, 1)
                for i in range(2 * NP):
                    pe.wait_ge(s_trf, 2 + NAB + i // 2 + 1)
                    if i >= 2:
                        pe.wait_ge(s_p1r, i - 1)
                    cols = anT[:, PT * (i // 2):PT * (i // 2) + PT]
                    if i % 2 == 0:
                        cols = cols.rearrange("p (b a c) -> p c b a", b=2, c=2)
                    pe.matmul(psum[:, 2 + i % 2, :], wT[:, i % 2, :], cols, start=True, stop=True).then_inc(s_pj, 1)
                for k in range(NT // 4):
                    if k >= 2:
                        pe.wait_ge(s_vr, k - 1)
                    for t in range(4):
                        last = pe.matmul(psum[:, 4 + k % 2, P * t:P * t + P],
                                         anT[:, P * (4 * k + t):P * (4 * k + t) + P], wT[:, 2, :], start=True, stop=True)
                    last.then_inc(s_vp, 1)
                pe.wait_ge(s_p1r, 2 * NP)
                pe.wait_ge(s_vr, NT // 4)
                pe.wait_ge(s_rk, 16 * 2 * TERMS)
                pe.wait_ge(s_rv, 16)

                def scores(s, pr, r):
                    b, q, later = SLOTS[s]
                    reach(pe, s_prob, NS * pr + s - 2)
                    for u in range(2):
                        qu, kb = (q, u) if later else (q + u, 0)
                        sc = psum[:, 2 * (s % 3) + u, :].rearrange("p (h c a) -> p h c a", h=H, c=2)
                        for a in range(16):
                            y = 2 * P - 2 - 2 * (16 * qu + a) + P * kb
                            pe.matmul(sc[:, :, :, a], rel_k[:, y:y + P], q_st[:, r, :, :, P * b + 16 * qu + a],
                                      start=(a == 0), stop=False, skip_group_check=True)
                        for h in range(H):
                            last = pe.matmul(sc[:, h], k_st[:, r, h, L * b + P * kb:L * b + P * kb + P],
                                             q_st[:, r, h, :, P * b + 16 * qu:P * b + 16 * qu + 16],
                                             start=False, stop=False, skip_group_check=True)
                    last.then_inc(s_score, 1)

                def turn_maxima(s, pr):
                    g = NS * pr + s
                    pe.wait_ge(s_T, g + 1)
                    if not (isinstance(g, int) and g == 0):
                        reach(pe, s_row, g)
                    pe.transpose(psum[0:32, T_BANK, 0:P], m_part[:, s % 3, :], ident).then_inc(s_tT, 1)

                def subtract_maxima(s, pr):
                    pe.wait_ge(s_m[s % 3], 32 * (NS // 3 * pr + (s // 3) + 1))
                    for u in range(2):
                        last = pe.matmul(psum[:, 2 * (s % 3) + u, :], ones_bf, m_row[:, s % 3, 512 * u:512 * u + 512],
                                         start=False, stop=True, skip_group_check=True)
                    last.then_inc(s_sub, 1)

                def chunk(i, pr, r):
                    later, j4 = i < 4, i % 4
                    if j4 == 0:
                        reach(pe, s_prob, NS * pr + (0 if later else 4))
                        if later:
                            r = 1 - r
                        else:
                            pe.wait_ge(s_vpair, pr + 1)
                    if i in (0, 3, 4, 7):
                        reach(pe, s_rrd, 4 * pr + {0: -2, 3: -1, 4: 0, 7: 1}[i])
                    else:
                        reach(pe, s_chr, 4 * pr + {1: -1, 2: 0, 5: 1, 6: 2}[i])
                    blocks = ((1, 0), (2, 1)) if later else ((0, 0),)
                    if j4 < 2:
                        rv = 1 - r if later and j4 else r
                        for g in range(4):
                            for blk, kb in blocks:
                                for j in range(4):
                                    last = pe.matmul(psum[32 * j:32 * j + HD + 1, O_BANK, P * g:P * g + P],
                                                     v_pair[:, rv, 2 * j4 + kb, 4 * g + j, :],
                                                     probs[:, blk, H * j4 + 4 * g + j, :],
                                                     start=(kb == 0), stop=(kb == len(blocks) - 1), skip_group_check=True)
                    else:
                        for u in range(4):
                            for blk, kb in blocks:
                                for j in range(4):
                                    q0 = 16 * (4 * (j4 - 2) + u) + 4 * j
                                    x = 2 * P - 4 - (q0 + (P if later else 0) - P * kb)
                                    at, a = 32 * (q0 // 32), q0 % 32 // 2
                                    qs4 = probs[:, blk, :, at:at + 32].rearrange("p n (c a) -> p n c a", c=2)
                                    last = pe.matmul(psum[32 * j:32 * j + 32, O_BANK, P * u:P * u + P],
                                                     rel_v[:, HD * x:HD * x + 32], qs4[:, :, :, a:a + 2],
                                                     start=(kb == 0), stop=(kb == len(blocks) - 1), skip_group_check=True)
                    last.then_inc(s_chunk, 1)

                def pair(pr, r, k):
                    first = isinstance(pr, int) and pr == 0
                    pe.wait_ge(s_load[r], 16 * 4 * TERMS * (k + 1))
                    for s in range(NS):
                        scores(s, pr, r)
                        if s >= 1 or not first:
                            turn_maxima(s - 1, pr)
                        if s >= 2 or not first:
                            subtract_maxima(s - 2, pr)
                        i = CHUNK_AT.get(s)
                        if i is not None and (i >= 4 or not first):
                            chunk(i, pr, r)

                in_pairs(pe, pair)
                turn_maxima(-1, NP)
                subtract_maxima(-2, NP)
                subtract_maxima(-1, NP)
                for i in range(4):
                    chunk(i, NP, 0)
                for k in range(NT // 4):
                    pe.wait_ge(s_nat, k // 2 + 1)
                    if k >= 2:
                        pe.wait_ge(s_wor, k - 1)
                    for t in range(4):
                        last = pe.matmul(psum[:, 2 + k % 2, P * t:P * t + P],
                                         o_nat[:, P * (4 * k + t):P * (4 * k + t) + P], wT[:, 3, :], start=True, stop=True)
                    last.then_inc(s_wo, 1)

            expert_layer(0)
            attention()
            expert_layer(1)

        @block.vector
        def _(dve):
            v = nc.vector

            def step(i):
                s_dve.inc(i)
                dve.wait_ge(s_dve.sem, s_dve.now())

            def normalise(src, dst, root, done=None):
                for t in range(NT):
                    if root == 0 and t % 8 == 0:
                        dve.wait_ge(s_x[t // 8], 16)
                    last = v.bn_stats(stats[:, t, :], src[:, t, :])
                step(last)
                for t in range(NT):
                    last = v.bn_aggr(mv[:, t, :], stats[:, t, :])
                step(last)
                v.tensor_scalar(vare, mv[:, :, 1], EPS, None, ALU.add).then_inc(s_sqrt_in, 1)
                dve.wait_ge(s_sqrt, root + 1)
                step(v.reciprocal(r0, s0))
                step(v.tensor_tensor(r0, r0, vare, ALU.mult))
                step(v.tensor_tensor(r0, r0, s0, ALU.add))
                step(v.tensor_scalar(r0, r0, 0.5, None, ALU.mult))
                step(v.reciprocal(rstd, r0))
                for t in range(NT):
                    i = v.tensor_scalar(dst[:, t, 0:D], src[:, t, :], mv[:, t, 0:1], rstd[:, t:t + 1],
                                        ALU.subtract, ALU.mult)
                    if done is not None and t % 4 == 3:
                        i.then_inc(done, 1)

            def expert_layer(n):
                tr = 2 + n * TRN + (NXB if n else 0)
                if n:
                    dve.wait_ge(s_wor, NT // 4)
                normalise(x_sb, xn, 3 * n, s_xn)
                dve.wait_ge(s_xn, (n + 1) * NXB)
                v.scalar_tensor_tensor(out=x_sb, in0=xn, scalar=0.5, in1=x_sb, op0=ALU.mult,
                                       op1=ALU.add).then_inc(s_init, 1)
                normalise(xn, zt, 3 * n + 1)
                dve.wait_ge(s_logit, n + 1)
                lg = psum[:, B_GATE, 0:ET].rearrange("p (t e) -> p t e", e=E)
                lv = logit.rearrange("p (t e) -> p t e", e=E)
                step(v.tensor_reduce(lmax, lg, AX.X, ALU.max))
                v.tensor_tensor(lv, lg, lmax.unsqueeze(2).to_broadcast([P, NT, E]),
                                ALU.subtract).then_inc(s_centred, 1)
                dve.wait_ge(s_exp, n + 1)
                step(v.tensor_reduce(lsum, lv, AX.X, ALU.add))
                step(v.reciprocal(lsum, lsum))
                v.tensor_tensor(by_et(score).rearrange("p e t -> p t e"), lv,
                                lsum.unsqueeze(2).to_broadcast([P, NT, E]), ALU.mult)
                step(v.memset(thr_i, 0))
                step(v.memset(bit_i, 1 << (SCORE_BITS - 1)))
                v.tensor_copy(zt[:, :, D:GW], by_et(score).rearrange("p e t -> p t e")).then_inc(s_z, 1)

                sc3 = by_et(score)
                PER = 4
                start = s_dve.n
                with dve.Fori(0, SCORE_BITS) as i:
                    s_dve.base = i * PER
                    step(v.tensor_tensor(cand_i, thr_i, bit_i, ALU.bitwise_or))
                    v.tensor_tensor(by_et(mask_bf), sc3, spread(cand, NT), ALU.is_ge).then_inc(s_mask, 1)
                    dve.wait_ge(s_cnt, i + n * SCORE_BITS + 1)
                    step(v.tensor_reduce(cnt, psum[:, B_CNT, 0:ET].rearrange("p (e t) -> p e t", e=E),
                                         AX.X, ALU.add))
                    step(v.tensor_scalar(pas_i, cnt, float(CAP), None, ALU.is_ge))
                    v.tensor_scalar(bit_i, bit_i, 1, None, ALU.logical_shift_right)
                    step(v.copy_predicated(thr_i, pas_i, cand_i))
                assert s_dve.n - start == PER
                s_dve.base = 0
                s_dve.n = start + PER * SCORE_BITS

                v.tensor_tensor(by_et(gt_bf), sc3, spread(thr, NT), ALU.is_gt)
                v.tensor_tensor(by_et(eq_bf), sc3, spread(thr, NT), ALU.is_equal).then_inc(s_pre, 1)
                dve.wait_ge(s_prer, 2 * n + 1)
                step(v.tensor_reduce(cnt, psum[:, B_GATE, 0:ET].rearrange("p (e t) -> p e t", e=E), AX.X, ALU.add))
                v.tensor_scalar(need, cnt, -1.0, float(CAP), ALU.mult, ALU.add)
                step(v.tensor_tensor_scan(scan, carry, psum[:, B_CNT, 0:ET], 0.0, ALU.mult, ALU.add))
                step(v.tensor_tensor(scan, scan, psum[:, B_CNT, 0:ET], ALU.subtract))
                step(v.tensor_tensor(rank, scan, psum[:, B_CNT, ET:2 * ET], ALU.add))
                step(v.tensor_tensor(by_et(tie_bf), by_et(rank), spread(need, NT), ALU.is_lt))
                step(v.tensor_tensor(tie_bf, tie_bf, eq_bf, ALU.mult))
                v.tensor_tensor(sel_bf, tie_bf, gt_bf, ALU.add).then_inc(s_pre, 1)
                dve.wait_ge(s_prer, 2 * n + 2)
                step(v.tensor_tensor_scan(scan, carry, psum[:, B_GATE, 0:ET], 0.0, ALU.mult, ALU.add))
                step(v.tensor_tensor(scan, scan, psum[:, B_GATE, 0:ET], ALU.subtract))
                step(v.tensor_tensor(rank, scan, psum[:, B_GATE, ET:2 * ET], ALU.add))
                step(v.scalar_tensor_tensor(out=pos, in0=sel_bf, scalar=-1024.0, in1=rank, op0=ALU.mult, op1=ALU.add))
                step(v.tensor_scalar(pos_i, pos, 1024.0, None, ALU.add))
                v.tensor_scalar(lo_i, pos_i, LO - 1, None, ALU.bitwise_and)
                step(v.tensor_scalar(hi_i, pos_i, 5, None, ALU.logical_shift_right))
                v.tensor_copy(lo_bf, lo_i)
                step(v.tensor_copy(hi_bf, hi_i))
                v.tensor_tensor(hot_lo, lo_bf.unsqueeze(2).to_broadcast([P, ET, LO]),
                                iota_lo.unsqueeze(1).to_broadcast([P, ET, LO]), ALU.is_equal)
                step(v.tensor_tensor(eqhi, hi_bf.unsqueeze(2).to_broadcast([P, ET, HI]),
                                     iota_lo[:, 0:HI].unsqueeze(1).to_broadcast([P, ET, HI]), ALU.is_equal))
                for e in range(E):
                    v.tensor_tensor(hot_hi[:, NT * e:NT * e + NT, 0, :], eqhi[:, NT * e:NT * e + NT, :],
                                    iota_lo.unsqueeze(2).to_broadcast([P, NT, HI]), ALU.mult)
                v.tensor_scalar(hot_hi[:, :, 1, :], eqhi, iota_p, None, ALU.mult).then_inc(s_hot, 1)
                dve.wait_ge(s_idx, n + 1)
                si = psum[0:LO, B_IDX, 0:2 * HI * E].rearrange("p (e w b) -> p e w b", e=E, w=2)
                ip = idx_p[0:LO, :].rearrange("p (e b) -> p e b", e=E)
                step(v.tensor_copy(ip, si[:, :, 1, :]))
                step(v.scalar_tensor_tensor(out=ip, in0=si[:, :, 0, :], scalar=float(P), in1=ip,
                                            op0=ALU.mult, op1=ALU.add))
                v.tensor_copy(idx_i[0:LO, :].rearrange("p (r e j) -> p r e j", r=4, e=E),
                              idx_p[0:LO, :].rearrange("p (e j r) -> p r e j", e=E, j=NJ)).then_inc(s_idxi, 1)

                def scale(e):
                    dve.wait_ge(s_o, n * E + e + 1)
                    if e >= 2:
                        dve.wait_ge(s_sc, 64 * (n * E + e - 1))
                    for j in range(NJ):
                        last = v.tensor_scalar(osb[:, e % 2, j, :], psum[:, O_B[e % 2], P * j:P * j + P],
                                               rows[:, e * NJ + j, D + e:D + e + 1], 0.5, ALU.mult, ALU.mult)
                    last.then_inc(s_os, 1)

                for e in range(E):
                    k = NWB + NXB + e
                    dve.wait_ge(s_tr, tr + k + 1)
                    if e >= 2:
                        dve.wait_ge(s_h, (n * E + e - 1) * NC)
                    if n == 0 and e == 0:
                        dve.wait_ge(s_rk, 16 * 2 * TERMS)
                    i = v.tensor_scalar(yT[:, e % 2, :], tr_bank(tr + k), lnw, lnb, ALU.mult, ALU.add)
                    i.then_inc(s_yT, 1)
                    if e:
                        scale(e - 1)
                scale(E - 1)

            dve.wait_ge(s_trf, 1)
            step(v.tensor_copy(ext_part[:, 0], ext))
            step(v.tensor_tensor(ext_rest, ext, ext_part[:, 0], ALU.subtract))
            step(v.tensor_copy(ext_part[:, 1], ext_rest))
            v.tensor_tensor(ext_part[:, 2], ext_rest, ext_part[:, 1], ALU.subtract).then_inc(s_ext, 1)

            def attention():
                for c in range(4):
                    dve.wait_ge(s_x[c], 32)
                normalise(x_sb, an, 2, s_an)
                dve.wait_ge(s_const, 7)
                step(v.tensor_copy(lane_i, iota_p))
                step(v.tensor_scalar(lane_i, lane_i, 3, 3, ALU.logical_shift_right, ALU.bitwise_and))
                step(v.tensor_copy(lane_f, lane_i))
                for c in range(2):
                    for a in range(2):
                        last = v.tensor_scalar(own_q[:, 2 * c + a:2 * c + a + 1], lane_f, float(3 - 2 * a - c), None,
                                               ALU.is_equal)
                step(last)

                def rest_of(i):
                    dve.wait_ge(s_p1, i + 1)
                    if i >= 2:
                        dve.wait_ge(s_part, i - 1)
                    v.tensor_tensor(rest[:, i % 2, :], psum[:, 2 + i % 2, :], part[:, i % 4, 0, :],
                                    ALU.subtract).then_inc(s_p1r, 1)

                def third_part(i):
                    dve.wait_ge(s_p2, i + 1)
                    v.tensor_tensor(part[:, i % 4, 2, :], rest[:, i % 2, :], part[:, i % 4, 1, :],
                                    ALU.subtract).then_inc(s_part, 1)

                rest_of(0)
                for i in range(2 * NP):
                    if i + 1 < 2 * NP:
                        rest_of(i + 1)
                    third_part(i)

                def partial_maxima(s, pr):
                    g = NS * pr + s
                    dve.wait_ge(s_score, g + 1)
                    later = SLOTS[s][2]
                    mp = m_part[:, s % 3, :]
                    i = v.tensor_reduce(mp, psum[:, 2 * (s % 3):2 * (s % 3) + 2, :].rearrange("p u (h n) -> p (u h) n", n=32),
                                        AX.X, ALU.max, apply_transpose=True)
                    if not later:
                        i.then_inc(s_T, 1)
                        return
                    step(i)
                    m2 = mp.rearrange("p (u h) -> p u h", u=2)
                    step(v.tensor_tensor(m2[:, 0, :], m2[:, 0, :], m2[:, 1, :], ALU.max))
                    v.tensor_copy(m2[:, 1, :], m2[:, 0, :]).then_inc(s_T, 1)

                def rows_of_maxima(s, pr):
                    g = NS * pr + s
                    dve.wait_ge(s_tT, g + 1)
                    hl = m_hl[0:32, s % 3]
                    step(v.tensor_reduce(m_neg[0:32, :], psum[0:32, T_BANK, 0:P].rearrange("p (i q) -> p q i", i=4),
                                         AX.X, ALU.max, negate=True))
                    step(v.tensor_copy(hl[:, 0, :], m_neg[0:32, :]))
                    v.tensor_tensor(hl[:, 1, :], m_neg[0:32, :], hl[:, 0, :], ALU.subtract).then_inc(s_row, 1)

                def reduce_relative(i, pr):
                    later, half = i < 4, i % 2
                    n = 4 * pr + (i - 3 if later else i - 5)
                    dve.wait_ge(s_chunk, 8 * pr + i - 3)
                    reach(dve, s_rr, n - 1)
                    v.tensor_tensor(r_tmp.rearrange("p (n q) -> p n q", q=4),
                                    psum[:, O_BANK, :].rearrange("p (n q) -> p n q", q=4),
                                    own_q.unsqueeze(1).to_broadcast([P, P, 4]), ALU.mult).then_inc(s_rrd, 1)
                    dve.wait_ge(s_rrd, n)
                    if i == 6:
                        reach(dve, s_rst, 16 * pr)
                    u = 8 * later + 4 * half
                    v.tensor_reduce(r_sb[:, :, :, u:u + 4].rearrange("p h b u -> p u b h"),
                                    r_tmp.rearrange("p (u b h q) -> p u b h q", u=4, b=2, h=H),
                                    AX.X, ALU.add).then_inc(s_rr, 1)

                def pair(pr, r, k):
                    first = isinstance(pr, int) and pr == 0
                    for s in range(NS):
                        i = CHUNK_AT.get(s - 1)
                        if i in (2, 3) and not first or i in (6, 7):
                            reduce_relative(i, pr)
                        if s >= 1 or not first:
                            rows_of_maxima(s - 1, pr)
                        partial_maxima(s, pr)

                per = 2 * (NS * 2 + 8 * 2)
                pair(0, 0, 0)
                start = s_dve.n
                with dve.Fori(0, NP // 2 - 1) as i:
                    s_dve.base = i * per
                    pair(2 * i + 1, 1, i)
                    pair(2 * i + 2, 0, i + 1)
                assert s_dve.n - start == per, (s_dve.n - start, per)
                s_dve.base, s_dve.n = 0, start + per * (NP // 2 - 1)
                pair(NP - 1, 1, NP // 2 - 1)
                rows_of_maxima(-1, NP)
                for i in (2, 3):
                    reduce_relative(i, NP)

                dve.wait_ge(s_fin, 16 * 24)
                step(v.reciprocal(o_sum, o_sum))
                nat = o_nat.rearrange("p (n j c) -> p j n c", j=4, c=4)
                for c in range(4):
                    last = v.tensor_copy(nat[:, :, :, c], o_rel.rearrange("p (j r) n -> p j r n", r=4)[:, :, 3 - c, :])
                step(last)
                own = lambda a, c: a.rearrange("p (n c a) -> p n c a", c=2, a=16)[:, :, c, :]
                tok = lambda c: o_nat.rearrange("p (n a c) -> p n a c", c=2, a=16)[:, :, :, c]
                for c in range(2):
                    last = v.tensor_tensor(tok(c), tok(c), own(o_all, c), ALU.add)
                step(last)
                for c in range(2):
                    last = v.tensor_tensor(tok(c), tok(c), own(o_sum, c), ALU.mult)
                last.then_inc(s_nat, 4)
                for k in range(NT // 4):
                    dve.wait_ge(s_wo, k + 1)
                    xk = x_sb[:, 4 * k:4 * k + 4, :]
                    v.tensor_tensor(xk, xk, psum[:, 2 + k % 2, :].rearrange("p (t d) -> p t d", t=4),
                                    ALU.add).then_inc(s_wor, 1)

            expert_layer(0)
            attention()
            expert_layer(1)


_INS = ['L0_attn_x', 'L0_attn_Wq', 'L0_attn_Wk', 'L0_attn_Wv', 'L0_attn_Wo', 'L0_attn_pek', 'L0_attn_pev',
        'L0_ffn_gate_w', 'L0_ffn_ln_w', 'L0_ffn_ln_b', 'L0_ffn_fc1s', 'L0_ffn_b1s', 'L0_ffn_fc2s', 'L0_ffn_b2s']
_OUTS = [((16, 256, 128), 'float32')]


def kernel(**inputs):
    import numpy as _np
    import concourse.bacc as _bacc
    from concourse import mybir as _mybir
    from concourse.bass_utils import run_bass_kernel_spmd as _run

    nc = _bacc.Bacc("TRN2", target_bir_lowering=False, num_devices=1)
    arrays, args = {}, []
    for name in _INS:
        a = _np.ascontiguousarray(inputs[name])
        arrays[f"in_{name}_dram"] = a
        args.append(nc.dram_tensor(f"in_{name}_dram", a.shape, _mybir.dt.from_np(a.dtype), kind="ExternalInput").ap())
    for i, (shape, dtype) in enumerate(_OUTS):
        dt = _mybir.dt.from_np(_np.dtype(dtype))
        args.append(nc.dram_tensor(f"out_{i}_dram", shape, dt, kind="ExternalOutput").ap())
    macaron_block(nc, *args)
    r = _run(nc, [arrays], core_ids=[0])
    got = tuple(r.results[0][f"out_{i}_dram"] for i in range(len(_OUTS)))
    return got[0]
```

```python
from contextlib import ExitStack

import concourse.bass as bass
from concourse import mybir

F32 = mybir.dt.float32
BF16 = mybir.dt.bfloat16
I32 = mybir.dt.int32
U32 = mybir.dt.uint32
ALU = mybir.AluOpType
ACT = mybir.ActivationFunctionType
AX = mybir.AxisListType
P = 128


class Tally:

    def __init__(self, sem):
        self.sem, self.n, self.base = sem, 0, 0

    def inc(self, instruction, by=1):
        instruction.then_inc(self.sem, by)
        self.n += by
        return self.n

    def now(self):
        return self.n + self.base if not isinstance(self.base, int) or self.base else self.n


def macaron_block(nc, x, wq, wk, wv, wo, pek, pev, gate_w, ln_w, ln_b, fc1s, b1s, fc2s, b2s, out):
    NB, L, D = x.shape
    E, FF, _ = fc1s.shape
    TOK = NB * L
    NT = TOK // P
    CAP = TOK // E
    NJ = CAP // P
    NC = FF // P
    ET = E * NT
    GW = D + E
    EPS = 1e-5
    SCORE_BITS, UNROLL = 30, 5
    LO, HI = 32, CAP // 32
    assert D == P and NJ == 4 and NT == 32 and E == 8 and NC == 4

    ctx = ExitStack()
    with ctx:
        def sem(name):
            return ctx.enter_context(nc.semaphore(name))

        ARENA = 52000
        arena = ctx.enter_context(nc.sbuf_tensor("arena", [P, ARENA], F32))
        psum = ctx.enter_context(nc.psum_tensor("banks", [P, 8, 512], F32))
        taken = [0]
        H, HD = 16, D // 16
        NP = NB // 2
        PT = 2 * L
        TERMS = 6
        Q_PART = (0, 0, 0, 1, 1, 2)
        K_PART = (0, 1, 2, 0, 1, 0)
        RUNS = ((0, 3), (3, 5), (5, 6))
        BIG = 1e30
        PW = 384
        assert L == 2 * P and H * HD == D and TERMS * 2 * HD <= 96

        def place(words, at=None):
            at = taken[0] if at is None else at
            taken[0] = max(taken[0], at + words)
            assert taken[0] <= ARENA, taken[0]
            return arena[:, at:at + words], at

        ident, _ = place(P)
        ones_bf = place(P // 2)[0].bitcast(BF16)
        same_bf = place(P // 2)[0].bitcast(BF16)
        before_bf = place(P // 2)[0].bitcast(BF16)
        tile_bf = place(ET // 2)[0].bitcast(BF16)
        iota_p = place(1)[0]
        carry, _ = place(ET)
        ones_row, _ = place(P)
        gwT, _ = place(E)
        b1T, _ = place(E * NC)
        b2row, _ = place(E * D)
        lnw, _ = place(1)
        lnb, _ = place(1)
        wT = place(4 * D)[0].rearrange("p (w d) -> p w d", w=4)
        rel_k = place(PW // 2)[0].bitcast(BF16)
        parity = place(2)[0]
        stats = place(NT * 6)[0].rearrange("p (t s) -> p t s", s=6)
        mv = place(NT * 2)[0].rearrange("p (t s) -> p t s", s=2)
        vare, s0, r0, rstd = (place(NT)[0] for _ in range(4))
        x_sb, _ = place(NT * D)
        x_sb = x_sb.rearrange("p (t d) -> p t d", d=D)
        PHASE = taken[0]

        w1T = place(E * FF)[0].rearrange("p (e f) -> p e f", e=E)
        w2T = place(E * FF)[0].rearrange("p (e c d) -> p e c d", e=E, c=NC)
        hT = place(2 * NC * CAP)[0].rearrange("p (b c s) -> p b c s", b=2, c=NC)
        xnT, _ = place(NT * D)
        raw1 = place(E * FF)[0].rearrange("p (e c d) -> p e c d", e=E, c=NC)
        raw2 = place(E * FF)[0].rearrange("p (e f) -> p e f", e=E)
        zt = place(NT * GW)[0].rearrange("p (t g) -> p t g", g=GW)
        rows, at_xn = place(E * NJ * GW)
        rows = rows.rearrange("p (s g) -> p s g", g=GW)
        xn = place(NT * D, at_xn)[0].rearrange("p (t d) -> p t d", d=D)
        half_xn = hT.rearrange("p b c s -> p (b c s)")
        yT, _ = place(2 * CAP)
        yT = yT.rearrange("p (b s) -> p b s", b=2)
        osb, _ = place(2 * CAP)
        osb = osb.rearrange("p (b j d) -> p b j d", b=2, j=NJ)
        hot_lo = place(ET * LO // 2)[0].bitcast(BF16).rearrange("p (a n) -> p a n", a=LO)
        hot_hi = half_xn.bitcast(BF16).rearrange("p (w b n) -> p w b n", w=2, b=HI)
        lmax, lsum = place(NT)[0], place(NT)[0]
        logit, _ = place(ET)
        score, _ = place(ET)
        score_t = place(2 * P)[0].rearrange("p (h n) -> p h n", h=2)
        cand, flip, seen = (place(2)[0].bitcast(I32) for _ in range(3))
        bits = place(UNROLL + 1)[0].bitcast(I32)
        lane_cnt = place(1)[0].bitcast(BF16)
        lane_tot = place(2)[0].bitcast(BF16)
        need, carry_at = place(2)[0], place(2)[0]
        mask_bf, gt_bf, eq_bf, sel_bf = (place(P)[0].bitcast(BF16).rearrange("p (h n) -> p h n", h=2)
                                         for _ in range(4))
        scan, place_t = (place(2 * P)[0].rearrange("p (h n) -> p h n", h=2) for _ in range(2))
        pos_i, lo_i, hi_i = (place(ET)[0].bitcast(I32) for _ in range(3))
        lo_bf, hi_bf = (place(ET // 2)[0].bitcast(BF16) for _ in range(2))
        neg_mean = place(NT)[0]
        idx_p, _ = place(E * HI)
        idx_i = place(E * HI)[0].bitcast(I32)
        idx = place(E * NJ)[0].bitcast(U32)
        eqhi = place(ET * HI // 2)[0].bitcast(BF16).rearrange("p (b n) -> p b n", b=HI)

        taken[0] = PHASE
        probs, at_probs = place(3 * 2 * H * P)
        probs = probs.rearrange("p (k n q) -> p k n q", k=3, n=2 * H)
        q_st, at_q = place(2 * H * PT // 2)
        q_st = q_st.bitcast(BF16).rearrange("p (r h c n) -> p r h c n", r=2, h=H, c=2)
        k_st, at_k = place(2 * H * PT // 2)
        k_st = k_st.bitcast(BF16).rearrange("p (r h n) -> p r h n", r=2, h=H)
        v_all = place(NT * H * 9)[0].rearrange("p (t h n) -> p t h n", t=NT, h=H)
        v_pair = place(2 * 4 * H * 9)[0].rearrange("p (r t h n) -> p r t h n", r=2, t=4, h=H)
        rel_v = place(2 * P * HD)[0]
        m_row = place(3 * 512)[0].bitcast(BF16).rearrange("p (r n) -> p r n", r=3)
        m_part = place(3 * 32)[0].rearrange("p (r n) -> p r n", r=3)
        m_neg = place(32)[0]
        m_hl = place(3 * 32)[0].bitcast(BF16).rearrange("p (r w n) -> p r w n", r=3, w=2)
        o_sb = place(2 * 512)[0].rearrange("p (r g n) -> p r g n", r=2, g=4)
        r_tmp = place(512)[0]
        r_sb = place(2 * H * 16)[0].rearrange("p (h b u) -> p h b u", h=H, b=2)
        own_q = place(4)[0]
        lane_i, lane_f = place(1)[0].bitcast(I32), place(1)[0]
        sums = place(4 * P)[0].rearrange("p (c n) -> p c n", c=4)
        assert taken[0] <= ARENA
        q_words = arena[:, at_q:at_q + H * PT].rearrange("p (h c n) -> p h c n", c=2, n=PT // 4)
        k_words = arena[:, at_k:at_k + H * PT].rearrange("p (h n) -> p h n", n=PT // 2)
        an = place(NT * D, at_probs)[0].rearrange("p (t d) -> p t d", d=D)
        anT = place(NT * D, at_probs + NT * D)[0]
        part = place(4 * 3 * 256, at_probs + 2 * NT * D)[0].bitcast(BF16).rearrange("p (r w n) -> p r w n", r=4, w=3)
        rest = place(2 * 512, at_probs + 2 * NT * D + 3072)[0].rearrange("p (r n) -> p r n", r=2)
        QT = TOK // 4
        quarter = [place(4 * QT, at_q + 4 * QT * b)[0].rearrange("p (w n) -> p w n", w=4) for b in (0, 2, 1, 3)]
        o_all, o_inv, o_rel, o_nat = ([a[:, w] for a in quarter] for w in range(4))

        def by_et(a):
            return a.rearrange("p (e t) -> p e t", e=E)

        table = [nc.dram_tensor(f"table{n}", [TOK, GW], F32).ap() for n in range(2)]
        x_mid = nc.dram_tensor("x_mid", [TOK, D], F32).ap()
        out_rows = out.rearrange("b l d -> (b l) d")
        total = [x_mid, out_rows]
        qs = nc.dram_tensor("query_parts", [3, HD, H, TOK], BF16).ap()
        ks = nc.dram_tensor("key_parts", [3, HD, H, TOK], BF16).ap()
        pv_ext = nc.dram_tensor("rel_v_extended", [PW, HD], F32).ap()
        o_dram = nc.dram_tensor("head_outputs", [H, 32, TOK], F32).ap()
        o_rows = o_dram.rearrange("(g j) d n -> (j d) g n", j=4)
        inv_dram = nc.dram_tensor("inverse_sums", [H, TOK], F32).ap()
        r_dram = nc.dram_tensor("relative_outputs", [P, H, 2 * P], F32).ap()

        s_par = sem("parameters_loaded")
        s_raw = sem("raw_weights_loaded")
        s_x = [sem(f"x_loaded{c}") for c in range(4)]
        s_const = sem("constants_ready")
        s_dve = Tally(sem("vector_steps"))
        s_pool = Tally(sem("pool_steps"))
        s_act = Tally(sem("scalar_steps"))
        s_sqrt_in, s_sqrt = sem("variance_ready"), sem("root_ready")
        s_tr = sem("transposed_bank")
        s_trf = sem("transposed_bank_read")
        s_xn = sem("xn_ready")
        s_z = sem("table_rows_ready")
        s_half, s_init = sem("half_xn_ready"), sem("residual_ready")
        s_zin = sem("row_statistics_ready")
        s_scored, s_scT = sem("scores_ready_by_expert"), sem("scores_transposed")
        s_q, s_qT = sem("places_ready"), sem("places_transposed")
        s_eqhi, s_hot_t = sem("high_places_ready"), sem("tile_numbers_placed")
        s_logit = sem("logits_ready")
        s_centred = sem("logits_centred")
        s_exp = sem("exp_ready")
        s_mask, s_cnt = sem("mask_counted"), sem("counts_ready")
        s_pre, s_prer = sem("prefix_asked"), sem("prefix_ready")
        s_hot, s_idx = sem("one_hots_ready"), sem("index_sums_ready")
        s_idxi, s_idxd = sem("indices_ready"), sem("indices_spread")
        s_tab, s_acc = sem("table_stored"), sem("residual_stored")
        s_rows = [sem(f"rows_gathered{e}") for e in range(E)]
        s_yT = sem("yT_ready")
        s_h, s_g = sem("fc1_ready"), sem("gelu_ready")
        s_o, s_os = sem("fc2_ready"), sem("out_scaled")
        s_sc = sem("scattered")
        s_back = sem("x_reloaded")
        s_ffn = sem("experts_done")
        s_pe1 = sem("rel_v_extended_stored")
        s_rk = sem("rel_k_rows_loaded")
        s_rv = sem("rel_v_loaded")
        s_ext = sem("rel_k_parts_ready")
        s_an, s_anT = sem("attention_input_ready"), sem("attention_input_transposed")
        s_pj, s_p1, s_p1r = sem("projection_ready"), sem("first_part_ready"), sem("rest_ready")
        s_p2, s_part, s_pst = sem("second_part_ready"), sem("parts_ready"), [sem(f"parts_stored{i}") for i in range(4)]
        s_vp, s_vr = sem("values_projected"), sem("values_read")
        s_zero = sem("attention_buffers_cleared")
        s_load = [sem(f"pair_loaded{i}") for i in range(2)]
        s_vpair = sem("pair_values_ready")
        s_score, s_T, s_tT = sem("scores_ready"), sem("partial_maxima_ready"), sem("maxima_transposed")
        s_row = sem("negated_maxima_ready")
        s_m = [sem(f"maxima_row_loaded{i}") for i in range(3)]
        s_sub, s_prob = sem("maxima_subtracted"), sem("probabilities_ready")
        s_chunk, s_chr = sem("outputs_ready"), sem("head_outputs_read")
        s_rr, s_rrd = sem("relative_outputs_reduced"), sem("relative_bank_read")
        s_ost = [sem(f"head_outputs_stored{i}") for i in range(2)]
        s_rst = sem("relative_outputs_stored")
        s_sum, s_inv, s_invst = sem("sums_loaded"), sem("sums_inverted"), sem("inverse_sums_stored")
        s_all = [sem(f"head_outputs_loaded{c}") for c in range(4)]
        s_rel = [sem(f"relative_outputs_loaded{c}") for c in range(4)]
        s_turned = sem("relative_outputs_in_token_order")
        s_nat = sem("outputs_normalised")
        s_wo, s_wor = sem("output_projected"), sem("output_added")

        block = ctx.enter_context(nc.Block())

        TR = (0, 1)
        B_GATE, B_CNT, B_IDX = 2, 3, 3
        H_B, O_B = (4, 5), (6, 7)

        NWB = 2 * E
        NXB = NT // 4
        NAB = NWB + NXB
        NYB = E
        TRN = NWB + NXB + NYB

        ext = osb.rearrange("p b j d -> p (b j d)")[0:HD, 0:PW]
        ext_rest = osb.rearrange("p b j d -> p (b j d)")[0:HD, PW:2 * PW]
        ext_part = yT.rearrange("p b s -> p (b s)").bitcast(BF16)[0:HD, 0:3 * PW].rearrange("p (w n) -> p w n", w=3)

        def in_pairs(engine, pair):
            pair(0, 0, 0)
            with engine.Fori(0, NP // 2 - 1) as i:
                pair(2 * i + 1, 1, i)
                pair(2 * i + 2, 0, i + 1)
            pair(NP - 1, 1, NP // 2 - 1)

        def reach(engine, semaphore, value):
            if not isinstance(value, int) or value > 0:
                engine.wait_ge(semaphore, value)

        SLOTS = [(0, 0, False), (0, 2, False), (1, 0, False), (1, 2, False)] + \
                [(b, q, True) for b in range(2) for q in range(4, 8)]
        NS = len(SLOTS)
        CHUNK_AT = {2: 0, 3: 1, 4: 2, 5: 3, 7: 4, 8: 5, 9: 6, 10: 7}
        T_BANK, O_BANK = 6, 7

        def load_sums(engine, c):
            src = o_dram[:, HD, c * QT:c * QT + QT].rearrange("h (m n) -> h m n", n=P)
            engine.dma_start(sums[:, c], src).then_inc(s_sum, 16)

        def store_inverses(engine, c):
            dst = inv_dram[:, c * QT:c * QT + QT].rearrange("h (m n) -> h m n", n=P)
            engine.dma_start(dst, sums[:, c]).then_inc(s_invst, 16)

        def load_outputs(engine, c):
            src = o_dram[:, 0:HD, c * QT:c * QT + QT]
            engine.dma_start(o_all[c], src).then_inc(s_all[c], 16)

        def load_relative(engine, c):
            u = QT // 16
            src = r_dram[:, :, c * u:c * u + u].rearrange("(c d) h n -> d h c n", d=HD)
            for d in range(HD):
                engine.dma_start(o_rel[c][d:P:HD, :].rearrange("h (c u) -> h c u", c=16), src[d]).then_inc(s_rel[c], 16)

        def load_inverses(engine, c):
            src = bass.AP(inv_dram.tensor, c * QT, [[TOK, H], [0, HD], [1, QT]])
            engine.dma_start(o_inv[c], src).then_inc(s_all[c], 16)

        def tr_bank(k):
            return psum[:, TR[k % 2], :]

        @block.sync
        def _(sp):
            xr = x.rearrange("b l d -> (b l) d").rearrange("(t p) d -> p t d", p=P)
            for c in range(4):
                sp.dma_start(x_sb[:, 8 * c:8 * c + 8, :], xr[:, 8 * c:8 * c + 8, :]).then_inc(s_x[c], 16)
            sp.dma_start(logit[0:E, 0:D], gate_w).then_inc(s_par, 16)
            sp.dma_start(logit[0:E * NC, D:2 * D], b1s.rearrange("e (c p) -> (e c) p", p=P)).then_inc(s_par, 16)
            sp.dma_start(b2row[0:1, :], b2s.rearrange("e d -> (e d)").unsqueeze(0)).then_inc(s_par, 16)
            sp.dma_start(lnw, ln_w.unsqueeze(1)).then_inc(s_par, 16)
            sp.dma_start(lnb, ln_b.unsqueeze(1)).then_inc(s_par, 16)
            for i, w in enumerate((wq, wk, wv, wo)):
                sp.dma_start(hT[:, 0, i, 0:D], w).then_inc(s_par, 16)
            sp.dma_start(hT[:, 1, 0, 0:2 * HD].rearrange("p (t d) -> p t d", t=2),
                         pek[0:2 * P, :].rearrange("(t p) d -> p t d", p=P)).then_inc(s_par, 16)
            sp.dma_start(pv_ext[0:P - 1, :], pev[0:1, :].to_broadcast([P - 1, HD])).then_inc(s_pe1, 16)
            sp.dma_start(pv_ext[P - 1:3 * P - 1, :], pev[0:2 * P, :]).then_inc(s_pe1, 16)

            def expert_layer(n):
                if n:
                    sp.wait_ge(s_wor, NT // 4)
                for h in range(2):
                    es = slice(4 * h, 4 * h + 4)
                    sp.dma_start(raw1[:, es], fc1s[es].rearrange("e (c p) d -> p e c d", p=P)).then_inc(s_raw, 16)
                    sp.dma_start(raw2[:, es], fc2s[es].rearrange("e d f -> d e f")).then_inc(s_raw, 16)
                sp.wait_ge(s_init, n + 1)
                sp.dma_start(total[n].rearrange("(t p) d -> p t d", p=P), x_sb).then_inc(s_acc, 16)
                sp.wait_ge(s_z, 2 * n + 2)
                sp.dma_start(table[n].rearrange("(t p) g -> p t g", p=P), zt).then_inc(s_tab, 16)
                sp.wait_ge(s_idxi, n + 1)
                for r in range(4):
                    sp.dma_start(idx[32 * r:32 * r + 32, :],
                                 idx_i[0:32, 32 * r:32 * r + 32].bitcast(U32)).then_inc(s_idxd, 16)

            sp.wait_ge(s_ext, 1)
            sp.wait_ge(s_const, 9)
            for t in range(TERMS):
                for c in range(2):
                    r = (TERMS * c + t) * HD
                    sp.dma_start(rel_k[r:r + HD, 0:PW - 2], ext_part[:, K_PART[t], 1 - c:PW - 1 - c]).then_inc(s_rk, 16)

            def attention():
                sp.wait_ge(s_ffn, 1)
                xm = x_mid.rearrange("(t p) d -> p t d", p=P)
                for c in range(4):
                    sp.dma_start(x_sb[:, 8 * c:8 * c + 8, :], xm[:, 8 * c:8 * c + 8, :]).then_inc(s_x[c], 16)
                sp.wait_ge(s_pe1, 32)
                sp.dma_start(rel_v, bass.AP(pv_ext.tensor, 0, [[HD, P], [1, 2 * P * HD]])).then_inc(s_rv, 16)
                for i in range(2 * NP):
                    sp.wait_ge(s_part, i + 1)
                    dst = (qs if i % 2 == 0 else ks)[:, :, :, PT * (i // 2):PT * (i // 2) + PT]
                    sp.dma_start(dst.rearrange("w d h n -> (d h) w n"), part[:, i % 4]).then_inc(s_pst[i % 4], 16)

                def pair(pr, r, k):
                    for s in range(NS):
                        sp.wait_ge(s_row, NS * pr + s + 1)
                        for w in range(2):
                            sp.dma_start(m_row[w:w + 1, s % 3, :].rearrange("o (a b) -> o a b", a=32),
                                         m_hl[0:32, s % 3, w, :]).then_inc(s_m[s % 3], 16)

                in_pairs(sp, pair)
                sp.wait_ge(s_score, NS * NP)
                sp.wait_ge(s_rst, 16 * (NP - 2))
                load_relative(sp, 2)
                sp.wait_ge(s_rst, 16 * NP)
                load_relative(sp, 3)
            expert_layer(0)
            attention()
            expert_layer(1)

        @block.gpsimd
        def _(pool):
            def step(i):
                s_pool.inc(i)
                pool.wait_ge(s_pool.sem, s_pool.now())

            step(pool.memset(ident, 0.0))
            pool.affine_select(out=ident, in_=ident, compare_op=ALU.not_equal, fill=1.0, base=0,
                               pattern=[[-1, P]], channel_multiplier=1).then_inc(s_const, 1)
            step(pool.memset(same_bf, 0.0))
            for b in range(4):
                last = pool.memset(same_bf[32 * b:32 * b + 32, 32 * b:32 * b + 32], 1.0)
            last.then_inc(s_const, 1)
            pool.wait_ge(s_const, 2)
            pool.affine_select(out=before_bf, in_=same_bf, compare_op=ALU.is_gt, fill=0.0, base=0,
                               pattern=[[1, P]], channel_multiplier=-1).then_inc(s_const, 1)
            pool.memset(ones_bf, 1.0).then_inc(s_const, 1)
            pool.memset(ones_row, 1.0).then_inc(s_const, 1)
            step(pool.memset(carry, 1.0))
            step(pool.memset(carry[:, P:P + 1], 0.0))
            step(pool.iota(pos_i, pattern=[[0, E], [1, NT]], base=0, channel_multiplier=0))
            pool.tensor_copy(tile_bf, pos_i).then_inc(s_const, 1)
            step(pool.iota(lo_i[:, 0:1], pattern=[[0, 1]], base=0, channel_multiplier=1))
            pool.tensor_copy(iota_p, lo_i[:, 0:1]).then_inc(s_const, 1)

            step(pool.memset(parity, 0.0))
            pool.affine_select(out=parity[96:P, :].bitcast(BF16).rearrange("p (c w) -> p c w", c=2),
                               in_=parity[96:P, :].bitcast(BF16).rearrange("p (c w) -> p c w", c=2),
                               compare_op=ALU.not_equal, fill=1.0, base=0, pattern=[[-1, 2], [0, 2]],
                               channel_multiplier=1).then_inc(s_const, 1)
            pool.wait_ge(s_const, 8)

            step(pool.memset(rel_k, 0.0))
            pool.affine_select(out=rel_k[96:P, :], in_=rel_k[96:P, :], compare_op=ALU.is_ge, fill=-BIG,
                               base=2 * P - 2, pattern=[[-1, PW]], channel_multiplier=1).then_inc(s_const, 1)

            def expert_layer(n):
                pool.wait_ge(s_scored, n + 1)
                pool.tensor_copy(zt[:, :, D:GW], by_et(score).rearrange("p e t -> p t e")).then_inc(s_z, 1)
                pool.wait_ge(s_half, n + 1)
                pool.tensor_tensor(x_sb.rearrange("p t d -> p (t d)"), x_sb.rearrange("p t d -> p (t d)"),
                                   half_xn, ALU.add).then_inc(s_init, 1)
                pool.wait_ge(s_eqhi, n + 1)
                pool.wait_ge(s_init, n + 1)
                pool.tensor_tensor(hot_hi[:, 0], eqhi, tile_bf.unsqueeze(1).to_broadcast([P, HI, ET]),
                                   ALU.mult).then_inc(s_hot_t, 1)
                pool.wait_ge(s_idxd, 64 * (n + 1))
                pool.wait_ge(s_tab, 16 * (n + 1))
                for e in range(E):
                    for j in range(NJ):
                        s = e * NJ + j
                        pool.indirect_dma_start(
                            out=rows[:, s, :], out_offset=None, in_=table[n],
                            in_offset=bass.IndirectOffsetOnAxis(ap=idx[:, s:s + 1], axis=0)).then_inc(s_rows[e], 16)
                pool.wait_ge(s_acc, 16 * (n + 1))
                for e in range(E):
                    pool.wait_ge(s_os, n * E + e + 1)
                    if e:
                        pool.wait_ge(s_sc, 64 * (n * E + e))
                    for j in range(NJ):
                        s = e * NJ + j
                        pool.indirect_dma_start(
                            out=total[n], out_offset=bass.IndirectOffsetOnAxis(ap=idx[:, s:s + 1], axis=0),
                            in_=osb[:, e % 2, j, :], in_offset=None, compute_op=ALU.add).then_inc(s_sc, 16)
                pool.wait_ge(s_sc, 64 * (n + 1) * E)
                pool.nop().then_inc(s_ffn, 1)

            def settled(semaphore, value):
                reach(pool, semaphore, value)
                pool.wait_ge(s_const, 9)

            def stacked(pr, r):
                for a, b in RUNS:
                    for c in range(2):
                        lanes = slice((TERMS * c + a) * HD, (TERMS * c + b) * HD)
                        q = qs[Q_PART[a], 0:HD, :, bass.ds(pr * PT + c * L, L)]
                        q = q.unsqueeze(0).to_broadcast([b - a, HD, H, L])
                        k = ks[0:b - a, :, :, bass.ds(pr * PT, PT)].rearrange("w d h n -> (w d) h n")
                        yield q_st[lanes, r, :, c, :], q
                        yield k_st[lanes, r, :, :], k

            def attention():
                pool.memset(v_all[:, :, :, HD:HD + 1], 1.0)
                step(pool.memset(m_row, 0.0))
                for i in range(2):
                    pool.wait_ge(s_pst[i], 16)
                for dst, src in stacked(0, 0):
                    pool.dma_start(dst, src).then_inc(s_load[0], 16)

                def pair(pr, r, k):
                    first, last = isinstance(pr, int) and pr == 0, isinstance(pr, int) and pr == NP - 1
                    if first:
                        pool.wait_ge(s_vr, NT // 4)
                    if not first:
                        settled(s_chunk, 8 * pr - 7)
                    pool.tensor_copy(v_pair[:, r], v_all[:, bass.ds(pr * 4, 4)]).then_inc(s_vpair, 1)
                    if first:
                        for i in range(4):
                            pool.wait_ge(s_pst[i], 16 * (NP // 2))
                    loads = [] if last else list(stacked(pr + 1, 1 - r))
                    if loads:
                        settled(s_score, NS * pr)

                    def load_some(n):
                        for dst, src in loads[:n]:
                            pool.dma_start(dst, src).then_inc(s_load[1 - r], 16)
                        del loads[:n]

                    def store_heads(i, b, q):
                        settled(s_chr, 4 * pr + i - 1)
                        pool.dma_start(o_rows[:, :, bass.ds(b * L + q * P, P)], o_sb[:, i % 2]
                                       ).then_inc(s_ost[i % 2], 16)

                    def store_relative(before):
                        settled(s_rr, 4 * before + 4)
                        pool.dma_start(r_dram[:, :, bass.ds(before * 32, 32)],
                                       r_sb.rearrange("p h b u -> p h (b u)")).then_inc(s_rst, 16)

                    if last:
                        for i in range(2):
                            pool.wait_ge(s_ost[i], 16 * 2 * (NP - 2))
                        pool.wait_ge(s_rst, 16 * (NP - 2))
                        for c in range(3):
                            load_sums(pool, c)
                        pool.wait_ge(s_score, NS * (NP - 1))
                        for c in range(2):
                            load_outputs(pool, c)
                            load_relative(pool, c)
                    load_some(3)
                    if not first:
                        store_heads(0, 2 * pr - 2, 1)
                        load_some(2)
                        store_heads(1, 2 * pr - 1, 1)
                        load_some(2)
                        store_relative(pr - 1)
                    load_some(2)
                    store_heads(2, 2 * pr, 0)
                    load_some(2)
                    store_heads(3, 2 * pr + 1, 0)
                    load_some(len(loads))
                    if last:
                        pool.wait_ge(s_inv, 1)
                        for c in range(3):
                            store_inverses(pool, c)
                        pool.wait_ge(s_invst, 48)
                        for c in range(2):
                            load_inverses(pool, c)
                        pool.wait_ge(s_score, NS * NP)
                        load_outputs(pool, 2)
                        load_inverses(pool, 2)
                        for b in range(2):
                            pool.wait_ge(s_chr, 4 * NP + b - 1)
                            pool.dma_start(o_rows[:, :, (2 * pr + b) * L + P:(2 * pr + b) * L + 2 * P],
                                           o_sb[:, b]).then_inc(s_ost[b], 16)
                        for b in range(2):
                            pool.wait_ge(s_ost[b], 16 * 2 * NP)
                        load_sums(pool, 3)
                        store_relative(pr)
                        load_outputs(pool, 3)
                        pool.wait_ge(s_inv, 2)
                        store_inverses(pool, 3)
                        pool.wait_ge(s_invst, 64)
                        load_inverses(pool, 3)

                in_pairs(pool, pair)

            expert_layer(0)
            attention()
            expert_layer(1)

        @block.scalar
        def _(act):
            act.wait_ge(s_tr, 1)
            nc.scalar.copy(b1T, tr_bank(0)[:, 0:E * NC])
            nc.scalar.copy(gwT, tr_bank(0)[:, E * NC:E * NC + E])
            nc.scalar.copy(ext[:, P - 1:3 * P - 1], tr_bank(0)[0:HD, P:3 * P])
            nc.scalar.copy(ext[:, 0:P - 1], tr_bank(0)[0:HD, P:P + 1].to_broadcast([HD, P - 1]))
            nc.scalar.copy(ext[:, 3 * P - 1:3 * P], tr_bank(0)[0:HD, P:P + 1]).then_inc(s_trf, 1)
            act.wait_ge(s_tr, 2)
            nc.scalar.copy(wT[:, 0:2].rearrange("p w (d h) -> p w d h", h=H),
                           tr_bank(1)[:, 0:2 * D].rearrange("p (w h d) -> p w d h", w=2, h=H))
            nc.scalar.copy(wT[:, 2:4], tr_bank(1)[:, 2 * D:4 * D].rearrange("p (w d) -> p w d", w=2)
                           ).then_inc(s_trf, 1)

            def expert_layer(n):
                tr = 2 + n * TRN + (NXB if n else 0)
                act.wait_ge(s_sqrt_in, 6 * n + 1)
                nc.scalar.activation(s0, vare, ACT.Sqrt).then_inc(s_sqrt, 1)
                for k in range(NXB):
                    act.wait_ge(s_tr, tr + k + 1)
                    nc.scalar.copy(xnT[:, 512 * k:512 * k + 512], tr_bank(tr + k)).then_inc(s_trf, 1)
                act.wait_ge(s_centred, n + 1)
                nc.scalar.activation(logit, logit, ACT.Exp).then_inc(s_exp, 1)
                act.wait_ge(s_sqrt_in, 6 * n + 2)
                nc.scalar.activation(s0, vare, ACT.Sqrt).then_inc(s_sqrt, 1)
                nc.scalar.activation(half_xn, xn.rearrange("p t d -> p (t d)"), ACT.Copy, scale=0.5).then_inc(s_half, 1)
                act.wait_ge(s_zin, n + 1)
                for t in range(NT):
                    last = nc.scalar.activation(zt[:, t, 0:D], xn[:, t, :], ACT.Identity,
                                                bias=neg_mean[:, t:t + 1], scale=rstd[:, t:t + 1])
                last.then_inc(s_z, 1)
                for k in range(NWB):
                    act.wait_ge(s_tr, tr + NXB + k + 1)
                    if k % 2 == 0:
                        nc.scalar.copy(w1T[:, k // 2, :], tr_bank(tr + NXB + k)).then_inc(s_trf, 1)
                    else:
                        nc.scalar.copy(w2T[:, k // 2, :, :],
                                       tr_bank(tr + NXB + k).rearrange("p (c d) -> p c d", c=NC)).then_inc(s_trf, 1)
                for e in range(E):
                    for c in range(NC):
                        k = (n * E + e) * NC + c
                        act.wait_ge(s_h, k + 1)
                        if e >= 2 or n:
                            act.wait_ge(s_o, n * E + e - 1)
                        nc.scalar.activation(hT[:, e % 2, c, :], psum[:, H_B[k % 2], :], ACT.Gelu_apprx_tanh,
                                             bias=b1T[:, e * NC + c:e * NC + c + 1]).then_inc(s_g, 1)

            def attention():
                def root(c):
                    act.wait_ge(s_sqrt_in, 3 + c)
                    nc.scalar.activation(s0[:, 8 * c:8 * c + 8], vare[:, 8 * c:8 * c + 8], ACT.Sqrt).then_inc(s_sqrt, 1)

                def first_part(i):
                    act.wait_ge(s_pj, i + 1)
                    if i >= 4:
                        act.wait_ge(s_pst[i % 4], 16 * (i // 4))
                    nc.scalar.copy(part[:, i % 4, 0, :], psum[:, 2 + i % 2, :]).then_inc(s_p1, 1)

                def second_part(i):
                    act.wait_ge(s_p1r, i + 1)
                    nc.scalar.copy(part[:, i % 4, 1, :], rest[:, i % 2, :]).then_inc(s_p2, 1)

                root(0)
                for c in range(4):
                    for k in (2 * c, 2 * c + 1):
                        act.wait_ge(s_tr, 2 + TRN + k + 1)
                        nc.scalar.copy(anT[:, 512 * k:512 * k + 512], tr_bank(2 + TRN + k)).then_inc(s_trf, 1)
                    if c < 3:
                        root(c + 1)
                    first_part(4 * c)
                    for i in range(4 * c, 4 * c + 4):
                        if i % 4 < 3:
                            first_part(i + 1)
                        second_part(i)
                for k in range(NT // 4):
                    act.wait_ge(s_vp, k + 1)
                    nc.scalar.copy(v_all[:, 4 * k:4 * k + 4, :, 0:HD],
                                   psum[:, 4 + k % 2, :].rearrange("p (t h d) -> p t h d", t=4, h=H)).then_inc(s_vr, 1)

                def exp(s, pr):
                    b, q, later = SLOTS[s]
                    s, g = s % NS, NS * pr + s
                    act.wait_ge(s_sub, g + 1)
                    if s == 0:
                        reach(act, s_chunk, 8 * pr - 4)
                    if s == 4:
                        reach(act, s_chunk, 8 * pr)
                    heads = slice(H * b, H * b + H)
                    if later:
                        dst = probs[:, 1:3, heads, 32 * (q - 4):32 * (q - 4) + 32]
                    else:
                        dst = probs[:, 0, heads, 32 * q:32 * q + 64].rearrange("p h (u n) -> p u h n", u=2)
                    r = s % 3
                    nc.scalar.activation(dst, psum[:, 2 * r:2 * r + 2, :].rearrange("p u (h n) -> p u h n", h=H),
                                         ACT.Exp, scale=HD ** -0.5).then_inc(s_prob, 1)

                def read_heads(pr, i):
                    act.wait_ge(s_chunk, 8 * pr + (i if i < 2 else i + 2) - 3)
                    reach(act, s_ost[i % 2], 16 * (2 * pr + (-1 if i < 2 else 0)))
                    nc.scalar.copy(o_sb[:, i % 2], psum[:, O_BANK, :].rearrange("p (g n) -> p g n", g=4)
                                   ).then_inc(s_chr, 1)

                def pair(pr, r, k):
                    first = isinstance(pr, int) and pr == 0
                    for s in range(NS):
                        if s - 1 in (2, 3) and not first:
                            read_heads(pr, s - 3)
                        if s - 1 in (7, 8):
                            read_heads(pr, s - 6)
                        if s >= 2 or not first:
                            exp(s - 2, pr)

                in_pairs(act, pair)
                for s in (-2, -1):
                    exp(s, NP)
                for i in range(2):
                    read_heads(NP, i)
                for c in range(4):
                    act.wait_ge(s_rel[c], 16 * HD)
                    nat = o_nat[c].rearrange("p (n j c) -> p j n c", j=4, c=4)
                    for u in range(4):
                        last = nc.scalar.copy(nat[:, :, :, u],
                                              o_rel[c].rearrange("p (j r n) -> p j r n", j=4, r=4)[:, :, 3 - u, :])
                    last.then_inc(s_turned, 1)

            expert_layer(0)
            attention()
            expert_layer(1)

        @block.tensor
        def _(pe):
            pe.wait_ge(s_const, 9)
            pe.wait_ge(s_par, 160)
            pe.transpose(tr_bank(0)[:, 0:E * NC], logit[0:E * NC, D:2 * D], ident[0:E * NC, 0:E * NC])
            pe.transpose(tr_bank(0)[:, E * NC:E * NC + E], logit[0:E, 0:D], ident[0:E, 0:E])
            for t in range(2):
                last = pe.transpose(tr_bank(0)[0:HD, P + P * t:2 * P + P * t], hT[:, 1, 0, HD * t:HD * t + HD], ident)
            last.then_inc(s_tr, 1)
            for i in range(4):
                last = pe.transpose(tr_bank(1)[:, D * i:D * i + D], hT[:, 0, i, 0:D], ident)
            last.then_inc(s_tr, 1)

            def expert_layer(n):
                tr = 2 + n * TRN + (NXB if n else 0)

                def bank_of(k):
                    read = 2 + n * (NAB + NXB) + k - 1
                    if k < NAB + 2:
                        pe.wait_ge(s_trf, read)
                    return tr_bank(tr + k)

                for k in range(NXB):
                    pe.wait_ge(s_xn, n * NXB + k + 1)
                    bank = bank_of(k)
                    for c in range(4):
                        last = pe.transpose(bank[:, P * c:P * c + P], xn[:, 4 * k + c, :], ident)
                    last.then_inc(s_tr, 1)
                for t in range(NT):
                    if t % 4 == 0:
                        pe.wait_ge(s_trf, 2 + n * (NAB + NXB) + t // 4 + 1)
                    last = pe.matmul(psum[:, B_GATE, E * t:E * t + E], xnT[:, P * t:P * t + P], gwT,
                                     start=True, stop=True)
                last.then_inc(s_logit, 1)
                pe.wait_ge(s_scored, n + 1)
                for h in range(2):
                    last = pe.transpose(psum[:, B_GATE, P * h:P * h + P], score[:, P * h:P * h + P], ident)
                last.then_inc(s_scT, 1)
                with pe.Fori(0, SCORE_BITS // UNROLL) as i:
                    for u in range(UNROLL):
                        pe.wait_ge(s_mask, i * UNROLL + (n * SCORE_BITS + u + 1))
                        pe.matmul(psum[:, B_CNT, 0:2], same_bf, lane_cnt, start=True, stop=True).then_inc(s_cnt, 1)
                pe.wait_ge(s_pre, 2 * n + 1)
                pe.matmul(psum[:, B_CNT, 0:2], same_bf, lane_tot[:, 0:2], start=True, stop=True)
                pe.matmul(psum[:, B_CNT, 2:4], before_bf, lane_tot[:, 2:4], start=True, stop=True).then_inc(s_prer, 1)
                pe.wait_ge(s_pre, 2 * n + 2)
                pe.matmul(psum[:, B_CNT, 4:6], before_bf, lane_tot[:, 0:2], start=True, stop=True).then_inc(s_prer, 1)
                pe.wait_ge(s_q, n + 1)
                for h in range(2):
                    last = pe.transpose(psum[:, B_GATE, P * h:P * h + P], place_t[:, h, :], ident)
                last.then_inc(s_qT, 1)
                pe.wait_ge(s_raw, 64 * (n + 1))
                for k in range(NWB):
                    bank, e = bank_of(NXB + k), k // 2
                    for c in range(NC):
                        src = raw2[:, e, P * c:P * c + P] if k % 2 else raw1[:, e, c, :]
                        last = pe.transpose(bank[:, P * c:P * c + P], src, ident)
                    last.then_inc(s_tr, 1)
                pe.wait_ge(s_hot, n + 1)
                pe.wait_ge(s_hot_t, n + 1)
                for e in range(E):
                    for t in range(NT):
                        last = pe.matmul(psum[0:LO, B_IDX, 2 * HI * e:2 * HI * e + 2 * HI],
                                         hot_lo[:, :, e * NT + t], hot_hi[:, :, :, e * NT + t],
                                         start=(t == 0), stop=(t == NT - 1))
                last.then_inc(s_idx, 1)

                def first_half(e):
                    pe.wait_ge(s_rows[e], 64 * (n + 1))
                    bank = bank_of(NWB + NXB + e)
                    for j in range(NJ):
                        last = pe.transpose(bank[:, P * j:P * j + P], rows[:, e * NJ + j, 0:D], ident)
                    last.then_inc(s_tr, 1)
                    pe.wait_ge(s_yT, n * E + e + 1)
                    for c in range(NC):
                        k = (n * E + e) * NC + c
                        if k >= 2:
                            pe.wait_ge(s_g, k - 1)
                        pe.matmul(psum[:, H_B[k % 2], :], w1T[:, e, P * c:P * c + P], yT[:, e % 2, :],
                                  start=True, stop=True).then_inc(s_h, 1)

                def second_half(e):
                    pe.wait_ge(s_g, (n * E + e + 1) * NC)
                    if n * E + e >= 2:
                        pe.wait_ge(s_os, n * E + e - 1)
                    for j in range(NJ):
                        o = psum[:, O_B[e % 2], P * j:P * j + P]
                        for c in range(NC):
                            pe.matmul(o, hT[:, e % 2, c, P * j:P * j + P], w2T[:, e, c, :],
                                      start=(c == 0), stop=False)
                        last = pe.matmul(o, ones_row[0:1, :], b2row[0:1, D * e:D * e + D], start=False, stop=True)
                    last.then_inc(s_o, 1)

                first_half(0)
                for e in range(1, E):
                    first_half(e)
                    second_half(e - 1)
                second_half(E - 1)

            def attention():
                for c in range(4):
                    for k in (2 * c, 2 * c + 1):
                        pe.wait_ge(s_an, k + 1)
                        if k >= 2:
                            pe.wait_ge(s_trf, 2 + NAB + k - 1)
                        for t in range(4):
                            last = pe.transpose(tr_bank(2 + TRN + k)[:, P * t:P * t + P], an[:, 4 * k + t, :], ident)
                        last.then_inc(s_tr, 1)
                    for i in range(4 * c, 4 * c + 4):
                        pe.wait_ge(s_trf, 2 + NAB + i // 2 + 1)
                        if i >= 2:
                            pe.wait_ge(s_p1r, i - 1)
                        cols = anT[:, PT * (i // 2):PT * (i // 2) + PT]
                        if i % 2 == 0:
                            cols = cols.rearrange("p (b a c) -> p c b a", b=2, c=2)
                        pe.matmul(psum[:, 2 + i % 2, :], wT[:, i % 2, :], cols, start=True, stop=True).then_inc(s_pj, 1)
                for k in range(NT // 4):
                    if k >= 2:
                        pe.wait_ge(s_vr, k - 1)
                    for t in range(4):
                        last = pe.matmul(psum[:, 4 + k % 2, P * t:P * t + P],
                                         anT[:, P * (4 * k + t):P * (4 * k + t) + P], wT[:, 2, :], start=True, stop=True)
                    last.then_inc(s_vp, 1)
                pe.wait_ge(s_p1r, 2 * NP)
                pe.wait_ge(s_vr, NT // 4)
                pe.wait_ge(s_rk, 16 * 2 * TERMS)
                pe.wait_ge(s_rv, 16)
                pe.wait_ge(s_zero, 1)

                def scores(s, pr, r):
                    b, q, later = SLOTS[s]
                    reach(pe, s_prob, NS * pr + s - 2)
                    for u in range(2):
                        qu, kb = (q, u) if later else (q + u, 0)
                        sc = psum[:, 2 * (s % 3) + u, :].rearrange("p (h c a) -> p h c a", h=H, c=2)
                        for a in range(16):
                            y = 2 * P - 2 - 2 * (16 * qu + a) + P * kb
                            pe.matmul(sc[:, :, :, a], rel_k[:, y:y + P], q_st[:, r, :, :, P * b + 16 * qu + a],
                                      start=(a == 0), stop=False, skip_group_check=True)
                        for h in range(H):
                            last = pe.matmul(sc[:, h], k_st[:, r, h, L * b + P * kb:L * b + P * kb + P],
                                             q_st[:, r, h, :, P * b + 16 * qu:P * b + 16 * qu + 16],
                                             start=False, stop=False, skip_group_check=True)
                    last.then_inc(s_score, 1)

                def turn_maxima(s, pr):
                    g = NS * pr + s
                    pe.wait_ge(s_T, g + 1)
                    if not (isinstance(g, int) and g == 0):
                        reach(pe, s_row, g)
                    pe.transpose(psum[0:32, T_BANK, 0:P], m_part[:, s % 3, :], ident).then_inc(s_tT, 1)

                def subtract_maxima(s, pr):
                    pe.wait_ge(s_m[s % 3], 32 * (NS // 3 * pr + (s // 3) + 1))
                    for u in range(2):
                        last = pe.matmul(psum[:, 2 * (s % 3) + u, :], ones_bf, m_row[:, s % 3, 512 * u:512 * u + 512],
                                         start=False, stop=True, skip_group_check=True)
                    last.then_inc(s_sub, 1)

                def chunk(i, pr, r):
                    later, j4 = i < 4, i % 4
                    if j4 == 0:
                        reach(pe, s_prob, NS * pr + (0 if later else 4))
                        if later:
                            r = 1 - r
                        else:
                            pe.wait_ge(s_vpair, pr + 1)
                    if i in (0, 3, 4, 7):
                        reach(pe, s_rrd, 4 * pr + {0: -2, 3: -1, 4: 0, 7: 1}[i])
                    else:
                        reach(pe, s_chr, 4 * pr + {1: -1, 2: 0, 5: 1, 6: 2}[i])
                    blocks = ((1, 0), (2, 1)) if later else ((0, 0),)
                    if j4 < 2:
                        rv = 1 - r if later and j4 else r
                        for g in range(4):
                            for blk, kb in blocks:
                                for j in range(4):
                                    last = pe.matmul(psum[32 * j:32 * j + HD + 1, O_BANK, P * g:P * g + P],
                                                     v_pair[:, rv, 2 * j4 + kb, 4 * g + j, :],
                                                     probs[:, blk, H * j4 + 4 * g + j, :],
                                                     start=(kb == 0), stop=(kb == len(blocks) - 1), skip_group_check=True)
                    else:
                        for u in range(4):
                            for blk, kb in blocks:
                                for j in range(4):
                                    q0 = 16 * (4 * (j4 - 2) + u) + 4 * j
                                    x = 2 * P - 4 - (q0 + (P if later else 0) - P * kb)
                                    at, a = 32 * (q0 // 32), q0 % 32 // 2
                                    qs4 = probs[:, blk, :, at:at + 32].rearrange("p n (c a) -> p n c a", c=2)
                                    last = pe.matmul(psum[32 * j:32 * j + 32, O_BANK, P * u:P * u + P],
                                                     rel_v[:, HD * x:HD * x + 32], qs4[:, :, :, a:a + 2],
                                                     start=(kb == 0), stop=(kb == len(blocks) - 1), skip_group_check=True)
                    last.then_inc(s_chunk, 1)

                def pair(pr, r, k):
                    first = isinstance(pr, int) and pr == 0
                    pe.wait_ge(s_load[r], 16 * 4 * len(RUNS) * (k + 1))
                    for s in range(NS):
                        scores(s, pr, r)
                        if s >= 1 or not first:
                            turn_maxima(s - 1, pr)
                        if s >= 2 or not first:
                            subtract_maxima(s - 2, pr)
                        i = CHUNK_AT.get(s)
                        if i is not None and (i >= 4 or not first):
                            chunk(i, pr, r)

                in_pairs(pe, pair)
                turn_maxima(-1, NP)
                subtract_maxima(-2, NP)
                subtract_maxima(-1, NP)
                for i in range(4):
                    chunk(i, NP, 0)
                for k in range(NT // 4):
                    pe.wait_ge(s_nat, k // 2 + 1)
                    if k >= 2:
                        pe.wait_ge(s_wor, k - 1)
                    for t in range(4):
                        last = pe.matmul(psum[:, 2 + k % 2, P * t:P * t + P],
                                         o_nat[k // 2][:, P * (4 * (k % 2) + t):P * (4 * (k % 2) + t) + P], wT[:, 3, :], start=True, stop=True)
                    last.then_inc(s_wo, 1)

            expert_layer(0)
            attention()
            expert_layer(1)

        @block.vector
        def _(dve):
            v = nc.vector

            def step(i):
                s_dve.inc(i)
                dve.wait_ge(s_dve.sem, s_dve.now())

            def row_statistics(src, tiles, first=False):
                for t in tiles:
                    if first and t % 8 == 0:
                        dve.wait_ge(s_x[t // 8], 16)
                    last = v.bn_stats(stats[:, t, :], src[:, t, :])
                return last

            def variances(tiles=range(NT)):
                for t in tiles:
                    last = v.bn_aggr(mv[:, t, :], stats[:, t, :])
                step(last)
                a = slice(tiles[0], tiles[-1] + 1)
                v.tensor_scalar(vare[:, a], mv[:, a, 1], EPS, None, ALU.add).then_inc(s_sqrt_in, 1)

            def inverse_deviations(root, tiles=range(NT)):
                a = slice(tiles[0], tiles[-1] + 1)
                dve.wait_ge(s_sqrt, root + 1)
                step(v.reciprocal(r0[:, a], s0[:, a]))
                step(v.tensor_tensor(r0[:, a], r0[:, a], vare[:, a], ALU.mult))
                step(v.tensor_tensor(r0[:, a], r0[:, a], s0[:, a], ALU.add))
                step(v.tensor_scalar(r0[:, a], r0[:, a], 0.5, None, ALU.mult))
                step(v.reciprocal(rstd[:, a], r0[:, a]))

            def normalise(src, dst, root, done, tiles=range(NT)):
                inverse_deviations(root, tiles)
                for t in tiles:
                    i = v.tensor_scalar(dst[:, t, 0:D], src[:, t, :], mv[:, t, 0:1], rstd[:, t:t + 1],
                                        ALU.subtract, ALU.mult)
                    if t % 4 == 3:
                        i.then_inc(done, 1)

            def expert_layer(n):
                tr = 2 + n * TRN + (NXB if n else 0)
                if not n:
                    step(row_statistics(x_sb, range(NT), True))
                variances()
                normalise(x_sb, xn, 6 * n, s_xn)
                dve.wait_ge(s_xn, (n + 1) * NXB)
                row_statistics(xn, range(NT // 2))
                dve.wait_ge(s_logit, n + 1)
                lg = psum[:, B_GATE, 0:ET].rearrange("p (t e) -> p t e", e=E)
                lv = logit.rearrange("p (t e) -> p t e", e=E)
                step(v.tensor_reduce(lmax, lg, AX.X, ALU.max))
                v.tensor_tensor(lv, lg, lmax.unsqueeze(2).to_broadcast([P, NT, E]),
                                ALU.subtract).then_inc(s_centred, 1)
                step(row_statistics(xn, range(NT // 2, NT)))
                dve.wait_ge(s_exp, n + 1)
                step(v.tensor_reduce(lsum, lv, AX.X, ALU.add))
                step(v.reciprocal(lsum, lsum))
                v.tensor_tensor(by_et(score).rearrange("p e t -> p t e"), lv,
                                lsum.unsqueeze(2).to_broadcast([P, NT, E]), ALU.mult).then_inc(s_scored, 1)
                variances()
                step(v.memset(cand, 1 << (SCORE_BITS - 1)))
                for u in range(UNROLL + 1):
                    last = v.memset(bits[:, u:u + 1], 1 << (SCORE_BITS - 1 - u))
                inverse_deviations(6 * n + 1)
                v.scalar_tensor_tensor(out=neg_mean, in0=mv[:, :, 0], scalar=-1.0, in1=rstd, op0=ALU.mult,
                                       op1=ALU.mult).then_inc(s_zin, 1)
                dve.wait_ge(s_scT, n + 1)
                step(v.tensor_copy(score_t, psum[:, B_GATE, 0:2 * P].rearrange("p (h n) -> p h n", h=2)))

                cand_f = cand.bitcast(F32)
                PER = 3 * UNROLL + 1
                start = s_dve.n
                with dve.Fori(0, SCORE_BITS // UNROLL) as i:
                    s_dve.base = i * PER
                    for u in range(UNROLL):
                        for h in range(2):
                            last = v.tensor_scalar(mask_bf[:, h, :], score_t[:, h, :], cand_f[:, h:h + 1], None,
                                                   ALU.is_ge, ALU.add, accum_out=lane_cnt[:, h:h + 1])
                        last.then_inc(s_mask, 1)
                        step(v.tensor_tensor(seen, cand, bits[:, u + 1:u + 2].to_broadcast([P, 2]), ALU.bitwise_xor))
                        dve.wait_ge(s_cnt, i * UNROLL + (n * SCORE_BITS + u + 1))
                        step(v.scalar_tensor_tensor(out=flip, in0=psum[:, B_CNT, 0:2], scalar=float(CAP),
                                                    in1=bits[:, u:u + 1].to_broadcast([P, 2]),
                                                    op0=ALU.is_lt, op1=ALU.mult))
                        step(v.tensor_tensor(cand, seen, flip, ALU.bitwise_xor))
                    step(v.tensor_scalar(bits, bits, UNROLL, None, ALU.logical_shift_right))
                assert s_dve.n - start == PER
                s_dve.base = 0
                s_dve.n = start + PER * (SCORE_BITS // UNROLL)

                for h in range(2):
                    v.tensor_scalar(gt_bf[:, h, :], score_t[:, h, :], cand_f[:, h:h + 1], None, ALU.is_gt, ALU.add,
                                    accum_out=lane_tot[:, h:h + 1])
                    last = v.tensor_scalar(eq_bf[:, h, :], score_t[:, h, :], cand_f[:, h:h + 1], None, ALU.is_equal,
                                           ALU.add, accum_out=lane_tot[:, 2 + h:3 + h])
                last.then_inc(s_pre, 1)
                dve.wait_ge(s_pre, 2 * n + 1)
                flat = lambda a: a.rearrange("p h n -> p (h n)")
                step(v.tensor_tensor_scan(flat(scan), carry, flat(eq_bf), 0.0, ALU.mult, ALU.add))
                dve.wait_ge(s_prer, 2 * n + 1)
                step(v.tensor_copy(carry_at, psum[:, B_CNT, 2:4]))
                step(v.tensor_tensor(need, psum[:, B_CNT, 0:2], carry_at, ALU.add))
                step(v.tensor_scalar(need, need, -1.0, float(CAP), ALU.mult, ALU.add))
                for h in range(2):
                    last = v.scalar_tensor_tensor(out=sel_bf[:, h, :], in0=scan[:, h, :], scalar=need[:, h:h + 1],
                                                  in1=eq_bf[:, h, :], op0=ALU.is_le, op1=ALU.mult)
                step(last)
                step(v.tensor_tensor(flat(sel_bf), flat(sel_bf), flat(gt_bf), ALU.add))
                step(v.tensor_tensor_scan(flat(scan), carry, flat(sel_bf), 0.0, ALU.mult, ALU.add))
                v.tensor_copy(lane_tot[:, 0:2], scan[:, :, P - 1]).then_inc(s_pre, 1)
                dve.wait_ge(s_prer, 2 * n + 2)
                step(v.tensor_copy(carry_at, psum[:, B_CNT, 4:6]))
                for h in range(2):
                    last = v.scalar_tensor_tensor(out=place_t[:, h, :], in0=scan[:, h, :], scalar=carry_at[:, h:h + 1],
                                                  in1=sel_bf[:, h, :], op0=ALU.add, op1=ALU.mult)
                last.then_inc(s_q, 1)
                dve.wait_ge(s_qT, n + 1)
                step(v.tensor_scalar(pos_i, psum[:, B_GATE, 0:ET], -1.0, None, ALU.add))
                v.tensor_scalar(lo_i, pos_i, LO - 1, None, ALU.bitwise_and)
                step(v.tensor_scalar(hi_i, pos_i, 5, None, ALU.arith_shift_right))
                v.tensor_copy(lo_bf, lo_i)
                step(v.tensor_copy(hi_bf, hi_i))
                for b in range(HI):
                    last = v.tensor_scalar(eqhi[:, b, :], hi_bf, float(b), None, ALU.is_equal)
                last.then_inc(s_eqhi, 1)
                for a in range(LO):
                    v.tensor_scalar(hot_lo[:, a, :], lo_bf, float(a), None, ALU.is_equal)
                dve.wait_ge(s_eqhi, n + 1)
                dve.wait_ge(s_init, n + 1)
                v.tensor_scalar(hot_hi[:, 1], eqhi, iota_p, None, ALU.mult).then_inc(s_hot, 1)
                dve.wait_ge(s_idx, n + 1)
                si = psum[0:LO, B_IDX, 0:2 * HI * E].rearrange("p (e w b) -> p e w b", e=E, w=2)
                ip = idx_p[0:LO, :].rearrange("p (e b) -> p e b", e=E)
                step(v.tensor_copy(ip, si[:, :, 1, :]))
                step(v.scalar_tensor_tensor(out=ip, in0=si[:, :, 0, :], scalar=float(P), in1=ip,
                                            op0=ALU.mult, op1=ALU.add))
                v.tensor_copy(idx_i[0:LO, :].rearrange("p (r e j) -> p r e j", r=4, e=E),
                              idx_p[0:LO, :].rearrange("p (e j r) -> p r e j", e=E, j=NJ)).then_inc(s_idxi, 1)

                def scale(e):
                    dve.wait_ge(s_o, n * E + e + 1)
                    if e >= 2:
                        dve.wait_ge(s_sc, 64 * (n * E + e - 1))
                    for j in range(NJ):
                        last = v.tensor_scalar(osb[:, e % 2, j, :], psum[:, O_B[e % 2], P * j:P * j + P],
                                               rows[:, e * NJ + j, D + e:D + e + 1], 0.5, ALU.mult, ALU.mult)
                    last.then_inc(s_os, 1)

                def clear_stacks(e):
                    heads = slice(4 * e, 4 * e + 4)
                    step(v.memset(q_words[:, heads], 0.0))
                    v.tensor_copy(q_words[96:P, heads],
                                  parity[96:P, :].unsqueeze(1).unsqueeze(3).to_broadcast([32, 4, 2, P]))
                    last = v.memset(k_words[96:P, heads], 0.0)
                    if e == E - 1:
                        last.then_inc(s_zero, 1)

                for e in range(E):
                    k = NWB + NXB + e
                    dve.wait_ge(s_tr, tr + k + 1)
                    if n == 0 and e == 0:
                        dve.wait_ge(s_tab, 16)
                        dve.wait_ge(s_const, 9)
                    if e >= 2:
                        dve.wait_ge(s_h, (n * E + e - 1) * NC)
                    if n == 0 and e == 0:
                        dve.wait_ge(s_rk, 16 * 2 * TERMS)
                    i = v.tensor_scalar(yT[:, e % 2, :], tr_bank(tr + k), lnw, lnb, ALU.mult, ALU.add)
                    i.then_inc(s_yT, 1)
                    if e:
                        scale(e - 1)
                    if n == 0:
                        clear_stacks(e)
                scale(E - 1)

            dve.wait_ge(s_trf, 1)
            step(v.tensor_copy(ext_part[:, 0], ext))
            step(v.tensor_tensor(ext_rest, ext, ext_part[:, 0], ALU.subtract))
            step(v.tensor_copy(ext_part[:, 1], ext_rest))
            v.tensor_tensor(ext_part[:, 2], ext_rest, ext_part[:, 1], ALU.subtract).then_inc(s_ext, 1)

            def attention():
                def statistics(c):
                    dve.wait_ge(s_x[c], 32)
                    tiles = range(8 * c, 8 * c + 8)
                    step(row_statistics(x_sb, tiles))
                    variances(tiles)

                dve.wait_ge(s_const, 7)
                step(v.tensor_copy(lane_i, iota_p))
                step(v.tensor_scalar(lane_i, lane_i, 3, 3, ALU.logical_shift_right, ALU.bitwise_and))
                step(v.tensor_copy(lane_f, lane_i))
                for c in range(2):
                    for a in range(2):
                        last = v.tensor_scalar(own_q[:, 2 * c + a:2 * c + a + 1], lane_f, float(3 - 2 * a - c), None,
                                               ALU.is_equal)
                step(last)

                def rest_of(i):
                    dve.wait_ge(s_p1, i + 1)
                    if i >= 2:
                        dve.wait_ge(s_part, i - 1)
                    v.tensor_tensor(rest[:, i % 2, :], psum[:, 2 + i % 2, :], part[:, i % 4, 0, :],
                                    ALU.subtract).then_inc(s_p1r, 1)

                def third_part(i):
                    dve.wait_ge(s_p2, i + 1)
                    v.tensor_tensor(part[:, i % 4, 2, :], rest[:, i % 2, :], part[:, i % 4, 1, :],
                                    ALU.subtract).then_inc(s_part, 1)

                statistics(0)
                for c in range(4):
                    normalise(x_sb, an, 2 + c, s_an, range(8 * c, 8 * c + 8))
                    if c < 3:
                        statistics(c + 1)
                    rest_of(4 * c)
                    for i in range(4 * c, 4 * c + 4):
                        if i % 4 < 3:
                            rest_of(i + 1)
                        third_part(i)

                def partial_maxima(s, pr):
                    g = NS * pr + s
                    dve.wait_ge(s_score, g + 1)
                    later = SLOTS[s][2]
                    mp = m_part[:, s % 3, :]
                    i = v.tensor_reduce(mp, psum[:, 2 * (s % 3):2 * (s % 3) + 2, :].rearrange("p u (h n) -> p (u h) n", n=32),
                                        AX.X, ALU.max, apply_transpose=True)
                    if not later:
                        i.then_inc(s_T, 1)
                        return
                    step(i)
                    m2 = mp.rearrange("p (u h) -> p u h", u=2)
                    step(v.tensor_tensor(m2[:, 0, :], m2[:, 0, :], m2[:, 1, :], ALU.max))
                    v.tensor_copy(m2[:, 1, :], m2[:, 0, :]).then_inc(s_T, 1)

                def rows_of_maxima(s, pr):
                    g = NS * pr + s
                    dve.wait_ge(s_tT, g + 1)
                    hl = m_hl[0:32, s % 3]
                    step(v.tensor_reduce(m_neg[0:32, :], psum[0:32, T_BANK, 0:P].rearrange("p (i q) -> p q i", i=4),
                                         AX.X, ALU.max, negate=True))
                    step(v.tensor_copy(hl[:, 0, :], m_neg[0:32, :]))
                    v.tensor_tensor(hl[:, 1, :], m_neg[0:32, :], hl[:, 0, :], ALU.subtract).then_inc(s_row, 1)

                def reduce_relative(i, pr):
                    later, half = i < 4, i % 2
                    n = 4 * pr + (i - 3 if later else i - 5)
                    dve.wait_ge(s_chunk, 8 * pr + i - 3)
                    reach(dve, s_rr, n - 1)
                    v.tensor_tensor(r_tmp.rearrange("p (n q) -> p n q", q=4),
                                    psum[:, O_BANK, :].rearrange("p (n q) -> p n q", q=4),
                                    own_q.unsqueeze(1).to_broadcast([P, P, 4]), ALU.mult).then_inc(s_rrd, 1)
                    dve.wait_ge(s_rrd, n)
                    if i == 6:
                        reach(dve, s_rst, 16 * pr)
                    u = 8 * later + 4 * half
                    v.tensor_reduce(r_sb[:, :, :, u:u + 4].rearrange("p h b u -> p u b h"),
                                    r_tmp.rearrange("p (u b h q) -> p u b h q", u=4, b=2, h=H),
                                    AX.X, ALU.add).then_inc(s_rr, 1)

                def pair(pr, r, k):
                    first = isinstance(pr, int) and pr == 0
                    for s in range(NS):
                        i = CHUNK_AT.get(s - 1)
                        if i in (2, 3) and not first or i in (6, 7):
                            reduce_relative(i, pr)
                        if s >= 1 or not first:
                            rows_of_maxima(s - 1, pr)
                        partial_maxima(s, pr)
                        if isinstance(pr, int) and pr == NP - 1 and s == 5:
                            dve.wait_ge(s_sum, 48)
                            v.reciprocal(sums[:, 0:3], sums[:, 0:3]).then_inc(s_inv, 1)

                per = 2 * (NS * 2 + 8 * 2)
                pair(0, 0, 0)
                start = s_dve.n
                with dve.Fori(0, NP // 2 - 1) as i:
                    s_dve.base = i * per
                    pair(2 * i + 1, 1, i)
                    pair(2 * i + 2, 0, i + 1)
                assert s_dve.n - start == per, (s_dve.n - start, per)
                s_dve.base, s_dve.n = 0, start + per * (NP // 2 - 1)
                pair(NP - 1, 1, NP // 2 - 1)
                rows_of_maxima(-1, NP)
                for i in (2, 3):
                    reduce_relative(i, NP)

                def normalised(c):
                    dve.wait_ge(s_all[c], 32)
                    dve.wait_ge(s_turned, c + 1)
                    own = lambda a, u: a.rearrange("p (n c a) -> p n c a", c=2, a=16)[:, :, u, :]
                    tok = lambda u: o_nat[c].rearrange("p (n a c) -> p n a c", c=2, a=16)[:, :, :, u]
                    for u in range(2):
                        last = v.tensor_tensor(tok(u), tok(u), own(o_all[c], u), ALU.add)
                    step(last)
                    for u in range(2):
                        last = v.tensor_tensor(tok(u), tok(u), own(o_inv[c], u), ALU.mult)
                    last.then_inc(s_nat, 1)

                def residual(c):
                    for k in (2 * c, 2 * c + 1):
                        dve.wait_ge(s_wo, k + 1)
                        xk = x_sb[:, 4 * k:4 * k + 4, :]
                        v.tensor_tensor(xk, xk, psum[:, 2 + k % 2, :].rearrange("p (t d) -> p t d", t=4),
                                        ALU.add).then_inc(s_wor, 1)

                def next_statistics(c):
                    dve.wait_ge(s_wor, 2 * c + 2)
                    return row_statistics(x_sb, range(8 * c, 8 * c + 8))

                for c in range(4):
                    if c == 3:
                        dve.wait_ge(s_sum, 64)
                        v.reciprocal(sums[:, 3], sums[:, 3]).then_inc(s_inv, 1)
                        next_statistics(1)
                    normalised(c)
                    if c:
                        residual(c - 1)
                residual(3)
                next_statistics(0)
                next_statistics(2)
                step(next_statistics(3))

            expert_layer(0)
            attention()
            expert_layer(1)


_INS = ['L0_attn_x', 'L0_attn_Wq', 'L0_attn_Wk', 'L0_attn_Wv', 'L0_attn_Wo', 'L0_attn_pek', 'L0_attn_pev',
        'L0_ffn_gate_w', 'L0_ffn_ln_w', 'L0_ffn_ln_b', 'L0_ffn_fc1s', 'L0_ffn_b1s', 'L0_ffn_fc2s', 'L0_ffn_b2s']
_OUTS = [((16, 256, 128), 'float32')]


def kernel(**inputs):
    import numpy as _np
    import concourse.bacc as _bacc
    from concourse import mybir as _mybir
    from concourse.bass_utils import run_bass_kernel_spmd as _run

    nc = _bacc.Bacc("TRN2", target_bir_lowering=False, num_devices=1)
    arrays, args = {}, []
    for name in _INS:
        a = _np.ascontiguousarray(inputs[name])
        arrays[f"in_{name}_dram"] = a
        args.append(nc.dram_tensor(f"in_{name}_dram", a.shape, _mybir.dt.from_np(a.dtype), kind="ExternalInput").ap())
    for i, (shape, dtype) in enumerate(_OUTS):
        dt = _mybir.dt.from_np(_np.dtype(dtype))
        args.append(nc.dram_tensor(f"out_{i}_dram", shape, dt, kind="ExternalOutput").ap())
    macaron_block(nc, *args)
    r = _run(nc, [arrays], core_ids=[0])
    got = tuple(r.results[0][f"out_{i}_dram"] for i in range(len(_OUTS)))
    return got[0]
```

```python
from contextlib import ExitStack

import concourse.bass as bass
from concourse import mybir

F32 = mybir.dt.float32
BF16 = mybir.dt.bfloat16
I32 = mybir.dt.int32
U32 = mybir.dt.uint32
ALU = mybir.AluOpType
ACT = mybir.ActivationFunctionType
AX = mybir.AxisListType
P = 128


class Tally:

    def __init__(self, sem):
        self.sem, self.n, self.base = sem, 0, 0

    def inc(self, instruction, by=1):
        instruction.then_inc(self.sem, by)
        self.n += by
        return self.n

    def now(self):
        return self.n + self.base if not isinstance(self.base, int) or self.base else self.n


def macaron_block(nc, x, wq, wk, wv, wo, pek, pev, gate_w, ln_w, ln_b, fc1s, b1s, fc2s, b2s, out):
    NB, L, D = x.shape
    E, FF, _ = fc1s.shape
    TOK = NB * L
    NT = TOK // P
    CAP = TOK // E
    NJ = CAP // P
    NC = FF // P
    ET = E * NT
    GW = D + E
    EPS = 1e-5
    SCORE_BITS, UNROLL = 30, 5
    LO, HI = 32, CAP // 32
    assert D == P and NJ == 4 and NT == 32 and E == 8 and NC == 4

    ctx = ExitStack()
    with ctx:
        def sem(name):
            return ctx.enter_context(nc.semaphore(name))

        ARENA = 52000
        arena = ctx.enter_context(nc.sbuf_tensor("arena", [P, ARENA], F32))
        psum = ctx.enter_context(nc.psum_tensor("banks", [P, 8, 512], F32))
        taken = [0]
        H, HD = 16, D // 16
        NP = NB // 2
        PT = 2 * L
        TERMS = 6
        Q_PART = (0, 0, 0, 1, 1, 2)
        K_PART = (0, 1, 2, 0, 1, 0)
        RUNS = ((0, 3), (3, 5), (5, 6))
        LOADS = 4 * len(RUNS)
        BIG = 1e30
        PW = 384
        assert L == 2 * P and H * HD == D and TERMS * 2 * HD <= 96

        def place(words, at=None):
            at = taken[0] if at is None else at
            taken[0] = max(taken[0], at + words)
            assert taken[0] <= ARENA, taken[0]
            return arena[:, at:at + words], at

        ident, _ = place(P)
        ones_bf = place(P // 2)[0].bitcast(BF16)
        same_bf = place(P // 2)[0].bitcast(BF16)
        before_bf = place(P // 2)[0].bitcast(BF16)
        tile_bf = place(ET // 2)[0].bitcast(BF16)
        iota_p = place(1)[0]
        carry, _ = place(ET)
        ones_row, _ = place(P)
        gwT, _ = place(E)
        b1T, _ = place(E * NC)
        b2_all = place(E * D)[0].rearrange("p (e d) -> p e d", e=E)
        lnw, _ = place(1)
        lnb, _ = place(1)
        wT = place(4 * D)[0].rearrange("p (w d) -> p w d", w=4)
        rel_k = place(PW // 2)[0].bitcast(BF16)
        parity = place(2)[0]
        stats = place(NT * 6)[0].rearrange("p (t s) -> p t s", s=6)
        mv = place(NT * 2)[0].rearrange("p (t s) -> p t s", s=2)
        vare, s0, r0, rstd = (place(NT)[0] for _ in range(4))
        x_sb, _ = place(NT * D)
        x_sb = x_sb.rearrange("p (t d) -> p t d", d=D)
        PHASE = taken[0]

        w1T = place(E * FF)[0].rearrange("p (e f) -> p e f", e=E)
        w2T = place(E * FF)[0].rearrange("p (e c d) -> p e c d", e=E, c=NC)
        hT = place(2 * NC * CAP)[0].rearrange("p (b c s) -> p b c s", b=2, c=NC)
        xnT, _ = place(NT * D)
        raw1 = place(E * FF)[0].rearrange("p (e c d) -> p e c d", e=E, c=NC)
        raw2 = place(E * FF)[0].rearrange("p (e f) -> p e f", e=E)
        zt = place(NT * GW)[0].rearrange("p (t g) -> p t g", g=GW)
        rows, at_xn = place(E * NJ * GW)
        rows = rows.rearrange("p (s g) -> p s g", g=GW)
        xn = place(NT * D, at_xn)[0].rearrange("p (t d) -> p t d", d=D)
        half_xn = hT.rearrange("p b c s -> p (b c s)")
        yT, _ = place(2 * CAP)
        yT = yT.rearrange("p (b s) -> p b s", b=2)
        osb, _ = place(2 * CAP)
        osb = osb.rearrange("p (b j d) -> p b j d", b=2, j=NJ)
        hot_lo = place(ET * LO // 2)[0].bitcast(BF16).rearrange("p (a n) -> p a n", a=LO)
        hot_hi = half_xn.bitcast(BF16).rearrange("p (w b n) -> p w b n", w=2, b=HI)
        lmax, lsum = place(NT)[0], place(NT)[0]
        logit, _ = place(ET)
        score, _ = place(ET)
        score_t = place(2 * P)[0].rearrange("p (h n) -> p h n", h=2)
        cand, flip, seen = (place(2)[0].bitcast(I32) for _ in range(3))
        bits = place(UNROLL + 1)[0].bitcast(I32)
        lane_cnt = place(1)[0].bitcast(BF16)
        lane_tot = place(2)[0].bitcast(BF16)
        need, carry_at = place(2)[0], place(2)[0]
        mask_bf, gt_bf, eq_bf, sel_bf = (place(P)[0].bitcast(BF16).rearrange("p (h n) -> p h n", h=2)
                                         for _ in range(4))
        scan, place_t = (place(2 * P)[0].rearrange("p (h n) -> p h n", h=2) for _ in range(2))
        pos_i, lo_i, hi_i = (place(ET)[0].bitcast(I32) for _ in range(3))
        lo_bf, hi_bf = (place(ET // 2)[0].bitcast(BF16) for _ in range(2))
        neg_mean = place(NT)[0]
        idx_p, _ = place(E * HI)
        idx_i = place(E * HI)[0].bitcast(I32)
        idx = place(E * NJ)[0].bitcast(U32)
        eqhi = place(ET * HI // 2)[0].bitcast(BF16).rearrange("p (b n) -> p b n", b=HI)

        taken[0] = PHASE
        probs, at_probs = place(3 * 2 * H * P)
        probs = probs.rearrange("p (k n q) -> p k n q", k=3, n=2 * H)
        q_st, at_q = place(2 * H * PT // 2)
        q_st = q_st.bitcast(BF16).rearrange("p (r h c n) -> p r h c n", r=2, h=H, c=2)
        k_st, at_k = place(2 * H * PT // 2)
        k_st = k_st.bitcast(BF16).rearrange("p (r h n) -> p r h n", r=2, h=H)
        v_all = place(NT * H * 9)[0].rearrange("p (t h n) -> p t h n", t=NT, h=H)
        v_pair = place(2 * 4 * H * 9)[0].rearrange("p (r t h n) -> p r t h n", r=2, t=4, h=H)
        rel_v = place(2 * P * HD)[0]
        m_row = place(3 * 512)[0].bitcast(BF16).rearrange("p (r n) -> p r n", r=3)
        m_part = place(3 * 32)[0].rearrange("p (r n) -> p r n", r=3)
        m_neg = place(32)[0]
        m_hl = place(3 * 32)[0].bitcast(BF16).rearrange("p (r w n) -> p r w n", r=3, w=2)
        o_sb = place(2 * 512)[0].rearrange("p (r g n) -> p r g n", r=2, g=4)
        r_tmp = place(512)[0]
        r_sb = place(2 * H * 16)[0].rearrange("p (h b u) -> p h b u", h=H, b=2)
        own_q = place(4)[0]
        lane_i, lane_f = place(1)[0].bitcast(I32), place(1)[0]
        sums = place(4 * P)[0].rearrange("p (c n) -> p c n", c=4)
        assert taken[0] <= ARENA
        q_words = arena[:, at_q:at_q + H * PT].rearrange("p (h c n) -> p h c n", c=2, n=PT // 4)
        k_words = arena[:, at_k:at_k + H * PT].rearrange("p (h n) -> p h n", n=PT // 2)
        an = place(NT * D, at_probs)[0].rearrange("p (t d) -> p t d", d=D)
        anT = place(NT * D, at_probs + NT * D)[0]
        part = place(4 * 3 * 256, at_probs + 2 * NT * D)[0].bitcast(BF16).rearrange("p (r w n) -> p r w n", r=4, w=3)
        rest = place(2 * 512, at_probs + 2 * NT * D + 3072)[0].rearrange("p (r n) -> p r n", r=2)
        QT = TOK // 4
        quarter = [place(4 * QT, at_q + 4 * QT * b)[0].rearrange("p (w n) -> p w n", w=4) for b in (0, 2, 1, 3)]
        o_all, o_inv, o_rel, o_nat = ([a[:, w] for a in quarter] for w in range(4))

        def by_et(a):
            return a.rearrange("p (e t) -> p e t", e=E)

        table = [nc.dram_tensor(f"table{n}", [TOK, GW], F32).ap() for n in range(2)]
        x_mid = nc.dram_tensor("x_mid", [TOK, D], F32).ap()
        out_rows = out.rearrange("b l d -> (b l) d")
        total = [x_mid, out_rows]
        qs = nc.dram_tensor("query_parts", [3, HD, H, TOK], BF16).ap()
        ks = nc.dram_tensor("key_parts", [3, HD, H, TOK], BF16).ap()
        pv_ext = nc.dram_tensor("rel_v_extended", [PW, HD], F32).ap()
        o_dram = nc.dram_tensor("head_outputs", [H, 32, TOK], F32).ap()
        o_rows = o_dram.rearrange("(g j) d n -> (j d) g n", j=4)
        inv_dram = nc.dram_tensor("inverse_sums", [H, TOK], F32).ap()
        r_dram = nc.dram_tensor("relative_outputs", [P, H, 2 * P], F32).ap()

        s_par = sem("parameters_loaded")
        s_b2 = sem("second_biases_loaded")
        s_raw = sem("raw_weights_loaded")
        s_x = [sem(f"x_loaded{c}") for c in range(4)]
        s_const = sem("constants_ready")
        s_dve = Tally(sem("vector_steps"))
        s_pool = Tally(sem("pool_steps"))
        s_act = Tally(sem("scalar_steps"))
        s_sqrt_in, s_sqrt = sem("variance_ready"), sem("root_ready")
        s_tr = sem("transposed_bank")
        s_trf = sem("transposed_bank_read")
        s_xn = sem("xn_ready")
        s_z = sem("table_rows_ready")
        s_half, s_init = sem("half_xn_ready"), sem("residual_ready")
        s_zin = sem("row_statistics_ready")
        s_scored, s_scT = sem("scores_ready_by_expert"), sem("scores_transposed")
        s_q, s_qT = sem("places_ready"), sem("places_transposed")
        s_eqhi, s_hot_t = sem("high_places_ready"), sem("tile_numbers_placed")
        s_logit = sem("logits_ready")
        s_centred = sem("logits_centred")
        s_exp = sem("exp_ready")
        s_mask, s_cnt = sem("mask_counted"), sem("counts_ready")
        s_pre, s_prer = sem("prefix_asked"), sem("prefix_ready")
        s_hot, s_idx = sem("one_hots_ready"), sem("index_sums_ready")
        s_idxi, s_idxd = sem("indices_ready"), sem("indices_spread")
        s_tab, s_acc = sem("table_stored"), sem("residual_stored")
        s_rows = [sem(f"rows_gathered{e}") for e in range(E)]
        s_yT = sem("yT_ready")
        s_h, s_g = sem("fc1_ready"), sem("gelu_ready")
        s_o, s_os = sem("fc2_ready"), sem("out_scaled")
        s_sc = sem("scattered")
        s_back = sem("x_reloaded")
        s_ffn = sem("experts_done")
        s_pe1 = sem("rel_v_extended_stored")
        s_rk = sem("rel_k_rows_loaded")
        s_rv = sem("rel_v_loaded")
        s_ext = sem("rel_k_parts_ready")
        s_an, s_anT = sem("attention_input_ready"), sem("attention_input_transposed")
        s_pj, s_p1, s_p1r = sem("projection_ready"), sem("first_part_ready"), sem("rest_ready")
        s_p2, s_part, s_pst = sem("second_part_ready"), sem("parts_ready"), [sem(f"parts_stored{i}") for i in range(4)]
        s_vp, s_vr = sem("values_projected"), sem("values_read")
        s_parity = sem("parity_rows_ready")
        s_zero = sem("attention_buffers_cleared")
        s_load = [sem(f"pair_loaded{i}") for i in range(2)]
        s_first = sem("first_pair_loaded")
        s_vpair = sem("pair_values_ready")
        s_score, s_T, s_tT = sem("scores_ready"), sem("partial_maxima_ready"), sem("maxima_transposed")
        s_row = sem("negated_maxima_ready")
        s_m = [sem(f"maxima_row_loaded{i}") for i in range(3)]
        s_sub, s_prob = sem("maxima_subtracted"), sem("probabilities_ready")
        s_chunk, s_chr = sem("outputs_ready"), sem("head_outputs_read")
        s_rr, s_rrd = sem("relative_outputs_reduced"), sem("relative_bank_read")
        s_ost = [sem(f"head_outputs_stored{i}") for i in range(2)]
        s_rst = sem("relative_outputs_stored")
        s_sum, s_inv, s_invst = sem("sums_loaded"), sem("sums_inverted"), sem("inverse_sums_stored")
        s_all = [sem(f"head_outputs_loaded{c}") for c in range(4)]
        s_rel = [sem(f"relative_outputs_loaded{c}") for c in range(4)]
        s_turned = sem("relative_outputs_in_token_order")
        s_nat = sem("outputs_normalised")
        s_wo, s_wor = sem("output_projected"), sem("output_added")

        block = ctx.enter_context(nc.Block())

        TR = (0, 1)
        B_GATE, B_CNT, B_IDX = 2, 3, 3
        H_B, O_B = (4, 5), (6, 7)

        NWB = 2 * E
        NXB = NT // 4
        NAB = NWB + NXB
        NYB = E
        TRN = NWB + NXB + NYB

        ext = osb.rearrange("p b j d -> p (b j d)")[0:HD, 0:PW]
        ext_rest = osb.rearrange("p b j d -> p (b j d)")[0:HD, PW:2 * PW]
        ext_part = yT.rearrange("p b s -> p (b s)").bitcast(BF16)[0:HD, 0:3 * PW].rearrange("p (w n) -> p w n", w=3)

        def in_pairs(engine, pair):
            pair(0, 0, 0)
            with engine.Fori(0, NP // 2 - 1) as i:
                pair(2 * i + 1, 1, i)
                pair(2 * i + 2, 0, i + 1)
            pair(NP - 1, 1, NP // 2 - 1)

        def reach(engine, semaphore, value):
            if not isinstance(value, int) or value > 0:
                engine.wait_ge(semaphore, value)

        SLOTS = [(0, 0, False), (0, 2, False), (1, 0, False), (1, 2, False)] + \
                [(b, q, True) for b in range(2) for q in range(4, 8)]
        NS = len(SLOTS)
        REL_EARLY, REL_LATER, AV_LATER1, AV_EARLY, AV_LATER0 = (0, 1), (2, 3), 4, (5, 6), 7
        CHUNK_AT = {0: (0, 0, 4), 1: (1, 0, 4), 2: (2, 0, 2), 3: (2, 2, 4), 4: (3, 0, 2), 5: (3, 2, 4),
                    6: (4, 0, 2), 7: (4, 2, 4), 8: (5, 0, 4), 9: (6, 0, 4), 10: (7, 0, 2), 11: (7, 2, 4)}

        TAIL = (0, 1, 4, 2, 3)

        def chunks(pr, i):
            return 8 * pr - 4 + (TAIL.index(i) if isinstance(pr, int) and pr == NP else i)

        def value_chunks(pr, i):
            return 4 * pr + i - 4

        def relative_chunks(pr, i):
            return 4 * pr + i - 3

        T_BANK, O_BANK = 6, 7
        WO_BANK = (4, 5)
        TAIL_BANK = (O_BANK, 0, 2, 3, 1)

        def stacked(pr, r):
            for a, b in RUNS:
                for c in range(2):
                    lanes = slice((TERMS * c + a) * HD, (TERMS * c + b) * HD)
                    q = qs[Q_PART[a], 0:HD, :, bass.ds(pr * PT + c * L, L)]
                    q = q.unsqueeze(0).to_broadcast([b - a, HD, H, L])
                    k = ks[0:b - a, :, :, bass.ds(pr * PT, PT)].rearrange("w d h n -> (w d) h n")
                    yield q_st[lanes, r, :, c, :], q
                    yield k_st[lanes, r, :, :], k

        def load_sums(engine, c):
            src = o_dram[:, HD, c * QT:c * QT + QT].rearrange("h (m n) -> h m n", n=P)
            engine.dma_start(sums[:, c], src).then_inc(s_sum, 16)

        def store_inverses(engine, c):
            dst = inv_dram[:, c * QT:c * QT + QT].rearrange("h (m n) -> h m n", n=P)
            engine.dma_start(dst, sums[:, c]).then_inc(s_invst, 16)

        def load_outputs(engine, c):
            src = o_dram[:, 0:HD, c * QT:c * QT + QT]
            engine.dma_start(o_all[c], src).then_inc(s_all[c], 16)

        def load_relative(engine, c):
            u = QT // 16
            src = r_dram[:, :, c * u:c * u + u].rearrange("(c d) h n -> d h c n", d=HD)
            for d in range(HD):
                engine.dma_start(o_rel[c][d:P:HD, :].rearrange("h (c u) -> h c u", c=16), src[d]).then_inc(s_rel[c], 16)

        def load_inverses(engine, c):
            src = bass.AP(inv_dram.tensor, c * QT, [[TOK, H], [0, HD], [1, QT]])
            engine.dma_start(o_inv[c], src).then_inc(s_all[c], 16)

        ALL = slice(0, NT)
        QUARTERS = [slice(8 * c, 8 * c + 8) for c in range(4)]

        def tr_bank(k):
            return psum[:, TR[k % 2], :]

        @block.sync
        def _(sp):
            xr = x.rearrange("b l d -> (b l) d").rearrange("(t p) d -> p t d", p=P)
            for c in range(4):
                sp.dma_start(x_sb[:, 8 * c:8 * c + 8, :], xr[:, 8 * c:8 * c + 8, :]).then_inc(s_x[c], 16)
            sp.dma_start(logit[0:E, 0:D], gate_w).then_inc(s_par, 16)
            sp.dma_start(logit[0:E * NC, D:2 * D], b1s.rearrange("e (c p) -> (e c) p", p=P)).then_inc(s_par, 16)
            sp.dma_start(lnw, ln_w.unsqueeze(1)).then_inc(s_par, 16)
            sp.dma_start(lnb, ln_b.unsqueeze(1)).then_inc(s_par, 16)
            for i, w in enumerate((wq, wk, wv, wo)):
                sp.dma_start(hT[:, 0, i, 0:D], w).then_inc(s_par, 16)
            sp.dma_start(hT[:, 1, 0, 0:2 * HD].rearrange("p (t d) -> p t d", t=2),
                         pek[0:2 * P, :].rearrange("(t p) d -> p t d", p=P)).then_inc(s_par, 16)
            sp.dma_start(b2_all, b2s.unsqueeze(0).to_broadcast([P, E, D])).then_inc(s_b2, 16)
            sp.dma_start(pv_ext[0:P - 1, :], pev[0:1, :].to_broadcast([P - 1, HD])).then_inc(s_pe1, 16)
            sp.dma_start(pv_ext[P - 1:3 * P - 1, :], pev[0:2 * P, :]).then_inc(s_pe1, 16)

            def expert_layer(n):
                if n:
                    sp.wait_ge(s_wor, NT // 4)
                for h in range(2):
                    es = slice(4 * h, 4 * h + 4)
                    sp.dma_start(raw1[:, es], fc1s[es].rearrange("e (c p) d -> p e c d", p=P)).then_inc(s_raw, 16)
                    sp.dma_start(raw2[:, es], fc2s[es].rearrange("e d f -> d e f")).then_inc(s_raw, 16)
                sp.wait_ge(s_init, n + 1)
                sp.dma_start(total[n].rearrange("(t p) d -> p t d", p=P), x_sb).then_inc(s_acc, 16)
                sp.wait_ge(s_z, 2 * n + 2)
                sp.dma_start(table[n].rearrange("(t p) g -> p t g", p=P), zt).then_inc(s_tab, 16)
                sp.wait_ge(s_idxi, n + 1)
                for r in range(4):
                    sp.dma_start(idx[32 * r:32 * r + 32, :],
                                 idx_i[0:32, 32 * r:32 * r + 32].bitcast(U32)).then_inc(s_idxd, 16)

            sp.wait_ge(s_ext, 1)
            sp.wait_ge(s_const, 9)
            for t in range(TERMS):
                for c in range(2):
                    r = (TERMS * c + t) * HD
                    sp.dma_start(rel_k[r:r + HD, 0:PW - 2], ext_part[:, K_PART[t], 1 - c:PW - 1 - c]).then_inc(s_rk, 16)

            def attention():
                sp.wait_ge(s_ffn, 1)
                xm = x_mid.rearrange("(t p) d -> p t d", p=P)
                for c in range(4):
                    sp.dma_start(x_sb[:, 8 * c:8 * c + 8, :], xm[:, 8 * c:8 * c + 8, :]).then_inc(s_x[c], 16)
                sp.wait_ge(s_pe1, 32)
                sp.dma_start(rel_v, bass.AP(pv_ext.tensor, 0, [[HD, P], [1, 2 * P * HD]])).then_inc(s_rv, 16)
                loads = list(stacked(0, 0))
                for i in range(2 * NP):
                    sp.wait_ge(s_part, i + 1)
                    dst = (qs if i % 2 == 0 else ks)[:, :, :, PT * (i // 2):PT * (i // 2) + PT]
                    sp.dma_start(dst.rearrange("w d h n -> (d h) w n"), part[:, i % 4]).then_inc(s_pst[i % 4], 16)
                    if i == 4:
                        for b in range(2):
                            sp.wait_ge(s_pst[b], 16)
                    if i >= 4:
                        sp.dma_start(*loads.pop(0)).then_inc(s_first, 16)

                def pair(pr, r, k):
                    for s in range(NS):
                        sp.wait_ge(s_row, NS * pr + s + 1)
                        for w in range(2):
                            sp.dma_start(m_row[w:w + 1, s % 3, :].rearrange("o (a b) -> o a b", a=32),
                                         m_hl[0:32, s % 3, w, :]).then_inc(s_m[s % 3], 16)

                in_pairs(sp, pair)
                sp.wait_ge(s_score, NS * NP)
                sp.wait_ge(s_rst, 16 * (NP - 1))
                load_relative(sp, 2)
                sp.wait_ge(s_rst, 16 * (NP + 1))
                load_relative(sp, 3)
            expert_layer(0)
            attention()
            expert_layer(1)

        @block.gpsimd
        def _(pool):
            def step(i):
                s_pool.inc(i)
                pool.wait_ge(s_pool.sem, s_pool.now())

            step(pool.memset(ident, 0.0))
            pool.affine_select(out=ident, in_=ident, compare_op=ALU.not_equal, fill=1.0, base=0,
                               pattern=[[-1, P]], channel_multiplier=1).then_inc(s_const, 1)
            step(pool.memset(same_bf, 0.0))
            for b in range(4):
                last = pool.memset(same_bf[32 * b:32 * b + 32, 32 * b:32 * b + 32], 1.0)
            last.then_inc(s_const, 1)
            pool.wait_ge(s_const, 2)
            pool.affine_select(out=before_bf, in_=same_bf, compare_op=ALU.is_gt, fill=0.0, base=0,
                               pattern=[[1, P]], channel_multiplier=-1).then_inc(s_const, 1)
            pool.memset(ones_bf, 1.0).then_inc(s_const, 1)
            pool.memset(ones_row, 1.0).then_inc(s_const, 1)
            step(pool.memset(carry, 1.0))
            step(pool.memset(carry[:, P:P + 1], 0.0))
            step(pool.iota(pos_i, pattern=[[0, E], [1, NT]], base=0, channel_multiplier=0))
            pool.tensor_copy(tile_bf, pos_i).then_inc(s_const, 1)
            step(pool.iota(lo_i[:, 0:1], pattern=[[0, 1]], base=0, channel_multiplier=1))
            pool.tensor_copy(iota_p, lo_i[:, 0:1]).then_inc(s_const, 1)

            step(pool.memset(parity, 0.0))
            pool.affine_select(out=parity[96:P, :].bitcast(BF16).rearrange("p (c w) -> p c w", c=2),
                               in_=parity[96:P, :].bitcast(BF16).rearrange("p (c w) -> p c w", c=2),
                               compare_op=ALU.not_equal, fill=1.0, base=0, pattern=[[-1, 2], [0, 2]],
                               channel_multiplier=1).then_inc(s_const, 1)
            pool.wait_ge(s_const, 8)

            step(pool.memset(rel_k, 0.0))
            pool.affine_select(out=rel_k[96:P, :], in_=rel_k[96:P, :], compare_op=ALU.is_ge, fill=-BIG,
                               base=2 * P - 2, pattern=[[-1, PW]], channel_multiplier=1).then_inc(s_const, 1)

            def expert_layer(n):
                pool.wait_ge(s_scored, n + 1)
                pool.tensor_copy(zt[:, :, D:GW], by_et(score).rearrange("p e t -> p t e")).then_inc(s_z, 1)
                pool.wait_ge(s_half, n + 1)
                pool.tensor_tensor(x_sb.rearrange("p t d -> p (t d)"), x_sb.rearrange("p t d -> p (t d)"),
                                   half_xn, ALU.add).then_inc(s_init, 1)
                pool.wait_ge(s_eqhi, n + 1)
                pool.wait_ge(s_init, n + 1)
                pool.tensor_tensor(hot_hi[:, 0], eqhi, tile_bf.unsqueeze(1).to_broadcast([P, HI, ET]),
                                   ALU.mult).then_inc(s_hot_t, 1)
                pool.wait_ge(s_idxd, 64 * (n + 1))
                pool.wait_ge(s_tab, 16 * (n + 1))

                def gather(e):
                    for j in range(NJ):
                        s = e * NJ + j
                        pool.indirect_dma_start(
                            out=rows[:, s, :], out_offset=None, in_=table[n],
                            in_offset=bass.IndirectOffsetOnAxis(ap=idx[:, s:s + 1], axis=0)).then_inc(s_rows[e], 16)

                def scatter(e):
                    pool.wait_ge(s_os, n * E + e + 1)
                    if e:
                        pool.wait_ge(s_sc, 64 * (n * E + e))
                    for j in range(NJ):
                        s = e * NJ + j
                        pool.indirect_dma_start(
                            out=total[n], out_offset=bass.IndirectOffsetOnAxis(ap=idx[:, s:s + 1], axis=0),
                            in_=osb[:, e % 2, j, :], in_offset=None, compute_op=ALU.add).then_inc(s_sc, 16)

                AHEAD = 5
                for e in range(AHEAD):
                    gather(e)
                pool.wait_ge(s_acc, 16 * (n + 1))
                for e in range(E):
                    scatter(e)
                    if e + AHEAD < E:
                        gather(e + AHEAD)
                    elif n == 0 and e < E - 1:
                        q, i = 2 * H // 4, e - (E - AHEAD)
                        pool.memset(k_words[96:P, q * i:q * i + q], 0.0).then_inc(s_zero, 1)
                        pool.wait_ge(s_zero, i + 2)
                pool.wait_ge(s_sc, 64 * (n + 1) * E)
                pool.nop().then_inc(s_ffn, 1)

            def settled(semaphore, value):
                reach(pool, semaphore, value)
                pool.wait_ge(s_const, 9)

            def attention():
                pool.dma_start(inv_dram[0:1, 0:P], ones_row[0:1, :]).then_inc(s_rst, 16)
                pool.memset(v_all[:, :, :, HD:HD + 1], 1.0)
                step(pool.memset(m_row, 0.0))

                def third_part(i):
                    pool.wait_ge(s_p2, i + 1)
                    pool.tensor_tensor(part[:, i % 4, 2, :], rest[:, i % 2, :], part[:, i % 4, 1, :],
                                       ALU.subtract).then_inc(s_part, 1)

                for i in range(2 * NP):
                    third_part(i)

                def pair(pr, r, k):
                    first, last = isinstance(pr, int) and pr == 0, isinstance(pr, int) and pr == NP - 1
                    if first:
                        pool.wait_ge(s_vr, NT // 4)
                    if not first:
                        settled(s_chunk, 8 * pr - 7)
                    pool.tensor_copy(v_pair[:, r], v_all[:, bass.ds(pr * 4, 4)]).then_inc(s_vpair, 1)
                    if first:
                        for i in range(4):
                            pool.wait_ge(s_pst[i], 16 * (NP // 2))
                    loads = [] if last else list(stacked(pr + 1, 1 - r))
                    if loads:
                        settled(s_score, NS * pr)

                    def load_some(n):
                        for dst, src in loads[:n]:
                            pool.dma_start(dst, src).then_inc(s_load[1 - r], 16)
                        del loads[:n]

                    def store_heads(i, before, b, q):
                        settled(s_chr, value_chunks(before, i))
                        pool.dma_start(o_rows[:, :, bass.ds(b * L + q * P, P)], o_sb[:, i % 2]
                                       ).then_inc(s_ost[i % 2], 16)

                    def store_relative(before):
                        settled(s_rr, relative_chunks(before + 1, REL_LATER[1]))
                        pool.dma_start(r_dram[:, :, bass.ds(before * 32, 32)],
                                       r_sb.rearrange("p h b u -> p h (b u)")).then_inc(s_rst, 16)

                    if last:
                        for i in range(2):
                            pool.wait_ge(s_ost[i], 16 * 2 * (NP - 2))
                        pool.wait_ge(s_rst, 16 * (NP - 1))
                        for c in range(3):
                            load_sums(pool, c)
                        pool.wait_ge(s_score, NS * (NP - 1))
                        for c in range(2):
                            load_outputs(pool, c)
                            load_relative(pool, c)
                    load_some(3)
                    if not first:
                        store_heads(AV_LATER0, pr - 1, 2 * pr - 2, 1)
                        load_some(3)
                        store_relative(pr - 1)
                        load_some(2)
                        store_heads(AV_LATER1, pr, 2 * pr - 1, 1)
                    load_some(2)
                    store_heads(AV_EARLY[0], pr, 2 * pr, 0)
                    load_some(2)
                    store_heads(AV_EARLY[1], pr, 2 * pr + 1, 0)
                    load_some(len(loads))
                    if last:
                        pool.wait_ge(s_inv, 1)
                        for c in range(3):
                            store_inverses(pool, c)
                        pool.wait_ge(s_invst, 48)
                        for c in range(2):
                            load_inverses(pool, c)
                        pool.wait_ge(s_score, NS * NP)
                        load_outputs(pool, 2)
                        load_inverses(pool, 2)
                        store_heads(AV_LATER0, pr, 2 * pr, 1)
                        store_heads(AV_LATER1, NP, 2 * pr + 1, 1)
                        for b in range(2):
                            pool.wait_ge(s_ost[b], 16 * 2 * NP)
                        load_sums(pool, 3)
                        store_relative(pr)
                        load_outputs(pool, 3)
                        pool.wait_ge(s_inv, 2)
                        store_inverses(pool, 3)
                        pool.wait_ge(s_invst, 64)
                        load_inverses(pool, 3)

                in_pairs(pool, pair)

            expert_layer(0)
            attention()
            expert_layer(1)

        @block.scalar
        def _(act):
            roots = [0]

            def root(tiles):
                roots[0] += 1
                act.wait_ge(s_sqrt_in, roots[0])
                nc.scalar.activation(s0[:, tiles], vare[:, tiles], ACT.Sqrt).then_inc(s_sqrt, 1)

            def parameters():
                act.wait_ge(s_tr, 1)
                nc.scalar.copy(b1T, tr_bank(0)[:, 0:E * NC])
                nc.scalar.copy(gwT, tr_bank(0)[:, E * NC:E * NC + E])
                nc.scalar.copy(ext[:, P - 1:3 * P - 1], tr_bank(0)[0:HD, P:3 * P])
                nc.scalar.copy(ext[:, 0:P - 1], tr_bank(0)[0:HD, P:P + 1].to_broadcast([HD, P - 1]))
                nc.scalar.copy(ext[:, 3 * P - 1:3 * P], tr_bank(0)[0:HD, P:P + 1]).then_inc(s_trf, 1)
                act.wait_ge(s_tr, 2)
                nc.scalar.copy(wT[:, 0:2].rearrange("p w (d h) -> p w d h", h=H),
                               tr_bank(1)[:, 0:2 * D].rearrange("p (w h d) -> p w d h", w=2, h=H))
                nc.scalar.copy(wT[:, 2:4], tr_bank(1)[:, 2 * D:4 * D].rearrange("p (w d) -> p w d", w=2)
                               ).then_inc(s_trf, 1)

            def expert_layer(n):
                tr = 2 + n * TRN + (NXB if n else 0)
                root(QUARTERS[0])
                root(QUARTERS[1])
                if not n:
                    parameters()
                for k in range(NXB):
                    act.wait_ge(s_tr, tr + k + 1)
                    nc.scalar.copy(xnT[:, 512 * k:512 * k + 512], tr_bank(tr + k)).then_inc(s_trf, 1)
                    if k in (1, 3):
                        root(QUARTERS[(k + 3) // 2])
                act.wait_ge(s_centred, n + 1)
                nc.scalar.activation(logit, logit, ACT.Exp).then_inc(s_exp, 1)
                root(ALL)
                nc.scalar.activation(half_xn, xn.rearrange("p t d -> p (t d)"), ACT.Copy, scale=0.5).then_inc(s_half, 1)
                act.wait_ge(s_zin, n + 1)
                for t in range(NT):
                    last = nc.scalar.activation(zt[:, t, 0:D], xn[:, t, :], ACT.Identity,
                                                bias=neg_mean[:, t:t + 1], scale=rstd[:, t:t + 1])
                last.then_inc(s_z, 1)
                for k in range(NWB):
                    act.wait_ge(s_tr, tr + NXB + k + 1)
                    if k % 2 == 0:
                        nc.scalar.copy(w1T[:, k // 2, :], tr_bank(tr + NXB + k)).then_inc(s_trf, 1)
                    else:
                        nc.scalar.copy(w2T[:, k // 2, :, :],
                                       tr_bank(tr + NXB + k).rearrange("p (c d) -> p c d", c=NC)).then_inc(s_trf, 1)
                for e in range(E):
                    for c in range(NC):
                        k = (n * E + e) * NC + c
                        act.wait_ge(s_h, k + 1)
                        if e >= 2 or n:
                            act.wait_ge(s_o, n * E + e - 1)
                        nc.scalar.activation(hT[:, e % 2, c, :], psum[:, H_B[k % 2], :], ACT.Gelu_apprx_tanh,
                                             bias=b1T[:, e * NC + c:e * NC + c + 1]).then_inc(s_g, 1)
                    if n == 0:
                        if e == 0:
                            act.wait_ge(s_zero, 1)
                            act.wait_ge(s_const, 9)
                        nc.scalar.copy(q_words[96:P, 4 * e:4 * e + 4],
                                       parity[96:P, :].unsqueeze(1).unsqueeze(3).to_broadcast([32, 4, 2, P])
                                       ).then_inc(s_parity, 1)

            def attention():
                def first_part(i):
                    act.wait_ge(s_pj, i + 1)
                    if i >= 4:
                        act.wait_ge(s_pst[i % 4], 16 * (i // 4))
                    nc.scalar.copy(part[:, i % 4, 0, :], psum[:, 2 + i % 2, :]).then_inc(s_p1, 1)

                def second_part(i):
                    act.wait_ge(s_p1r, i + 1)
                    nc.scalar.copy(part[:, i % 4, 1, :], rest[:, i % 2, :]).then_inc(s_p2, 1)

                def turned(c):
                    for k in (2 * c, 2 * c + 1):
                        act.wait_ge(s_tr, 2 + TRN + k + 1)
                        nc.scalar.copy(anT[:, 512 * k:512 * k + 512], tr_bank(2 + TRN + k)).then_inc(s_trf, 1)

                root(QUARTERS[0])
                turned(0)
                root(QUARTERS[1])
                for c in range(4):
                    if c == 0:
                        turned(1)
                    first_part(4 * c)
                    for i in range(4 * c, 4 * c + 4):
                        if i % 4 < 3:
                            first_part(i + 1)
                        second_part(i)
                        if i % 4 == 0 and 1 <= c < 3:
                            turned(c + 1)
                        if i % 4 == 1 and c < 2:
                            root(QUARTERS[c + 2])
                    for k in (2 * c, 2 * c + 1):
                        act.wait_ge(s_vp, k + 1)
                        nc.scalar.copy(v_all[:, 4 * k:4 * k + 4, :, 0:HD],
                                       psum[:, 4 + k % 2, :].rearrange("p (t h d) -> p t h d", t=4, h=H)
                                       ).then_inc(s_vr, 1)

                def exp(s, pr):
                    b, q, later = SLOTS[s]
                    s, g = s % NS, NS * pr + s
                    act.wait_ge(s_sub, g + 1)
                    if s == 0:
                        reach(act, s_chunk, chunks(pr, REL_EARLY[1]))
                    if s == 4:
                        reach(act, s_chunk, chunks(pr, REL_LATER[1]))
                    if s == 8:
                        reach(act, s_chunk, chunks(pr, AV_LATER1))
                    heads = slice(H * b, H * b + H)
                    if later:
                        dst = probs[:, 1:3, heads, 32 * (q - 4):32 * (q - 4) + 32]
                    else:
                        dst = probs[:, 0, heads, 32 * q:32 * q + 64].rearrange("p h (u n) -> p u h n", u=2)
                    r = s % 3
                    nc.scalar.activation(dst, psum[:, 2 * r:2 * r + 2, :].rearrange("p u (h n) -> p u h n", h=H),
                                         ACT.Exp, scale=HD ** -0.5).then_inc(s_prob, 1)

                def read_heads(pr, i, bank=O_BANK):
                    act.wait_ge(s_chunk, chunks(pr, i))
                    reach(act, s_ost[i % 2], 16 * (2 * pr + {4: -1, 5: 0, 6: 0, 7: 1}[i]))
                    nc.scalar.copy(o_sb[:, i % 2], psum[:, bank, :].rearrange("p (g n) -> p g n", g=4)
                                   ).then_inc(s_chr, 1)

                def pair(pr, r, k):
                    first = isinstance(pr, int) and pr == 0
                    for s in range(NS):
                        if s == 0 and not first:
                            read_heads(pr - 1, AV_LATER0)
                        if s == 8 and not first:
                            read_heads(pr, AV_LATER1)
                        if s in (9, 10):
                            read_heads(pr, AV_EARLY[s - 9])
                        if s >= 2 or not first:
                            exp(s - 2, pr)

                in_pairs(act, pair)
                read_heads(NP - 1, AV_LATER0)
                for s in (-2, -1):
                    exp(s, NP)
                read_heads(NP, AV_LATER1, TAIL_BANK[AV_LATER1])
                for c in range(4):
                    act.wait_ge(s_rel[c], 16 * HD)
                    nat = o_nat[c].rearrange("p (n j c) -> p j n c", j=4, c=4)
                    for u in range(4):
                        last = nc.scalar.copy(nat[:, :, :, u],
                                              o_rel[c].rearrange("p (j r n) -> p j r n", j=4, r=4)[:, :, 3 - u, :])
                    last.then_inc(s_turned, 1)

            expert_layer(0)
            attention()
            expert_layer(1)

        @block.tensor
        def _(pe):
            pe.wait_ge(s_const, 9)
            pe.wait_ge(s_par, 144)
            pe.transpose(tr_bank(0)[:, 0:E * NC], logit[0:E * NC, D:2 * D], ident[0:E * NC, 0:E * NC])
            pe.transpose(tr_bank(0)[:, E * NC:E * NC + E], logit[0:E, 0:D], ident[0:E, 0:E])
            for t in range(2):
                last = pe.transpose(tr_bank(0)[0:HD, P + P * t:2 * P + P * t], hT[:, 1, 0, HD * t:HD * t + HD], ident)
            last.then_inc(s_tr, 1)
            for i in range(4):
                last = pe.transpose(tr_bank(1)[:, D * i:D * i + D], hT[:, 0, i, 0:D], ident)
            last.then_inc(s_tr, 1)

            def expert_layer(n):
                tr = 2 + n * TRN + (NXB if n else 0)

                def bank_of(k):
                    read = 2 + n * (NAB + NXB) + k - 1
                    if k < NAB + 2:
                        pe.wait_ge(s_trf, read)
                    return tr_bank(tr + k)

                def gate(k):
                    pe.wait_ge(s_trf, 2 + n * (NAB + NXB) + k + 1)
                    for t in range(4 * k, 4 * k + 4):
                        last = pe.matmul(psum[:, B_GATE, E * t:E * t + E], xnT[:, P * t:P * t + P], gwT,
                                         start=True, stop=True)
                    return last

                for k in range(NXB):
                    pe.wait_ge(s_xn, n * NXB + k + 1)
                    bank = bank_of(k)
                    for c in range(4):
                        last = pe.transpose(bank[:, P * c:P * c + P], xn[:, 4 * k + c, :], ident)
                    last.then_inc(s_tr, 1)
                    if k:
                        gate(k - 1)
                gate(NXB - 1).then_inc(s_logit, 1)
                pe.wait_ge(s_scored, n + 1)
                for h in range(2):
                    last = pe.transpose(psum[:, B_GATE, P * h:P * h + P], score[:, P * h:P * h + P], ident)
                last.then_inc(s_scT, 1)
                with pe.Fori(0, SCORE_BITS // UNROLL) as i:
                    for u in range(UNROLL):
                        pe.wait_ge(s_mask, i * UNROLL + (n * SCORE_BITS + u + 1))
                        pe.matmul(psum[:, B_CNT, 0:2], same_bf, lane_cnt, start=True, stop=True).then_inc(s_cnt, 1)
                pe.wait_ge(s_pre, 2 * n + 1)
                pe.matmul(psum[:, B_CNT, 0:2], same_bf, lane_tot[:, 0:2], start=True, stop=True)
                pe.matmul(psum[:, B_CNT, 2:4], before_bf, lane_tot[:, 2:4], start=True, stop=True).then_inc(s_prer, 1)
                pe.wait_ge(s_pre, 2 * n + 2)
                pe.matmul(psum[:, B_CNT, 4:6], before_bf, lane_tot[:, 0:2], start=True, stop=True).then_inc(s_prer, 1)
                pe.wait_ge(s_q, n + 1)
                for h in range(2):
                    last = pe.transpose(psum[:, B_GATE, P * h:P * h + P], place_t[:, h, :], ident)
                last.then_inc(s_qT, 1)
                pe.wait_ge(s_raw, 64 * (n + 1))
                for k in range(NWB):
                    bank, e = bank_of(NXB + k), k // 2
                    for c in range(NC):
                        src = raw2[:, e, P * c:P * c + P] if k % 2 else raw1[:, e, c, :]
                        last = pe.transpose(bank[:, P * c:P * c + P], src, ident)
                    last.then_inc(s_tr, 1)
                pe.wait_ge(s_hot, n + 1)
                pe.wait_ge(s_hot_t, n + 1)
                for e in range(E):
                    for t in range(NT):
                        last = pe.matmul(psum[0:LO, B_IDX, 2 * HI * e:2 * HI * e + 2 * HI],
                                         hot_lo[:, :, e * NT + t], hot_hi[:, :, :, e * NT + t],
                                         start=(t == 0), stop=(t == NT - 1))
                last.then_inc(s_idx, 1)

                def turn_rows(e):
                    pe.wait_ge(s_rows[e], 64 * (n + 1))
                    bank = bank_of(NWB + NXB + e)
                    for j in range(NJ):
                        last = pe.transpose(bank[:, P * j:P * j + P], rows[:, e * NJ + j, 0:D], ident)
                    last.then_inc(s_tr, 1)

                def first_half(e):
                    pe.wait_ge(s_yT, n * E + e + 1)
                    for c in range(NC):
                        k = (n * E + e) * NC + c
                        if k >= 2:
                            pe.wait_ge(s_g, k - 1)
                        pe.matmul(psum[:, H_B[k % 2], :], w1T[:, e, P * c:P * c + P], yT[:, e % 2, :],
                                  start=True, stop=True).then_inc(s_h, 1)

                def second_half(e):
                    pe.wait_ge(s_g, (n * E + e + 1) * NC)
                    if n * E + e >= 2:
                        pe.wait_ge(s_os, n * E + e - 1)
                    for j in range(NJ):
                        o = psum[:, O_B[e % 2], P * j:P * j + P]
                        for c in range(NC):
                            last = pe.matmul(o, hT[:, e % 2, c, P * j:P * j + P], w2T[:, e, c, :],
                                             start=(c == 0), stop=(c == NC - 1))
                    last.then_inc(s_o, 1)

                turn_rows(0)
                for e in range(E):
                    first_half(e)
                    if e + 1 < E:
                        turn_rows(e + 1)
                    if 0 < e < E - 1:
                        second_half(e - 1)
                    if e >= E - 2:
                        second_half(e)

            def attention():
                def turn(c):
                    for k in (2 * c, 2 * c + 1):
                        pe.wait_ge(s_an, k + 1)
                        if k >= 2:
                            pe.wait_ge(s_trf, 2 + NAB + k - 1)
                        for t in range(4):
                            last = pe.transpose(tr_bank(2 + TRN + k)[:, P * t:P * t + P], an[:, 4 * k + t, :], ident)
                        last.then_inc(s_tr, 1)

                turn(0)
                turn(1)
                for c in range(4):
                    for i in range(4 * c, 4 * c + 4):
                        if i % 4 == 2 and 1 <= c < 3:
                            turn(c + 1)
                        pe.wait_ge(s_trf, 2 + NAB + i // 2 + 1)
                        if i >= 2:
                            pe.wait_ge(s_p1r, i - 1)
                        cols = anT[:, PT * (i // 2):PT * (i // 2) + PT]
                        if i % 2 == 0:
                            cols = cols.rearrange("p (b a c) -> p c b a", b=2, c=2)
                        pe.matmul(psum[:, 2 + i % 2, :], wT[:, i % 2, :], cols, start=True, stop=True).then_inc(s_pj, 1)
                    for k in (2 * c, 2 * c + 1):
                        if k >= 2:
                            pe.wait_ge(s_vr, k - 1)
                        for t in range(4):
                            last = pe.matmul(psum[:, 4 + k % 2, P * t:P * t + P],
                                             anT[:, P * (4 * k + t):P * (4 * k + t) + P], wT[:, 2, :],
                                             start=True, stop=True)
                        last.then_inc(s_vp, 1)
                pe.wait_ge(s_p1r, 2 * NP)
                pe.wait_ge(s_vr, NT // 4)
                pe.wait_ge(s_rk, 16 * 2 * TERMS)
                pe.wait_ge(s_rv, 16)
                pe.wait_ge(s_zero, 5)
                pe.wait_ge(s_parity, E)

                def scores(s, pr, r, turn):
                    b, q, later = SLOTS[s]
                    reach(pe, s_prob, NS * pr + s - 2)
                    for u in range(2):
                        qu, kb = (q, u) if later else (q + u, 0)
                        sc = psum[:, 2 * (s % 3) + u, :].rearrange("p (h c a) -> p h c a", h=H, c=2)
                        for a in range(16):
                            y = 2 * P - 2 - 2 * (16 * qu + a) + P * kb
                            pe.matmul(sc[:, :, :, a], rel_k[:, y:y + P], q_st[:, r, :, :, P * b + 16 * qu + a],
                                      start=(a == 0), stop=False, skip_group_check=True)
                        for h in range(H):
                            last = pe.matmul(sc[:, h], k_st[:, r, h, L * b + P * kb:L * b + P * kb + P],
                                             q_st[:, r, h, :, P * b + 16 * qu:P * b + 16 * qu + 16],
                                             start=False, stop=False, skip_group_check=True)
                        if u == 0 and turn:
                            turn_maxima(s - 1, pr)
                    last.then_inc(s_score, 1)

                def turn_maxima(s, pr):
                    g = NS * pr + s
                    pe.wait_ge(s_T, g + 1)
                    if not (isinstance(g, int) and g == 0):
                        reach(pe, s_row, g)
                    pe.transpose(psum[0:32, T_BANK, 0:P], m_part[:, s % 3, :], ident).then_inc(s_tT, 1)

                def subtract_maxima(s, pr):
                    pe.wait_ge(s_m[s % 3], 32 * (NS // 3 * pr + (s // 3) + 1))
                    for u in range(2):
                        last = pe.matmul(psum[:, 2 * (s % 3) + u, :], ones_bf, m_row[:, s % 3, 512 * u:512 * u + 512],
                                         start=False, stop=True, skip_group_check=True)
                    last.then_inc(s_sub, 1)

                def chunk(i, first, last, pr, r, bank=O_BANK):
                    later = i in REL_LATER or i in (AV_LATER1, AV_LATER0)
                    if first == 0:
                        if i == REL_LATER[0]:
                            pe.wait_ge(s_prob, NS * pr)
                        if i == AV_EARLY[0]:
                            pe.wait_ge(s_vpair, pr + 1)
                        if i > AV_LATER1:
                            pe.wait_ge(s_prob, NS * pr + {5: 2, 6: 4, 7: 8}[i])
                        if bank != O_BANK:
                            pe.wait_ge(s_prob, NS * NP - (2 if i == 1 else 0))
                        elif 1 <= i <= 4:
                            pe.wait_ge(s_rrd, relative_chunks(pr, i - 1))
                        else:
                            reach(pe, s_chr, value_chunks(pr, i - 1) if i else value_chunks(pr - 1, AV_LATER0))
                    blocks = ((1, 0), (2, 1)) if later else ((0, 0),)
                    for u in range(first, last):
                        if i >= AV_LATER1:
                            batch = 1 if i in (AV_LATER1, AV_EARLY[1]) else 0
                            buffer = 1 - r if i == AV_LATER1 else r
                            for blk, kb in blocks:
                                for j in range(4):
                                    end = pe.matmul(psum[32 * j:32 * j + HD + 1, bank, P * u:P * u + P],
                                                    v_pair[:, buffer, 2 * batch + kb, 4 * u + j, :],
                                                    probs[:, blk, H * batch + 4 * u + j, :],
                                                    start=(kb == 0), stop=(kb == len(blocks) - 1), skip_group_check=True)
                            continue
                        for blk, kb in blocks:
                            for j in range(4):
                                q0 = 16 * (4 * (i % 2) + u) + 4 * j
                                x = 2 * P - 4 - (q0 + (P if later else 0) - P * kb)
                                at, a = 32 * (q0 // 32), q0 % 32 // 2
                                qs4 = probs[:, blk, :, at:at + 32].rearrange("p n (c a) -> p n c a", c=2)
                                end = pe.matmul(psum[32 * j:32 * j + 32, bank, P * u:P * u + P],
                                                rel_v[:, HD * x:HD * x + 32], qs4[:, :, :, a:a + 2],
                                                start=(kb == 0), stop=(kb == len(blocks) - 1), skip_group_check=True)
                    if last == 4:
                        end.then_inc(s_chunk, 1)

                def pair(pr, r, k):
                    first = isinstance(pr, int) and pr == 0
                    if isinstance(pr, int) and pr == 0:
                        pe.wait_ge(s_first, 16 * LOADS)
                    else:
                        pe.wait_ge(s_load[r], 16 * LOADS * (k + r))
                    for s in range(NS):
                        scores(s, pr, r, turn=s >= 1 or not first)
                        if s >= 2 or not first:
                            subtract_maxima(s - 2, pr)
                        if s >= 8 or not first:
                            chunk(*CHUNK_AT[s], pr, r)

                in_pairs(pe, pair)
                turn_maxima(-1, NP)
                subtract_maxima(-2, NP)
                for i in TAIL:
                    if i == AV_LATER1:
                        subtract_maxima(-1, NP)
                    chunk(i, 0, 4, NP, 0, TAIL_BANK[i])
                for k in range(NT // 4):
                    pe.wait_ge(s_nat, k // 2 + 1)
                    if k >= 2:
                        pe.wait_ge(s_wor, k - 1)
                    for t in range(4):
                        last = pe.matmul(psum[:, WO_BANK[k % 2], P * t:P * t + P],
                                         o_nat[k // 2][:, P * (4 * (k % 2) + t):P * (4 * (k % 2) + t) + P], wT[:, 3, :], start=True, stop=True)
                    last.then_inc(s_wo, 1)

            expert_layer(0)
            attention()
            expert_layer(1)

        @block.vector
        def _(dve):
            v = nc.vector

            def step(i):
                s_dve.inc(i)
                dve.wait_ge(s_dve.sem, s_dve.now())

            def row_statistics(src, tiles, first=False):
                for t in tiles:
                    if first and t % 8 == 0:
                        dve.wait_ge(s_x[t // 8], 16)
                    last = v.bn_stats(stats[:, t, :], src[:, t, :])
                return last

            def variances(tiles=range(NT)):
                for t in tiles:
                    last = v.bn_aggr(mv[:, t, :], stats[:, t, :])
                step(last)
                a = slice(tiles[0], tiles[-1] + 1)
                v.tensor_scalar(vare[:, a], mv[:, a, 1], EPS, None, ALU.add).then_inc(s_sqrt_in, 1)

            roots = [0]

            def inverse_deviations(tiles=range(NT)):
                a = slice(tiles[0], tiles[-1] + 1)
                roots[0] += 1
                dve.wait_ge(s_sqrt, roots[0])
                step(v.reciprocal(r0[:, a], s0[:, a]))
                step(v.tensor_tensor(r0[:, a], r0[:, a], vare[:, a], ALU.mult))
                step(v.tensor_tensor(r0[:, a], r0[:, a], s0[:, a], ALU.add))
                step(v.tensor_scalar(r0[:, a], r0[:, a], 0.5, None, ALU.mult))
                step(v.reciprocal(rstd[:, a], r0[:, a]))

            def normalise(src, dst, done, tiles=range(NT)):
                inverse_deviations(tiles)
                for t in tiles:
                    i = v.tensor_scalar(dst[:, t, 0:D], src[:, t, :], mv[:, t, 0:1], rstd[:, t:t + 1],
                                        ALU.subtract, ALU.mult)
                    if t % 4 == 3:
                        i.then_inc(done, 1)

            def parts_of_pek():
                dve.wait_ge(s_trf, 1)
                step(v.tensor_copy(ext_part[:, 0], ext))
                step(v.tensor_tensor(ext_rest, ext, ext_part[:, 0], ALU.subtract))
                step(v.tensor_copy(ext_part[:, 1], ext_rest))
                v.tensor_tensor(ext_part[:, 2], ext_rest, ext_part[:, 1], ALU.subtract).then_inc(s_ext, 1)

            def expert_layer(n):
                tr = 2 + n * TRN + (NXB if n else 0)
                if not n:
                    for c in range(5):
                        if c < 4:
                            tiles = range(8 * c, 8 * c + 8)
                            step(row_statistics(x_sb, tiles, True))
                            variances(tiles)
                        if c:
                            normalise(x_sb, xn, s_xn, range(8 * c - 8, 8 * c))
                    parts_of_pek()
                dve.wait_ge(s_xn, (n + 1) * NXB)
                row_statistics(xn, range(NT // 2))
                dve.wait_ge(s_logit, n + 1)
                lg = psum[:, B_GATE, 0:ET].rearrange("p (t e) -> p t e", e=E)
                lv = logit.rearrange("p (t e) -> p t e", e=E)
                step(v.tensor_reduce(lmax, lg, AX.X, ALU.max))
                v.tensor_tensor(lv, lg, lmax.unsqueeze(2).to_broadcast([P, NT, E]),
                                ALU.subtract).then_inc(s_centred, 1)
                step(row_statistics(xn, range(NT // 2, NT)))
                dve.wait_ge(s_exp, n + 1)
                step(v.tensor_reduce(lsum, lv, AX.X, ALU.add))
                step(v.reciprocal(lsum, lsum))
                v.tensor_tensor(by_et(score).rearrange("p e t -> p t e"), lv,
                                lsum.unsqueeze(2).to_broadcast([P, NT, E]), ALU.mult).then_inc(s_scored, 1)
                variances()
                step(v.memset(cand, 1 << (SCORE_BITS - 1)))
                for u in range(UNROLL + 1):
                    last = v.memset(bits[:, u:u + 1], 1 << (SCORE_BITS - 1 - u))
                inverse_deviations()
                v.scalar_tensor_tensor(out=neg_mean, in0=mv[:, :, 0], scalar=-1.0, in1=rstd, op0=ALU.mult,
                                       op1=ALU.mult).then_inc(s_zin, 1)
                dve.wait_ge(s_scT, n + 1)
                step(v.tensor_copy(score_t, psum[:, B_GATE, 0:2 * P].rearrange("p (h n) -> p h n", h=2)))

                cand_f = cand.bitcast(F32)
                PER = 3 * UNROLL + 1
                start = s_dve.n
                with dve.Fori(0, SCORE_BITS // UNROLL) as i:
                    s_dve.base = i * PER
                    for u in range(UNROLL):
                        for h in range(2):
                            last = v.tensor_scalar(mask_bf[:, h, :], score_t[:, h, :], cand_f[:, h:h + 1], None,
                                                   ALU.is_ge, ALU.add, accum_out=lane_cnt[:, h:h + 1])
                        last.then_inc(s_mask, 1)
                        step(v.tensor_tensor(seen, cand, bits[:, u + 1:u + 2].to_broadcast([P, 2]), ALU.bitwise_xor))
                        dve.wait_ge(s_cnt, i * UNROLL + (n * SCORE_BITS + u + 1))
                        step(v.scalar_tensor_tensor(out=flip, in0=psum[:, B_CNT, 0:2], scalar=float(CAP),
                                                    in1=bits[:, u:u + 1].to_broadcast([P, 2]),
                                                    op0=ALU.is_lt, op1=ALU.mult))
                        step(v.tensor_tensor(cand, seen, flip, ALU.bitwise_xor))
                    step(v.tensor_scalar(bits, bits, UNROLL, None, ALU.logical_shift_right))
                assert s_dve.n - start == PER
                s_dve.base = 0
                s_dve.n = start + PER * (SCORE_BITS // UNROLL)

                for h in range(2):
                    v.tensor_scalar(gt_bf[:, h, :], score_t[:, h, :], cand_f[:, h:h + 1], None, ALU.is_gt, ALU.add,
                                    accum_out=lane_tot[:, h:h + 1])
                    last = v.tensor_scalar(eq_bf[:, h, :], score_t[:, h, :], cand_f[:, h:h + 1], None, ALU.is_equal,
                                           ALU.add, accum_out=lane_tot[:, 2 + h:3 + h])
                last.then_inc(s_pre, 1)
                dve.wait_ge(s_pre, 2 * n + 1)
                flat = lambda a: a.rearrange("p h n -> p (h n)")
                step(v.tensor_tensor_scan(flat(scan), carry, flat(eq_bf), 0.0, ALU.mult, ALU.add))
                dve.wait_ge(s_prer, 2 * n + 1)
                step(v.tensor_copy(carry_at, psum[:, B_CNT, 2:4]))
                step(v.tensor_tensor(need, psum[:, B_CNT, 0:2], carry_at, ALU.add))
                step(v.tensor_scalar(need, need, -1.0, float(CAP), ALU.mult, ALU.add))
                for h in range(2):
                    last = v.scalar_tensor_tensor(out=sel_bf[:, h, :], in0=scan[:, h, :], scalar=need[:, h:h + 1],
                                                  in1=eq_bf[:, h, :], op0=ALU.is_le, op1=ALU.mult)
                step(last)
                step(v.tensor_tensor(flat(sel_bf), flat(sel_bf), flat(gt_bf), ALU.add))
                step(v.tensor_tensor_scan(flat(scan), carry, flat(sel_bf), 0.0, ALU.mult, ALU.add))
                v.tensor_copy(lane_tot[:, 0:2], scan[:, :, P - 1]).then_inc(s_pre, 1)
                dve.wait_ge(s_prer, 2 * n + 2)
                step(v.tensor_copy(carry_at, psum[:, B_CNT, 4:6]))
                for h in range(2):
                    last = v.scalar_tensor_tensor(out=place_t[:, h, :], in0=scan[:, h, :], scalar=carry_at[:, h:h + 1],
                                                  in1=sel_bf[:, h, :], op0=ALU.add, op1=ALU.mult)
                last.then_inc(s_q, 1)
                dve.wait_ge(s_qT, n + 1)
                step(v.tensor_scalar(pos_i, psum[:, B_GATE, 0:ET], -1.0, None, ALU.add))
                v.tensor_scalar(lo_i, pos_i, LO - 1, None, ALU.bitwise_and)
                step(v.tensor_scalar(hi_i, pos_i, 5, None, ALU.arith_shift_right))
                v.tensor_copy(lo_bf, lo_i)
                step(v.tensor_copy(hi_bf, hi_i))
                for b in range(HI):
                    last = v.tensor_scalar(eqhi[:, b, :], hi_bf, float(b), None, ALU.is_equal)
                last.then_inc(s_eqhi, 1)
                for a in range(LO):
                    v.tensor_scalar(hot_lo[:, a, :], lo_bf, float(a), None, ALU.is_equal)
                dve.wait_ge(s_eqhi, n + 1)
                dve.wait_ge(s_init, n + 1)
                v.tensor_scalar(hot_hi[:, 1], eqhi, iota_p, None, ALU.mult).then_inc(s_hot, 1)
                dve.wait_ge(s_idx, n + 1)
                si = psum[0:LO, B_IDX, 0:2 * HI * E].rearrange("p (e w b) -> p e w b", e=E, w=2)
                ip = idx_p[0:LO, :].rearrange("p (e b) -> p e b", e=E)
                step(v.tensor_copy(ip, si[:, :, 1, :]))
                step(v.scalar_tensor_tensor(out=ip, in0=si[:, :, 0, :], scalar=float(P), in1=ip,
                                            op0=ALU.mult, op1=ALU.add))
                v.tensor_copy(idx_i[0:LO, :].rearrange("p (r e j) -> p r e j", r=4, e=E),
                              idx_p[0:LO, :].rearrange("p (e j r) -> p r e j", e=E, j=NJ)).then_inc(s_idxi, 1)

                def scale(e):
                    dve.wait_ge(s_o, n * E + e + 1)
                    if e >= 2:
                        dve.wait_ge(s_sc, 64 * (n * E + e - 1))
                    if n == 0 and e == 0:
                        dve.wait_ge(s_b2, 16)
                    step(v.tensor_tensor(osb[:, e % 2], psum[:, O_B[e % 2], :].rearrange("p (j d) -> p j d", j=NJ),
                                         b2_all[:, e].unsqueeze(1).to_broadcast([P, NJ, D]), ALU.add))
                    for j in range(NJ):
                        last = v.tensor_scalar(osb[:, e % 2, j, :], osb[:, e % 2, j, :],
                                               rows[:, e * NJ + j, D + e:D + e + 1], 0.5, ALU.mult, ALU.mult)
                    last.then_inc(s_os, 1)

                if n == 0:
                    dve.wait_ge(s_tr, tr + NAB)
                    dve.wait_ge(s_tab, 16)
                    v.memset(q_words, 0.0).then_inc(s_zero, 1)

                def rows_in(e):
                    k = NWB + NXB + e
                    dve.wait_ge(s_tr, tr + k + 1)
                    if e >= 2:
                        dve.wait_ge(s_h, (n * E + e - 1) * NC)
                    if n == 0 and e == 0:
                        dve.wait_ge(s_rk, 16 * 2 * TERMS)
                    v.tensor_scalar(yT[:, e % 2, :], tr_bank(tr + k), lnw, lnb, ALU.mult, ALU.add).then_inc(s_yT, 1)

                rows_in(0)
                for e in range(1, E + 1):
                    if e < E:
                        rows_in(e)
                    if e >= 2:
                        scale(e - 2)
                scale(E - 1)

            def attention():
                dve.wait_ge(s_const, 7)
                step(v.tensor_copy(lane_i, iota_p))
                step(v.tensor_scalar(lane_i, lane_i, 3, 3, ALU.logical_shift_right, ALU.bitwise_and))
                step(v.tensor_copy(lane_f, lane_i))
                for c in range(2):
                    for a in range(2):
                        last = v.tensor_scalar(own_q[:, 2 * c + a:2 * c + a + 1], lane_f, float(3 - 2 * a - c), None,
                                               ALU.is_equal)
                step(last)

                def rest_of(i):
                    dve.wait_ge(s_p1, i + 1)
                    if i >= 2:
                        dve.wait_ge(s_part, i - 1)
                    v.tensor_tensor(rest[:, i % 2, :], psum[:, 2 + i % 2, :], part[:, i % 4, 0, :],
                                    ALU.subtract).then_inc(s_p1r, 1)

                def statistics(c):
                    dve.wait_ge(s_x[c], 32)
                    return row_statistics(x_sb, range(8 * c, 8 * c + 8))

                for c in range(2):
                    step(statistics(c))
                    variances(range(8 * c, 8 * c + 8))
                    normalise(x_sb, an, s_an, range(8 * c, 8 * c + 8))
                for c in range(4):
                    ahead = c + 2 < 4
                    tiles = range(8 * c + 16, 8 * c + 24)
                    rest_of(4 * c)
                    if ahead:
                        last = statistics(c + 2)
                    rest_of(4 * c + 1)
                    if ahead:
                        step(last)
                        variances(tiles)
                    rest_of(4 * c + 2)
                    rest_of(4 * c + 3)
                    if ahead:
                        normalise(x_sb, an, s_an, tiles)

                def partial_maxima(s, pr):
                    g = NS * pr + s
                    dve.wait_ge(s_score, g + 1)
                    later = SLOTS[s][2]
                    mp = m_part[:, s % 3, :]
                    i = v.tensor_reduce(mp, psum[:, 2 * (s % 3):2 * (s % 3) + 2, :].rearrange("p u (h n) -> p (u h) n", n=32),
                                        AX.X, ALU.max, apply_transpose=True)
                    if not later:
                        i.then_inc(s_T, 1)
                        return
                    step(i)
                    m2 = mp.rearrange("p (u h) -> p u h", u=2)
                    step(v.tensor_tensor(m2[:, 0, :], m2[:, 0, :], m2[:, 1, :], ALU.max))
                    v.tensor_copy(m2[:, 1, :], m2[:, 0, :]).then_inc(s_T, 1)

                def rows_of_maxima(s, pr):
                    g = NS * pr + s
                    dve.wait_ge(s_tT, g + 1)
                    hl = m_hl[0:32, s % 3]
                    step(v.tensor_reduce(m_neg[0:32, :], psum[0:32, T_BANK, 0:P].rearrange("p (i q) -> p q i", i=4),
                                         AX.X, ALU.max, negate=True))
                    step(v.tensor_copy(hl[:, 0, :], m_neg[0:32, :]))
                    v.tensor_tensor(hl[:, 1, :], m_neg[0:32, :], hl[:, 0, :], ALU.subtract).then_inc(s_row, 1)

                def reduce_relative(i, pr, bank=O_BANK):
                    dve.wait_ge(s_chunk, chunks(pr, i))
                    if i:
                        dve.wait_ge(s_rr, relative_chunks(pr, i) - 1)
                    else:
                        dve.wait_ge(s_rst, 16 * pr)
                    v.tensor_tensor(r_tmp.rearrange("p (n q) -> p n q", q=4),
                                    psum[:, bank, :].rearrange("p (n q) -> p n q", q=4),
                                    own_q.unsqueeze(1).to_broadcast([P, P, 4]), ALU.mult).then_inc(s_rrd, 1)
                    dve.wait_ge(s_rrd, relative_chunks(pr, i))
                    u = 8 * (i in REL_LATER) + 4 * (i % 2)
                    v.tensor_reduce(r_sb[:, :, :, u:u + 4].rearrange("p h b u -> p u b h"),
                                    r_tmp.rearrange("p (u b h q) -> p u b h q", u=4, b=2, h=H),
                                    AX.X, ALU.add).then_inc(s_rr, 1)

                def pair(pr, r, k):
                    first = isinstance(pr, int) and pr == 0
                    for s in range(NS):
                        if s in (1, 2, 4, 6) and not first:
                            reduce_relative({1: 0, 2: 1, 4: 2, 6: 3}[s], pr)
                        if s >= 1 or not first:
                            rows_of_maxima(s - 1, pr)
                        partial_maxima(s, pr)
                        if isinstance(pr, int) and pr == NP - 1 and s == 5:
                            dve.wait_ge(s_sum, 48)
                            v.reciprocal(sums[:, 0:3], sums[:, 0:3]).then_inc(s_inv, 1)

                per = 2 * (NS * 2 + 8 * 2)
                pair(0, 0, 0)
                start = s_dve.n
                with dve.Fori(0, NP // 2 - 1) as i:
                    s_dve.base = i * per
                    pair(2 * i + 1, 1, i)
                    pair(2 * i + 2, 0, i + 1)
                assert s_dve.n - start == per, (s_dve.n - start, per)
                s_dve.base, s_dve.n = 0, start + per * (NP // 2 - 1)
                pair(NP - 1, 1, NP // 2 - 1)
                rows_of_maxima(-1, NP)
                for i in range(4):
                    reduce_relative(i, NP, TAIL_BANK[i])

                def normalised(c):
                    dve.wait_ge(s_all[c], 32)
                    dve.wait_ge(s_turned, c + 1)
                    own = lambda a, u: a.rearrange("p (n c a) -> p n c a", c=2, a=16)[:, :, u, :]
                    tok = lambda u: o_nat[c].rearrange("p (n a c) -> p n a c", c=2, a=16)[:, :, :, u]
                    for u in range(2):
                        last = v.tensor_tensor(tok(u), tok(u), own(o_all[c], u), ALU.add)
                    step(last)
                    for u in range(2):
                        last = v.tensor_tensor(tok(u), tok(u), own(o_inv[c], u), ALU.mult)
                    last.then_inc(s_nat, 1)

                def residual(c):
                    for k in (2 * c, 2 * c + 1):
                        dve.wait_ge(s_wo, k + 1)
                        xk = x_sb[:, 4 * k:4 * k + 4, :]
                        v.tensor_tensor(xk, xk, psum[:, WO_BANK[k % 2], :].rearrange("p (t d) -> p t d", t=4),
                                        ALU.add).then_inc(s_wor, 1)

                def next_statistics(c):
                    dve.wait_ge(s_wor, 2 * c + 2)
                    tiles = range(8 * c, 8 * c + 8)
                    step(row_statistics(x_sb, tiles))
                    variances(tiles)

                def next_layer(c):
                    normalise(x_sb, xn, s_xn, range(8 * c, 8 * c + 8))

                normalised(0)
                dve.wait_ge(s_sum, 64)
                v.reciprocal(sums[:, 3], sums[:, 3]).then_inc(s_inv, 1)
                normalised(1)
                residual(0)
                normalised(2)
                residual(1)
                residual(2)
                for c in range(3):
                    next_statistics(c)
                normalised(3)
                next_layer(0)
                residual(3)
                next_statistics(3)
                for c in range(1, 4):
                    next_layer(c)

            expert_layer(0)
            attention()
            expert_layer(1)


_INS = ['L0_attn_x', 'L0_attn_Wq', 'L0_attn_Wk', 'L0_attn_Wv', 'L0_attn_Wo', 'L0_attn_pek', 'L0_attn_pev',
        'L0_ffn_gate_w', 'L0_ffn_ln_w', 'L0_ffn_ln_b', 'L0_ffn_fc1s', 'L0_ffn_b1s', 'L0_ffn_fc2s', 'L0_ffn_b2s']
_OUTS = [((16, 256, 128), 'float32')]


def kernel(**inputs):
    import numpy as _np
    import concourse.bacc as _bacc
    from concourse import mybir as _mybir
    from concourse.bass_utils import run_bass_kernel_spmd as _run

    nc = _bacc.Bacc("TRN2", target_bir_lowering=False, num_devices=1)
    arrays, args = {}, []
    for name in _INS:
        a = _np.ascontiguousarray(inputs[name])
        arrays[f"in_{name}_dram"] = a
        args.append(nc.dram_tensor(f"in_{name}_dram", a.shape, _mybir.dt.from_np(a.dtype), kind="ExternalInput").ap())
    for i, (shape, dtype) in enumerate(_OUTS):
        dt = _mybir.dt.from_np(_np.dtype(dtype))
        args.append(nc.dram_tensor(f"out_{i}_dram", shape, dt, kind="ExternalOutput").ap())
    macaron_block(nc, *args)
    r = _run(nc, [arrays], core_ids=[0])
    got = tuple(r.results[0][f"out_{i}_dram"] for i in range(len(_OUTS)))
    return got[0]
```
